# Optimizing a Trainium2 kernel written in Bass

```python
import numpy as np
import jax
import jax.numpy as jnp

def _softmax(x, axis=-1):
    return jax.nn.softmax(x, axis=axis)

def _gelu(x):
    return jax.nn.gelu(x, approximate=True)

def _silu(x):
    return jax.nn.silu(x)

def _sigmoid(x):
    return jax.nn.sigmoid(x)

def _layernorm(x, axis=-1, eps=1e-05):
    m = jnp.mean(x, axis=axis, keepdims=True)
    v = jnp.var(x, axis=axis, keepdims=True)
    return (x - m) / jnp.sqrt(v + eps)

def _scatter_add(tgt, idx, src, axis=0):
    return tgt.at[idx].add(src)

def _segment_sum(src, seg, n):
    return jax.ops.segment_sum(src, seg, n)
kernel_name = 'mk_gnn_preln_d4_gnn_r32_aa65f3'

def setup_inputs(seed: int=0):
    np.random.seed(seed)
    _w = jnp.asarray

    def _rec_inputs():
        import jax
        import jax.numpy as jnp
        _gk = jax.random.key(seed)
        x = -0.0006008 + 1.001 * jax.random.normal(jax.random.fold_in(_gk, 1), (3125, 256), jnp.float32)
        src = jax.random.randint(jax.random.fold_in(_gk, 2), (50000,), 0, 3125, jnp.int32)
        dst = jnp.minimum((3125 * jax.random.uniform(jax.random.fold_in(_gk, 3), (50000,)) ** 2.0).astype(jnp.int32), 99999)
        _o = jnp.argsort(dst, stable=True)
        src = src[_o]
        dst = dst[_o]
        edge_type_8 = jax.random.randint(jax.random.fold_in(_gk, 13), (50000,), 0, 8, jnp.int32)
        return (x, src, dst, edge_type_8)
    x, src, dst, edge_type_8 = _rec_inputs()

    def _L0_gnn_setup():
        import jax, jax.numpy as jnp
        import numpy as np
        LN_EPS = 1e-05

        def layer_norm(h, gamma, beta):
            mu = jnp.mean(h, axis=-1, keepdims=True)
            var = jnp.mean(jnp.square(h - mu), axis=-1, keepdims=True)
            return (h - mu) * jax.lax.rsqrt(var + LN_EPS) * gamma + beta

        def gcn_conv(x, src, dst, W, b, n_nodes):
            h = x @ W
            deg = jax.ops.segment_sum(jnp.ones_like(src, dtype=h.dtype), dst, num_segments=n_nodes)
            dinv = jax.lax.rsqrt(jnp.maximum(deg, 1.0))
            norm = dinv[src] * dinv[dst]
            msg = h[src] * norm[:, None]
            return jax.ops.segment_sum(msg, dst, num_segments=n_nodes) + b
        key = jax.random.key(seed)
        ks = jax.random.split(key, 8)
        N, E, Cin, Ch, Cout = (10000, 5000, 256, 512, 256)
        x = jax.random.normal(ks[0], (N, Cin), dtype=jnp.float32)
        edge_index = jax.random.randint(ks[1], (2, E), 0, N, dtype=jnp.int64)
        W1 = jax.random.normal(ks[2], (Cin, Ch), dtype=jnp.float32) * (1.0 / np.sqrt(Cin))
        b1 = jnp.zeros((Ch,), dtype=jnp.float32)
        gamma1 = jnp.ones((Ch,), dtype=jnp.float32)
        beta1 = jnp.zeros((Ch,), dtype=jnp.float32)
        W2 = jax.random.normal(ks[3], (Ch, Cout), dtype=jnp.float32) * (1.0 / np.sqrt(Ch))
        b2 = jnp.zeros((Cout,), dtype=jnp.float32)
        gamma2 = jnp.ones((Cout,), dtype=jnp.float32)
        beta2 = jnp.zeros((Cout,), dtype=jnp.float32)
        return {'x': x, 'edge_index': edge_index, 'W1': W1, 'b1': b1, 'gamma1': gamma1, 'beta1': beta1, 'W2': W2, 'b2': b2, 'gamma2': gamma2, 'beta2': beta2}
    _L0_gnn_all = _L0_gnn_setup()
    _L0_gnn_in = {k: v for k, v in _L0_gnn_all.items() if k in ('W1', 'b1', 'gamma1', 'beta1', 'W2', 'b2', 'gamma2', 'beta2')}
    del _L0_gnn_all

    def _L1_gnn_setup():
        import jax, jax.numpy as jnp
        import numpy as np
        key = jax.random.key(seed)
        k1, k2, k3 = jax.random.split(key, 3)
        N, E, D_IN, D_OUT = (3125, 100000, 256, 256)
        x = jax.random.normal(k1, (N, D_IN), dtype=jnp.float32)
        W = jax.random.normal(k2, (D_OUT, D_IN), dtype=jnp.float32) * (1.0 / np.sqrt(D_IN))
        edge_index = jax.random.randint(k3, (2, E), 0, N, dtype=jnp.int32)
        return {'x': x, 'W': W, 'edge_index': edge_index}
    _L1_gnn_all = _L1_gnn_setup()
    _L1_gnn_in = {k: v for k, v in _L1_gnn_all.items() if k in ('W',)}
    del _L1_gnn_all

    def _L2_gnn_setup():
        import jax, jax.numpy as jnp
        import numpy as np
        N_NODES = 50000
        N_EDGES = 12500
        G_DIM = 256
        H1 = 128
        H2 = 64
        HEADS = 4
        N_REL = 8
        BN_EPS = 1e-05
        LEAKY_SLOPE = 0.01

        def _rgcn(x, src, dst, edge_type, weight, root, bias):
            xw = jnp.einsum('nd,rdh->rnh', x, weight)
            m = xw[edge_type, src]
            N = x.shape[0]
            R = weight.shape[0]
            seg = dst * R + edge_type
            cnt = jax.ops.segment_sum(jnp.ones((m.shape[0],), m.dtype), seg, num_segments=N * R)
            m = m / jnp.maximum(cnt[seg], 1.0)[:, None]
            agg = jax.ops.segment_sum(m, dst, num_segments=N)
            return agg + x @ root + bias

        def _transformer_conv(x, src, dst, heads, wq, bq, wk, bk, wv, bv, wskip, bskip):
            N = x.shape[0]
            d = wq.shape[1] // heads
            q = (x @ wq + bq).reshape(N, heads, d)
            k = (x @ wk + bk).reshape(N, heads, d)
            v = (x @ wv + bv).reshape(N, heads, d)
            score = jnp.sum(q[dst] * k[src], axis=-1) / jnp.sqrt(jnp.asarray(d, x.dtype))
            smax = jax.ops.segment_max(score, dst, num_segments=N)
            smax = jnp.where(jnp.isfinite(smax), smax, 0.0)
            e = jnp.exp(score - jax.lax.stop_gradient(smax)[dst])
            den = jax.ops.segment_sum(e, dst, num_segments=N)
            alpha = e / jnp.maximum(den, 1e-16)[dst]
            out = jax.ops.segment_sum(alpha[:, :, None] * v[src], dst, num_segments=N)
            out = out.reshape(N, heads * d)
            return out + x @ wskip + bskip
        key = jax.random.key(seed)
        ks = jax.random.split(key, 16)
        HD = HEADS * H2
        return {'node_features': jax.random.normal(ks[0], (N_NODES, G_DIM), jnp.float32), 'edge_index': jax.random.randint(ks[1], (2, N_EDGES), 0, N_NODES, jnp.int64), 'edge_type': jax.random.randint(ks[2], (N_EDGES,), 0, N_REL, jnp.int64), 'heads': HEADS, 'rgcn_weight': jax.random.normal(ks[3], (N_REL, G_DIM, H1), jnp.float32) * 0.05, 'rgcn_root': jax.random.normal(ks[4], (G_DIM, H1), jnp.float32) * 0.05, 'rgcn_bias': jnp.zeros((H1,), jnp.float32), 'wq': jax.random.normal(ks[5], (H1, HD), jnp.float32) * 0.05, 'bq': jnp.zeros((HD,), jnp.float32), 'wk': jax.random.normal(ks[6], (H1, HD), jnp.float32) * 0.05, 'bk': jnp.zeros((HD,), jnp.float32), 'wv': jax.random.normal(ks[7], (H1, HD), jnp.float32) * 0.05, 'bv': jnp.zeros((HD,), jnp.float32), 'wskip': jax.random.normal(ks[8], (H1, HD), jnp.float32) * 0.05, 'bskip': jnp.zeros((HD,), jnp.float32), 'bn_gamma': jnp.ones((HD,), jnp.float32), 'bn_beta': jnp.zeros((HD,), jnp.float32)}
    _L2_gnn_all = _L2_gnn_setup()
    _L2_gnn_in = {k: v for k, v in _L2_gnn_all.items() if k in ('rgcn_weight', 'rgcn_root', 'rgcn_bias', 'wq', 'bq', 'wk', 'bk', 'wv', 'bv', 'wskip', 'bskip', 'bn_gamma', 'bn_beta')}
    del _L2_gnn_all

    def _L3_gnn_setup():
        import jax, jax.numpy as jnp
        import numpy as np
        N = 3125
        E = 50000
        IN_FEATS = 256
        OUT_FEATS = 256
        MAXK = 32

        def _maxk(x, k):
            _, idx = jax.lax.top_k(x, k)
            rows = jnp.arange(x.shape[0])[:, None]
            mask = jnp.zeros_like(x).at[rows, idx].set(1.0)
            return x * mask
        key = jax.random.key(seed)
        k1, k2, k3, k4, k5 = jax.random.split(key, 5)
        feat = jax.random.normal(k1, (N, IN_FEATS), dtype=jnp.float32)
        W_self = jax.random.normal(k2, (IN_FEATS, OUT_FEATS), dtype=jnp.float32) * (1.0 / np.sqrt(IN_FEATS))
        W_neigh = jax.random.normal(k3, (IN_FEATS, OUT_FEATS), dtype=jnp.float32) * (1.0 / np.sqrt(IN_FEATS))
        src = jax.random.randint(k4, (E,), 0, N, dtype=jnp.int64)
        dst = jax.random.randint(k5, (E,), 0, N, dtype=jnp.int64)
        return {'feat': feat, 'W_self': W_self, 'W_neigh': W_neigh, 'src': src, 'dst': dst}
    _L3_gnn_all = _L3_gnn_setup()
    _L3_gnn_in = {k: v for k, v in _L3_gnn_all.items() if k in ('W_self', 'W_neigh')}
    del _L3_gnn_all
    return {'x': x, 'src': src, 'dst': dst, 'edge_type_8': edge_type_8, 'L0_gnn_W1': _L0_gnn_in['W1'], 'L0_gnn_b1': _L0_gnn_in['b1'], 'L0_gnn_gamma1': _L0_gnn_in['gamma1'], 'L0_gnn_beta1': _L0_gnn_in['beta1'], 'L0_gnn_W2': _L0_gnn_in['W2'], 'L0_gnn_b2': _L0_gnn_in['b2'], 'L0_gnn_gamma2': _L0_gnn_in['gamma2'], 'L0_gnn_beta2': _L0_gnn_in['beta2'], 'L1_gnn_W': _L1_gnn_in['W'], 'L2_gnn_rgcn_weight': _L2_gnn_in['rgcn_weight'], 'L2_gnn_rgcn_root': _L2_gnn_in['rgcn_root'], 'L2_gnn_rgcn_bias': _L2_gnn_in['rgcn_bias'], 'L2_gnn_wq': _L2_gnn_in['wq'], 'L2_gnn_bq': _L2_gnn_in['bq'], 'L2_gnn_wk': _L2_gnn_in['wk'], 'L2_gnn_bk': _L2_gnn_in['bk'], 'L2_gnn_wv': _L2_gnn_in['wv'], 'L2_gnn_bv': _L2_gnn_in['bv'], 'L2_gnn_wskip': _L2_gnn_in['wskip'], 'L2_gnn_bskip': _L2_gnn_in['bskip'], 'L2_gnn_bn_gamma': _L2_gnn_in['bn_gamma'], 'L2_gnn_bn_beta': _L2_gnn_in['bn_beta'], 'L3_gnn_W_self': _L3_gnn_in['W_self'], 'L3_gnn_W_neigh': _L3_gnn_in['W_neigh']}

def reference(x, src, dst, edge_type_8, L0_gnn_W1, L0_gnn_b1, L0_gnn_gamma1, L0_gnn_beta1, L0_gnn_W2, L0_gnn_b2, L0_gnn_gamma2, L0_gnn_beta2, L1_gnn_W, L2_gnn_rgcn_weight, L2_gnn_rgcn_root, L2_gnn_rgcn_bias, L2_gnn_wq, L2_gnn_bq, L2_gnn_wk, L2_gnn_bk, L2_gnn_wv, L2_gnn_bv, L2_gnn_wskip, L2_gnn_bskip, L2_gnn_bn_gamma, L2_gnn_bn_beta, L3_gnn_W_self, L3_gnn_W_neigh):
    import jax
    import jax.numpy as jnp

    def _L0_gnn_ref(x, edge_index, W1, b1, gamma1, beta1, W2, b2, gamma2, beta2):
        import jax, jax.numpy as jnp
        import numpy as np
        LN_EPS = 1e-05

        def layer_norm(h, gamma, beta):
            mu = jnp.mean(h, axis=-1, keepdims=True)
            var = jnp.mean(jnp.square(h - mu), axis=-1, keepdims=True)
            return (h - mu) * jax.lax.rsqrt(var + LN_EPS) * gamma + beta

        def gcn_conv(x, src, dst, W, b, n_nodes):
            h = x @ W
            deg = jax.ops.segment_sum(jnp.ones_like(src, dtype=h.dtype), dst, num_segments=n_nodes)
            dinv = jax.lax.rsqrt(jnp.maximum(deg, 1.0))
            norm = dinv[src] * dinv[dst]
            msg = h[src] * norm[:, None]
            return jax.ops.segment_sum(msg, dst, num_segments=n_nodes) + b
        n = x.shape[0]
        loops = jnp.arange(n, dtype=edge_index.dtype)
        src = jnp.concatenate([edge_index[0], loops])
        dst = jnp.concatenate([edge_index[1], loops])
        h = gcn_conv(x, src, dst, W1, b1, n)
        h = jax.nn.relu(layer_norm(h, gamma1, beta1))
        g = gcn_conv(h, src, dst, W2, b2, n)
        g = jax.nn.relu(layer_norm(g, gamma2, beta2))
        return g

    def _L1_gnn_ref(x, W, edge_index):
        import jax, jax.numpy as jnp
        import numpy as np
        N = x.shape[0]
        loops = jnp.arange(N, dtype=edge_index.dtype)
        src = jnp.concatenate([edge_index[0], loops])
        dst = jnp.concatenate([edge_index[1], loops])
        deg = jax.ops.segment_sum(jnp.ones_like(src, dtype=x.dtype), src, num_segments=N)
        deg_rsqrt = jax.lax.rsqrt(deg)
        vals = deg_rsqrt[src] * deg_rsqrt[dst]
        h = x @ W.T
        msgs = vals[:, None] * h[dst]
        out = jax.ops.segment_sum(msgs, src, num_segments=N)
        return out

    def _L2_gnn_ref(node_features, edge_index, edge_type, heads, rgcn_weight, rgcn_root, rgcn_bias, wq, bq, wk, bk, wv, bv, wskip, bskip, bn_gamma, bn_beta):
        import jax, jax.numpy as jnp
        import numpy as np
        N_NODES = 50000
        N_EDGES = 12500
        G_DIM = 256
        H1 = 128
        H2 = 64
        HEADS = 4
        N_REL = 8
        BN_EPS = 1e-05
        LEAKY_SLOPE = 0.01

        def _rgcn(x, src, dst, edge_type, weight, root, bias):
            xw = jnp.einsum('nd,rdh->rnh', x, weight)
            m = xw[edge_type, src]
            N = x.shape[0]
            R = weight.shape[0]
            seg = dst * R + edge_type
            cnt = jax.ops.segment_sum(jnp.ones((m.shape[0],), m.dtype), seg, num_segments=N * R)
            m = m / jnp.maximum(cnt[seg], 1.0)[:, None]
            agg = jax.ops.segment_sum(m, dst, num_segments=N)
            return agg + x @ root + bias

        def _transformer_conv(x, src, dst, heads, wq, bq, wk, bk, wv, bv, wskip, bskip):
            N = x.shape[0]
            d = wq.shape[1] // heads
            q = (x @ wq + bq).reshape(N, heads, d)
            k = (x @ wk + bk).reshape(N, heads, d)
            v = (x @ wv + bv).reshape(N, heads, d)
            score = jnp.sum(q[dst] * k[src], axis=-1) / jnp.sqrt(jnp.asarray(d, x.dtype))
            smax = jax.ops.segment_max(score, dst, num_segments=N)
            smax = jnp.where(jnp.isfinite(smax), smax, 0.0)
            e = jnp.exp(score - jax.lax.stop_gradient(smax)[dst])
            den = jax.ops.segment_sum(e, dst, num_segments=N)
            alpha = e / jnp.maximum(den, 1e-16)[dst]
            out = jax.ops.segment_sum(alpha[:, :, None] * v[src], dst, num_segments=N)
            out = out.reshape(N, heads * d)
            return out + x @ wskip + bskip
        src, dst = (edge_index[0], edge_index[1])
        h = _rgcn(node_features, src, dst, edge_type, rgcn_weight, rgcn_root, rgcn_bias)
        out = _transformer_conv(h, src, dst, heads, wq, bq, wk, bk, wv, bv, wskip, bskip)
        mean = jnp.mean(out, axis=0)
        var = jnp.mean((out - mean) ** 2, axis=0)
        y = bn_gamma * (out - mean) * jax.lax.rsqrt(var + BN_EPS) + bn_beta
        return jnp.where(y >= 0, y, LEAKY_SLOPE * y)

    def _L3_gnn_ref(feat, W_self, W_neigh, src, dst):
        import jax, jax.numpy as jnp
        import numpy as np
        N = 3125
        E = 50000
        IN_FEATS = 256
        OUT_FEATS = 256
        MAXK = 32

        def _maxk(x, k):
            _, idx = jax.lax.top_k(x, k)
            rows = jnp.arange(x.shape[0])[:, None]
            mask = jnp.zeros_like(x).at[rows, idx].set(1.0)
            return x * mask
        n = feat.shape[0]
        h_self = feat @ W_self
        h_neigh = feat @ W_neigh
        h_sparse = _maxk(h_neigh, MAXK)
        msg = h_sparse[src]
        summed = jax.ops.segment_sum(msg, dst, num_segments=n)
        deg = jax.ops.segment_sum(jnp.ones((src.shape[0],), dtype=feat.dtype), dst, num_segments=n)
        neigh = summed / jnp.maximum(deg, 1.0)[:, None]
        return h_self + neigh
    edge_index = jnp.stack([src, dst])
    h = jnp.maximum(_layernorm(x, axis=-1), 0.0)
    x = x + _L0_gnn_ref(h, edge_index, L0_gnn_W1, L0_gnn_b1, L0_gnn_gamma1, L0_gnn_beta1, L0_gnn_W2, L0_gnn_b2, L0_gnn_gamma2, L0_gnn_beta2)
    h = jnp.maximum(_layernorm(x, axis=-1), 0.0)
    x = x + _L1_gnn_ref(h, L1_gnn_W, edge_index)
    h = jnp.maximum(_layernorm(x, axis=-1), 0.0)
    x = x + _L2_gnn_ref(h, edge_index, edge_type_8, 4, L2_gnn_rgcn_weight, L2_gnn_rgcn_root, L2_gnn_rgcn_bias, L2_gnn_wq, L2_gnn_bq, L2_gnn_wk, L2_gnn_bk, L2_gnn_wv, L2_gnn_bv, L2_gnn_wskip, L2_gnn_bskip, L2_gnn_bn_gamma, L2_gnn_bn_beta)
    h = jnp.maximum(_layernorm(x, axis=-1), 0.0)
    x = x + _L3_gnn_ref(h, L3_gnn_W_self, L3_gnn_W_neigh, src, dst)
    return x

_drawn_inputs = setup_inputs


def setup_inputs(seed=0):
    import zlib

    import numpy as np

    out = dict(_drawn_inputs(seed))
    spreads = {'L0_gnn_b1': (0.0, 0.1),
     'L0_gnn_gamma1': (1.0, 0.2),
     'L0_gnn_beta1': (0.0, 0.1),
     'L0_gnn_b2': (0.0, 0.1),
     'L0_gnn_gamma2': (1.0, 0.2),
     'L0_gnn_beta2': (0.0, 0.1),
     'L2_gnn_rgcn_bias': (0.0, 2.0),
     'L2_gnn_bq': (0.0, 0.8),
     'L2_gnn_bk': (0.0, 2.0),
     'L2_gnn_bv': (0.0, 2.0),
     'L2_gnn_bskip': (0.0, 2.0),
     'L2_gnn_bn_gamma': (1.0, 0.2),
     'L2_gnn_bn_beta': (0.0, 0.1)}
    factors = {}
    for name, (base, spread) in spreads.items():
        noise = np.random.default_rng([zlib.crc32(name.encode()), seed]).standard_normal(out[name].shape)
        drawn = base * np.exp(spread * noise) if base else spread * noise
        out[name] = jnp.asarray(drawn.astype(out[name].dtype))
    for name, factor in factors.items():
        out[name] = (out[name] * factor).astype(out[name].dtype)
    return out
```

```python
from contextlib import ExitStack

import concourse.bass as bass
from concourse import mybir

P = 128
N = 3125
C = 256
E = 50000
NB = -(-N // P)
TAIL = N - (NB - 1) * P
NPAD = NB * P
EP = 125
EC = E // EP
HALF = 8
BODY = 2 * HALF
T = -(-((E + NB * (P - 1)) // P) // BODY) * BODY
HEADS = 4
HD = C // HEADS
NREL = 8
H1 = 128
CW = 512
MAXK = 32
HCH = 20
RCH = 8
AW = C + NREL
BIG = 2.0 ** 127
LN_EPS = 1e-5
BN_EPS = 1e-5
SLOPE = 0.01

F32 = mybir.dt.float32
BF16 = mybir.dt.bfloat16
I32 = mybir.dt.int32
ALU = mybir.AluOpType
ACT = mybir.ActivationFunctionType
AX = mybir.AxisListType.X
DVE_ENGINE = mybir.EngineType.DVE
PE_ENGINE = mybir.EngineType.PE


class Chain:

    def __init__(self, eng, sem):
        self.eng, self.sem, self.n = eng, sem, 0

    def done(self, ins):
        self.n += 1
        ins.then_inc(self.sem, 1)
        self.eng.wait_ge(self.sem, self.n)


def hold(eng, sem, value, passed):
    eng.wait_ge(sem, value)
    eng.sem_inc(passed, 1)


def spread(ap, shape):
    return ap.unsqueeze(2).to_broadcast(shape)


def repeat(ap, shape):
    return ap.unsqueeze(1).to_broadcast(shape)


def block_numbers(nc, engine, table, first, n):
    _, regs = nc.values_load_multi_w_load_instructions(
        table[0:1, bass.ds(first, n)], engines=(engine,), min_val=0, max_val=NB - 1,
        skip_runtime_bounds_check_because="counts of blocks that start at or before a tile, less one")
    return regs


class IndirectCount:

    def __init__(self, nc, ctx):
        self.sems = [ctx.enter_context(nc.semaphore(f"indirect{s}")) for s in range(2)]
        self.before = 0

    def after(self, steps):
        return steps * (16 * HALF) + self.before

    def end(self, steps):
        self.before += 16 * HALF * steps


class Order:

    def __init__(self, sb, dram, name):
        self.name = name
        self.count = sb(f"{name}_count", [P, NB], F32)
        self.block = sb(f"{name}_block", [1, T], I32)
        self.other = sb(f"{name}_other", [P, T], I32)
        self.low = sb(f"{name}_low", [P, T], F32)
        self.kind = sb(f"{name}_kind", [P, T], F32)
        self.records = dram(f"{name}_records", [P * T, 4], F32)


def rank_edges(nc, block, ctx, o, key_i, other_i, kind_i, k, slot_i, record):
    n = o.name

    def sb(name, shape, dt):
        return ctx.enter_context(nc.sbuf_tensor(f"{n}_{name}", shape, dt))

    def ps(name, shape, dt):
        return ctx.enter_context(nc.psum_tensor(f"{n}_{name}", shape, dt))

    def sem(name):
        return ctx.enter_context(nc.semaphore(f"{n}_{name}"))

    low_i = sb("low_i", [EP, EC], I32)
    high_i = sb("high_i", [EP, EC], I32)
    low_b = sb("low_b", [EP, EC], BF16)
    high_b = sb("high_b", [EP, EC], BF16)
    is_low = sb("is_low", [EP, 2, HCH, P], BF16)
    is_high = sb("is_high", [EP, 2, HCH, NB], BF16)
    seen = sb("seen", [P, NB, EC + 1], F32)
    going = sb("going", [P, NB, EC + 1], BF16)
    low_t = sb("low_t", [P, 2, RCH, EP], F32)
    same = sb("same", [EP, 2, RCH, EP], BF16)
    picked = sb("picked", [EP, 2, RCH, NB], F32)
    slot = sb("slot", [EP, EC], F32)
    part_i = sb("part_i", [EP, EC], I32)
    tile_i = sb("tile_i", [EP, EC], I32)
    part_f = sb("part_f", [EP, EC], F32)
    small_i = sb("small_i", [P, NB], I32)
    tiles = sb("tiles", [P, NB], F32)
    ends = sb("ends", [P, NB], F32)
    starts = sb("starts", [P, NB], F32)
    started = sb("started", [1, T, NB], BF16)
    block_f = sb("block_f", [1, T], F32)

    hist_ps = [ps(f"hist{s}", [P, 512], F32) for s in range(2)]
    turn_ps = [ps(f"turn{s}", [P, RCH, P], BF16) for s in range(2)]
    pair_ps = ps("pair", [EP, 2, 2, 512], F32)
    total_ps = hist_ps
    slot_ps = hist_ps

    onehots = sem("onehots")
    hist_done = sem("hist_done")
    hist_copied = sem("hist_copied")
    passed_act = sem("passed_act")
    chain = sem("chain")
    totals_ready = sem("totals_ready")
    totals_done = sem("totals_done")
    prefix_ready = sem("prefix_ready")
    ranked_onehots = sem("ranked_onehots")
    turned = sem("turned")
    turned_copied = sem("turned_copied")
    paired = sem("paired")
    masked = sem("masked")
    looked_up = sem("looked_up")
    picked_done = sem("picked_done")
    ranks_done = sem("ranks_done")
    passed_dve = sem("passed_dve")

    @block.vector
    def _(dve):
        ch = Chain(dve, chain)
        dve.sem_inc(hist_done, 2)
        dve.tensor_scalar(low_i[:, :], key_i[:, :], P - 1, None, ALU.bitwise_and)
        ch.done(dve.tensor_scalar(high_i[:, :], key_i[:, :], 7, None, ALU.logical_shift_right))
        dve.tensor_copy(low_b[:, :], low_i[:, :])
        dve.tensor_copy(high_b[:, :], high_i[:, :])
        dve.tensor_copy(record[:, :, 0], other_i[:, :])
        dve.tensor_copy(record[:, :, 1], low_i[:, :])
        dve.tensor_copy(record[:, :, 2], kind_i[:, :])
        dve.memset(record[:, :, 3], 0.0)
        dve.memset(going[:, :, 1:EC + 1], 1.0)
        ch.done(dve.memset(going[:, :, 0:1], 0.0))
        with dve.Fori(0, EC // (2 * HCH), 1) as it:
            for s in range(2):
                at = it * (2 * HCH) + s * HCH
                dve.wait_ge(hist_done, it * 2 + s + 1)
                dve.tensor_tensor(is_low[:, s], repeat(k.iota_b[0:EP, :], [EP, HCH, P]),
                                  spread(low_b[:, bass.ds(at, HCH)], [EP, HCH, P]), ALU.is_equal)
                dve.tensor_tensor(is_high[:, s], repeat(k.iota_b[0:EP, 0:NB], [EP, HCH, NB]),
                                  spread(high_b[:, bass.ds(at, HCH)], [EP, HCH, NB]), ALU.is_equal)\
                   .then_inc(onehots, 1)
        dve.wait_ge(hist_copied, EC // HCH + 2)
        dve.tensor_reduce(o.count[:, :], seen[:, :, 1:EC + 1], AX, ALU.add).then_inc(totals_ready, 1)
        dve.wait_ge(totals_done, 1)
        ch.done(dve.tensor_scalar(small_i[:, :], total_ps[1][:, 0:NB], float(P - 1), None, ALU.add))
        ch.done(dve.tensor_scalar(small_i[:, :], small_i[:, :], 7, None, ALU.logical_shift_right))
        ch.done(dve.tensor_copy(tiles[:, :], small_i[:, :]))
        ch.done(dve.tensor_tensor_scan(ends[:, :], k.ones[:, 0:NB], tiles[:, :], 0.0, ALU.mult, ALU.add))
        ch.done(dve.tensor_tensor(starts[:, :], ends[:, :], tiles[:, :], ALU.subtract))
        ch.done(dve.scalar_tensor_tensor(seen[:, :, 0], starts[:, :], float(P), total_ps[0][:, 0:NB],
                                         ALU.mult, ALU.add))
        flat = seen[:, :, :].rearrange("p h t -> p (h t)")
        dve.tensor_tensor_scan(flat, going[:, :, :].rearrange("p h t -> p (h t)"), flat, 0.0,
                               ALU.mult, ALU.add).then_inc(prefix_ready, 1)
        ch.done(dve.tensor_tensor(started[:, :, :], spread(k.iota_t[0:1, :], [1, T, NB]),
                                  repeat(starts[0:1, :], [1, T, NB]), ALU.is_ge))
        ch.done(dve.tensor_reduce(block_f[:, :], started[:, :, :], AX, ALU.add))
        dve.tensor_scalar(o.block[:, :], block_f[:, :], -1.0, None, ALU.add)

        with dve.Fori(0, EC // (2 * RCH), 1) as it:
            def columns(s):
                return bass.ds(it * (2 * RCH) + s * RCH, RCH)
            for s in range(2):
                dve.tensor_tensor(is_low[:, s, 0:RCH], repeat(k.iota_b[0:EP, :], [EP, RCH, P]),
                                  spread(low_b[:, columns(s)], [EP, RCH, P]), ALU.is_equal)
                dve.tensor_tensor(is_high[:, s, 0:RCH], repeat(k.iota_b[0:EP, 0:NB], [EP, RCH, NB]),
                                  spread(high_b[:, columns(s)], [EP, RCH, NB]), ALU.is_equal)\
                   .then_inc(ranked_onehots, 1)
            for s in range(2):
                dve.wait_ge(paired, it * 2 + s + 1)
                for q in range(2):
                    last = dve.tensor_tensor(
                        same[:, s, 4 * q:4 * q + 4],
                        pair_ps[:, s, q, 0:4 * EP].rearrange("p (j e) -> p j e", j=4),
                        repeat(k.earlier[0:EP, 0:EP], [EP, 4, EP]), ALU.mult)
                last.then_inc(masked, 1)
            for s in range(2):
                dve.wait_ge(looked_up, it * 2 + s + 1)
                dve.tensor_tensor(picked[:, s], slot_ps[s][0:EP, 0:RCH * NB].rearrange("p (j h) -> p j h", j=RCH),
                                  is_high[:, s, 0:RCH], ALU.mult).then_inc(picked_done, 1)
                dve.wait_ge(picked_done, it * 2 + s + 1)
                dve.tensor_reduce(slot[:, columns(s)], picked[:, s], AX, ALU.add).then_inc(ranks_done, 1)
        dve.wait_ge(ranks_done, EC // RCH)
        ch.done(dve.tensor_copy(slot_i[:, :], slot[:, :]))
        dve.tensor_scalar(part_i[:, :], slot_i[:, :], P - 1, None, ALU.bitwise_and)
        ch.done(dve.tensor_scalar(tile_i[:, :], slot_i[:, :], 7, None, ALU.logical_shift_right))
        dve.tensor_copy(part_f[:, :], part_i[:, :])
        ch.done(dve.tensor_copy(slot[:, :], tile_i[:, :]))
        ch.done(dve.scalar_tensor_tensor(slot_i[:, :], part_f[:, :], float(T), slot[:, :], ALU.mult, ALU.add))

    @block.tensor
    def _(pe):
        with pe.Fori(0, EC // (2 * HCH), 1) as it:
            for s in range(2):
                pe.wait_ge(onehots, it * 2 + s + 1)
                pe.wait_ge(hist_copied, it * 2 + s + 1)
                for j in range(HCH):
                    last = pe.matmul(hist_ps[s][:, j * NB:(j + 1) * NB], is_low[:, s, j], is_high[:, s, j],
                                     start=True, stop=True)
                last.then_inc(hist_done, 1)
        pe.wait_ge(totals_ready, 1)
        pe.matmul(total_ps[0][:, 0:NB], k.earlier[:, :], o.count[:, :], start=True, stop=True)
        pe.matmul(total_ps[1][:, 0:NB], k.ones[:, :], o.count[:, :], start=True, stop=True)\
          .then_inc(totals_done, 1)
        pe.wait_ge(prefix_ready, 1)
        with pe.Fori(0, EC // (2 * RCH), 1) as it:
            for s in range(2):
                pe.wait_ge(ranked_onehots, it * 2 + s + 1)
                for j in range(RCH):
                    last = pe.transpose(turn_ps[s][:, j, 0:EP], is_low[:, s, j], k.ident_b[0:EP, 0:EP])
                last.then_inc(turned, 1)
            for s in range(2):
                pe.wait_ge(turned_copied, it * 2 + s + 1)
                for j in range(RCH):
                    last = pe.matmul(pair_ps[:, s, j // 4, j % 4 * EP:(j % 4 + 1) * EP], low_t[:, s, j],
                                     low_t[:, s, j], start=True, stop=True)
                last.then_inc(paired, 1)
            for s in range(2):
                pe.wait_ge(masked, it * 2 + s + 1)
                for j in range(RCH):
                    out = slot_ps[s][0:EP, j * NB:(j + 1) * NB]
                    pe.matmul(out, low_t[:, s, j], seen[:, :, bass.ds(it * (2 * RCH) + s * RCH + j, 1)].rearrange("p h o -> p (h o)"),
                              start=True, stop=False)
                    last = pe.matmul(out, same[:, s, j], is_high[:, s, j], start=False, stop=True)
                last.then_inc(looked_up, 1)

    @block.scalar
    def _(act):
        act.sem_inc(hist_copied, 2)
        with act.Fori(0, EC // (2 * HCH), 1) as it:
            for s in range(2):
                hold(act, hist_done, it * 2 + s + 3, passed_act)
                act.copy(seen[:, :, bass.ds(it * (2 * HCH) + s * HCH + 1, HCH)],
                         hist_ps[s][:, 0:HCH * NB].rearrange("p (t h) -> p h t", t=HCH)).then_inc(hist_copied, 1)
        with act.Fori(0, EC // (2 * RCH), 1) as it:
            for s in range(2):
                act.wait_ge(turned, it * 2 + s + 1)
                act.copy(low_t[:, s], turn_ps[s][:, :, 0:EP]).then_inc(turned_copied, 1)


def scatter_records(nc, block, ctx, o, slot_i, record, moved):
    n = o.name
    slots = ctx.enter_context(nc.sbuf_tensor(f"{n}_slots", [EP, 2, HALF], I32))
    rows = ctx.enter_context(nc.sbuf_tensor(f"{n}_rows", [EP, 2, HALF, 4], F32))
    staged = ctx.enter_context(nc.semaphore(f"{n}_staged"))
    written = moved.sems
    passed = ctx.enter_context(nc.semaphore(f"{n}_passed_pool"))

    @block.gpsimd
    def _(pool):
        def step(it, s, first):
            at = it * (2 * HALF) + s * HALF
            if not first:
                hold(pool, written[s], moved.after(it), passed)
            pool.tensor_copy(slots[:, s], slot_i[:, bass.ds(at, HALF)])
            pool.tensor_copy(rows[:, s], record[:, bass.ds(at, HALF), :]).then_inc(staged, 1)
            hold(pool, staged, it * 2 + s + 1, passed)
            for j in range(HALF):
                pool.indirect_dma_start(o.records, bass.IndirectOffsetOnAxis(ap=slots[:, s, j:j + 1], axis=0),
                                        rows[:, s, j], None).then_inc(written[s], 16)

        for s in range(2):
            step(0, s, True)
        with pool.Fori(1, EC // (2 * HALF), 1) as it:
            for s in range(2):
                step(it, s, False)
        for s in range(2):
            pool.wait_ge(written[s], moved.after(EC // (2 * HALF)))

    moved.end(EC // (2 * HALF))


def fetch_records(nc, block, ctx, o, rows_per_other=1):
    n = o.name
    got = ctx.enter_context(nc.sbuf_tensor(f"{n}_got", [P, T, 4], F32))
    fetched = ctx.enter_context(nc.semaphore(f"{n}_fetched"))

    @block.sync
    def _(sp):
        sp.dma_start(got[:, :, :], o.records.rearrange("(p t) c -> p t c", p=P)).then_inc(fetched, 16)
        sp.wait_ge(fetched, 16)

    @block.vector
    def _(dve):
        dve.wait_ge(fetched, 16)
        dve.tensor_copy(o.other[:, :], got[:, :, 0])
        dve.tensor_copy(o.low[:, :], got[:, :, 1])
        dve.tensor_copy(o.kind[:, :], got[:, :, 2])


class Consts:
    pass


def make_consts(nc, ctx, sb):
    k = Consts()
    k.iota_i = sb("iota_i", [P, T], I32)
    k.iota_t = sb("iota_t", [P, T], F32)
    k.iota_b = sb("iota_b", [P, P], BF16)
    k.ident = sb("ident", [P, P], F32)
    k.ident_b = sb("ident_b", [P, P], BF16)
    k.ones = sb("ones", [P, P], F32)
    k.earlier = sb("earlier", [P, P], F32)
    return k


def setup(nc, ctx, k, orders, x_dram, x_sb, loads):
    filler = ctx.enter_context(nc.sbuf_tensor("filler", [P, T, 4], F32))
    loaded = ctx.enter_context(nc.semaphore("loaded"))
    pool_step = ctx.enter_context(nc.semaphore("pool_step"))
    iota_ready = ctx.enter_context(nc.semaphore("iota_ready"))
    tail_zero = ctx.enter_context(nc.semaphore("tail_zero"))
    filler_ready = ctx.enter_context(nc.semaphore("filler_ready"))
    filled = ctx.enter_context(nc.semaphore("filled"))
    with nc.Block() as block:
        @block.sync
        def _(sp):
            for dst, src in loads:
                sp.dma_start(dst, src).then_inc(loaded, 16)
            sp.wait_ge(tail_zero, 1)
            sp.dma_start(x_sb[:, 0:(NB - 1) * C].rearrange("p (b c) -> p b c", b=NB - 1),
                         x_dram[0:(NB - 1) * P, :].rearrange("(b p) c -> p b c", p=P)).then_inc(loaded, 16)
            sp.dma_start(x_sb[0:TAIL, (NB - 1) * C:NB * C], x_dram[(NB - 1) * P:N, :]).then_inc(loaded, 16)
            sp.wait_ge(loaded, 16 * (len(loads) + 2))

        @block.scalar
        def _(act):
            act.wait_ge(filler_ready, 1)
            for o in orders:
                act.dma_start(o.records.rearrange("(p t) c -> p t c", p=P), filler[:, :, :]).then_inc(filled, 16)
            act.wait_ge(filled, 16 * len(orders))

        @block.gpsimd
        def _(pool):
            pool.iota(k.iota_i[:, :], [[1, T]], base=0, channel_multiplier=0).then_inc(iota_ready, 1)
            pool.memset(k.ones[:, :], 1.0)
            pool.memset(k.earlier[:, :], 1.0).then_inc(pool_step, 1)
            pool.memset(k.ident[:, :], 0.0).then_inc(pool_step, 1)
            pool.wait_ge(pool_step, 2)
            pool.affine_select(out=k.earlier[:, :], in_=k.earlier[:, :], compare_op=ALU.is_gt, fill=0.0,
                               base=0, pattern=[[1, P]], channel_multiplier=-1)
            pool.affine_select(out=k.ident[:, :], in_=k.ident[:, :], compare_op=ALU.not_equal, fill=1.0,
                               base=0, pattern=[[1, P]], channel_multiplier=-1).then_inc(pool_step, 1)

        @block.vector
        def _(dve):
            dve.memset(x_sb[:, (NB - 1) * C:NB * C], 0.0)
            dve.memset(filler[:, :, :], 0.0).then_inc(tail_zero, 1)
            dve.wait_ge(tail_zero, 1)
            dve.memset(filler[:, :, 1:2], -1.0).then_inc(filler_ready, 1)
            dve.wait_ge(iota_ready, 1)
            dve.tensor_copy(k.iota_t[:, :], k.iota_i[:, :])
            dve.tensor_copy(k.iota_b[:, :], k.iota_i[:, 0:P])
            dve.wait_ge(pool_step, 3)
            dve.tensor_copy(k.ident_b[:, :], k.ident[:, :])


class Phase:

    def __init__(self, nc, ctx, name):
        self.nc, self.ctx, self.name = nc, ctx, name

    def sb(self, name, shape, dt=F32):
        return self.ctx.enter_context(self.nc.sbuf_tensor(f"{self.name}_{name}", shape, dt))

    def ps(self, name, shape, dt=F32):
        return self.ctx.enter_context(self.nc.psum_tensor(f"{self.name}_{name}", shape, dt))

    def sem(self, name):
        return self.ctx.enter_context(self.nc.semaphore(f"{self.name}_{name}"))


def blocks(t, width=C):
    return t[:, 0:NB * width].rearrange("p (b c) -> p b c", b=NB)


def inverse_root(dve, ch, y, a, t):
    ch.done(dve.reciprocal(y, y))
    ch.done(dve.tensor_tensor(t, y, y, ALU.mult))
    ch.done(dve.tensor_tensor(t, t, a, ALU.mult))
    ch.done(dve.tensor_scalar(t, t, -0.5, 1.5, ALU.mult, ALU.add))
    ch.done(dve.tensor_tensor(y, y, t, ALU.mult))


def degrees(nc, by_dst, by_src, root_d, root_s, mean_d):
    with ExitStack() as ctx, nc.Block() as block:
        f = Phase(nc, ctx, "deg")
        a = f.sb("a", [P, 2, NB])
        y = f.sb("y", [P, 2, NB])
        t = f.sb("t", [P, 2, NB])
        step, added, rooted = f.sem("step"), f.sem("added"), f.sem("rooted")

        @block.vector
        def _(dve):
            ch = Chain(dve, step)
            dve.tensor_scalar(a[:, 0], by_dst.count[:, :], 1.0, None, ALU.add)
            dve.tensor_scalar(a[:, 1], by_src.count[:, :], 1.0, None, ALU.add).then_inc(added, 1)
            ch.done(dve.tensor_scalar(mean_d[:, :], by_dst.count[:, :], 1.0, None, ALU.max))
            ch.done(dve.reciprocal(mean_d[:, :], mean_d[:, :]))
            dve.wait_ge(rooted, 1)
            inverse_root(dve, ch, y[:, :, :], a[:, :, :], t[:, :, :])
            dve.tensor_copy(root_d[:, :], y[:, 0])
            dve.tensor_copy(root_s[:, :], y[:, 1])

        @block.scalar
        def _(act):
            act.wait_ge(added, 1)
            act.activation(y[:, :, :], a[:, :, :], ACT.Sqrt).then_inc(rooted, 1)


def norm_relu(nc, name, src, dst, width, scale=None, gamma=None, beta=None, add_to=None):
    with ExitStack() as ctx, nc.Block() as block:
        f = Phase(nc, ctx, name)
        sq = f.sb("sq", [P, NB * width])
        mean = f.sb("mean", [P, NB])
        a = f.sb("a", [P, NB])
        y = f.sb("y", [P, NB])
        t = f.sb("t", [P, NB])
        step, centred, squared, var_ready, rooted = (f.sem(n) for n in (
            "step", "centred", "squared", "var_ready", "rooted"))
        s3, d3, q3 = blocks(src, width), blocks(dst, width), blocks(sq, width)
        full = [P, NB, width]

        @block.vector
        def _(dve):
            ch = Chain(dve, step)
            ch.done(dve.tensor_reduce(mean[:, :], s3, AX, ALU.add))
            ch.done(dve.tensor_scalar(mean[:, :], mean[:, :], 1.0 / width, None, ALU.mult))
            dve.tensor_tensor(d3, s3, spread(mean[:, :], full), ALU.subtract).then_inc(centred, 1)
            dve.wait_ge(squared, 1)
            ch.done(dve.tensor_reduce(a[:, :], q3, AX, ALU.add))
            dve.tensor_scalar(a[:, :], a[:, :], 1.0 / width, LN_EPS, ALU.mult, ALU.add).then_inc(var_ready, 1)
            dve.wait_ge(rooted, 1)
            inverse_root(dve, ch, y[:, :], a[:, :], t[:, :])
            if gamma is None:
                if scale is not None:
                    ch.done(dve.tensor_tensor(y[:, :], y[:, :], scale[:, :], ALU.mult))
                ch.done(dve.scalar_tensor_tensor(d3, d3, 0.0, spread(y[:, :], full), ALU.max, ALU.mult))
                return
            ch.done(dve.tensor_tensor(d3, d3, spread(y[:, :], full), ALU.mult))
            ch.done(dve.tensor_tensor(d3, d3, repeat(gamma[:, :], full), ALU.mult))
            ch.done(dve.tensor_tensor(d3, d3, repeat(beta[:, :], full), ALU.add))
            if add_to is not None:
                ch.done(dve.scalar_tensor_tensor(blocks(add_to, width), d3, 0.0, blocks(add_to, width),
                                                 ALU.max, ALU.add))
            else:
                ch.done(dve.scalar_tensor_tensor(d3, d3, 0.0, spread(scale[:, :], full), ALU.max, ALU.mult))

        @block.scalar
        def _(act):
            act.wait_ge(centred, 1)
            act.activation(sq[:, :], dst[:, 0:NB * width], ACT.Square).then_inc(squared, 1)
            act.wait_ge(var_ready, 1)
            act.activation(y[:, :], a[:, :], ACT.Sqrt).then_inc(rooted, 1)


DB = 5


def dense(nc, name, k, src, kc, nout, weight_loads, outs):
    with ExitStack() as ctx, nc.Block() as block:
        f = Phase(nc, ctx, name)
        w = f.sb("w", [P, kc, nout])
        staged_rows = f.sb("staged_rows", [P, DB, kc * P])
        rows_t = f.sb("rows_t", [P, DB, kc, P])
        turn = [f.ps(f"turn{s}", [P, kc, P]) for s in range(2)]
        prod = [f.ps(f"prod{s}", [P, nout]) for s in range(2)]
        loaded, staged, turned, turned_copied, product, copied, passed_act, passed_dve = (f.sem(n) for n in (
            "loaded", "staged", "turned", "turned_copied", "product", "copied", "passed_act", "passed_dve"))
        loads = weight_loads(w)

        @block.sync
        def _(sp):
            for dst, s in loads:
                sp.dma_start(dst, s).then_inc(loaded, 16)

        @block.scalar
        def _(act):
            with act.Fori(0, NB // DB, 1) as it:
                act.copy(staged_rows[:, :, :].rearrange("p j c -> p (j c)"),
                         src[:, bass.ds(it * (DB * kc * P), DB * kc * P)]).then_inc(staged, 1)
                for j in range(DB):
                    act.wait_ge(turned, it * DB + j + 1)
                    act.copy(rows_t[:, j], turn[j % 2][:, :, :]).then_inc(turned_copied, 1)

        @block.tensor
        def _(pe):
            pe.wait_ge(loaded, 16 * len(loads))

            def product_of(it, j):
                pe.wait_ge(turned_copied, it * DB + j + 1)
                pe.wait_ge(copied, it * DB + j + (2 if j == 0 else 1))
                for c0 in range(0, nout, 512):
                    c1 = min(c0 + 512, nout)
                    for c in range(kc):
                        last = pe.matmul(prod[j % 2][:, c0:c1], rows_t[:, j, c], w[:, c, c0:c1],
                                         start=(c == 0), stop=(c == kc - 1))
                last.then_inc(product, 1)

            with pe.Fori(0, NB // DB, 1) as it:
                pe.wait_ge(staged, it + 1)
                for j in range(DB):
                    for c in range(kc):
                        last = pe.transpose(turn[j % 2][:, c], staged_rows[:, j, c * P:(c + 1) * P], k.ident[:, :])
                    last.then_inc(turned, 1)
                    if j > 0:
                        product_of(it, j - 1)
                product_of(it, DB - 1)

        @block.vector
        def _(dve):
            dve.sem_inc(copied, 2)
            with dve.Fori(0, NB // DB, 1) as it:
                for j in range(DB):
                    hold(dve, product, it * DB + j + 1, passed_dve)
                    for c0, width, dst, bias in outs:
                        for a in range(c0, c0 + width, 512):
                            n = min(512, c0 + width - a)
                            to = dst[:, bass.ds((it * DB + j) * width + (a - c0), n)]
                            if bias is None:
                                last = dve.tensor_copy(to, prod[j % 2][:, a:a + n])
                            else:
                                last = dve.tensor_tensor(to, prod[j % 2][:, a:a + n], bias[:, a - c0:a - c0 + n], ALU.add)
                    last.then_inc(copied, 1)


def whole(weight):
    return lambda w: [(w[:, :, :], weight.rearrange("(k p) n -> p k n", p=P))]


def gather_rows(f, block, index, table, rows, width, landed, used):
    slots = f.sb("slots", [P, 2, HALF], I32)
    staged = f.sem("staged")
    passed = f.sem("passed_pool")

    @block.gpsimd
    def _(pool):
        with pool.Fori(0, T // BODY, 1) as it:
            for s in range(2):
                hold(pool, used, it * BODY + (s + 1) * HALF, passed)
                pool.tensor_copy(slots[:, s], index[:, bass.ds(it * BODY + s * HALF, HALF)]).then_inc(staged, 1)
                hold(pool, staged, it * 2 + s + 1, passed)
                for j in range(HALF):
                    pool.indirect_dma_start(rows[:, s * HALF + j, 0:width], None, table,
                                            bass.IndirectOffsetOnAxis(ap=slots[:, s, j:j + 1], axis=0))\
                        .then_inc(landed[s], 16)


def select_matrix(dve, k, o, sel, it, s):
    return dve.tensor_tensor(sel[:, s * HALF:(s + 1) * HALF], repeat(k.iota_t[:, 0:P], [P, HALF, P]),
                             spread(o.low[:, bass.ds(it * BODY + s * HALF, HALF)], [P, HALF, P]), ALU.is_equal)


def select_kind(dve, k, o, out, it, s):
    return dve.tensor_tensor(out, repeat(k.iota_t[:, 0:NREL], [P, HALF, NREL]),
                             spread(o.kind[:, bass.ds(it * BODY + s * HALF, HALF)], [P, HALF, NREL]), ALU.is_equal)


def add_tiles(nc, dve, o, acc, width, bank, it, first, n, done, done_start, added, lead):
    regs = block_numbers(nc, DVE_ENGINE, o.block, it * BODY + first, n)
    for i in range(n):
        tile = it * BODY + first + i
        dve.wait_ge(done, tile + done_start + 1)
        dve.wait_ge(added, tile + lead)
        to = acc[:, bass.ds(regs[i] * width, width)]
        dve.tensor_tensor(to, bank(first + i)[:, 0:width], to, ALU.add).then_inc(added, 1)


def aggregate(nc, name, k, moved, o, table, acc, count_kinds=False):
    with ExitStack() as ctx, nc.Block() as block:
        f = Phase(nc, ctx, name)
        width = C + NREL if count_kinds else C
        rows = f.sb("rows", [P, BODY, width])
        sel = f.sb("sel", [P, BODY, P])
        bank = [f.ps(f"sum{j}", [P, 512]) for j in range(8)]
        landed = moved.sems
        sel_ready, tile_done, added = f.sem("sel_ready"), f.sem("tile_done"), f.sem("added")

        gather_rows(f, block, o.other, table, rows, C, landed, tile_done)

        @block.vector
        def _(dve):
            dve.sem_inc(added, 8)
            with dve.Fori(0, T // BODY, 1) as it:
                for s in range(2):
                    if count_kinds:
                        select_kind(dve, k, o, rows[:, s * HALF:(s + 1) * HALF, C:width], it, s)
                    select_matrix(dve, k, o, sel, it, s).then_inc(sel_ready, 1)
                for s in range(2):
                    add_tiles(nc, dve, o, acc, width, lambda j: bank[j % 8], it, s * HALF, HALF,
                              tile_done, BODY, added, 8)

        @block.tensor
        def _(pe):
            pe.sem_inc(tile_done, BODY)
            with pe.Fori(0, T // BODY, 1) as it:
                for s in range(2):
                    pe.wait_ge(sel_ready, it * 2 + s + 1)
                    pe.wait_ge(landed[s], moved.after(it + 1))
                    for j in range(s * HALF, (s + 1) * HALF):
                        pe.wait_ge(added, it * BODY + j + 1)
                        pe.matmul(bank[j % 8][:, 0:width], sel[:, j], rows[:, j], start=True, stop=True)\
                          .then_inc(tile_done, 1)
    moved.end(T // BODY)


def turn_select(pe, k, turn, sel, first, n):
    for i in range(n):
        last = pe.transpose(turn[:, i], sel[:, first + i], k.ident[:, :])
    return last


QUAD = 4


def aggregate_kinds(nc, name, k, moved, o, index, table, share, acc):
    with ExitStack() as ctx, nc.Block() as block:
        f = Phase(nc, ctx, name)
        rows = f.sb("rows", [P, BODY, H1])
        sel = f.sb("sel", [P, BODY, P])
        sel_t = f.sb("sel_t", [P, BODY, P])
        kinds = f.sb("kinds", [P, BODY, NREL])
        part = f.sb("part", [P, BODY, NREL])
        weight = f.sb("weight", [P, BODY])
        turn = [f.ps(f"turn{s}", [P, QUAD, P]) for s in range(2)]
        share_ps = [f.ps(f"share{s}", [P, HALF, NREL]) for s in range(2)]
        bank = [f.ps(f"sum{j}", [P, 512]) for j in range(4)]
        landed = moved.sems
        (sel_ready, turned, turned_copied, shares, parted, weighed, scaled, tile_done, added) = (
            f.sem(n) for n in ("sel_ready", "turned", "turned_copied", "shares", "parted", "weighed",
                               "scaled", "tile_done", "added"))

        gather_rows(f, block, index, table, rows, H1, landed, tile_done)

        @block.vector
        def _(dve):
            dve.sem_inc(added, 4)
            with dve.Fori(0, T // BODY, 1) as it:
                for s in range(2):
                    select_kind(dve, k, o, kinds[:, s * HALF:(s + 1) * HALF], it, s)
                    select_matrix(dve, k, o, sel, it, s).then_inc(sel_ready, 1)
                for s in range(2):
                    half = slice(s * HALF, (s + 1) * HALF)
                    dve.wait_ge(shares, it * 2 + s + 1)
                    dve.tensor_tensor(part[:, half], share_ps[s][:, :, :], kinds[:, half], ALU.mult)\
                       .then_inc(parted, 1)
                    dve.wait_ge(parted, it * 2 + s + 1)
                    dve.tensor_reduce(weight[:, half], part[:, half], AX, ALU.add).then_inc(weighed, 1)
                    dve.wait_ge(weighed, it * 2 + s + 1)
                    dve.wait_ge(landed[s], moved.after(it + 1))
                    dve.tensor_tensor(rows[:, half], rows[:, half], spread(weight[:, half], [P, HALF, H1]),
                                      ALU.mult).then_inc(scaled, 1)
                for s in range(2):
                    add_tiles(nc, dve, o, acc, H1, lambda j: bank[j % 4], it, s * HALF, HALF,
                              tile_done, BODY, added, 4)

        @block.scalar
        def _(act):
            with act.Fori(0, T // BODY, 1) as it:
                for q in range(BODY // QUAD):
                    act.wait_ge(turned, it * (BODY // QUAD) + q + 1)
                    act.copy(sel_t[:, q * QUAD:(q + 1) * QUAD], turn[q % 2][:, :, :]).then_inc(turned_copied, 1)

        @block.tensor
        def _(pe):
            pe.sem_inc(tile_done, BODY)
            with pe.Fori(0, T // BODY, 1) as it:
                for s in range(2):
                    pe.wait_ge(sel_ready, it * 2 + s + 1)
                    for q in range(2 * s, 2 * s + 2):
                        turn_select(pe, k, turn[q % 2], sel, q * QUAD, QUAD).then_inc(turned, 1)
                    regs = block_numbers(nc, PE_ENGINE, o.block, it * BODY + s * HALF, HALF)
                    pe.wait_ge(turned_copied, it * (BODY // QUAD) + 2 * s + 2)
                    for j in range(HALF):
                        last = pe.matmul(share_ps[s][:, j], sel_t[:, s * HALF + j],
                                         share[:, bass.ds(regs[j] * NREL, NREL)], start=True, stop=True)
                    last.then_inc(shares, 1)
                for s in range(2):
                    pe.wait_ge(scaled, it * 2 + s + 1)
                    for j in range(s * HALF, (s + 1) * HALF):
                        pe.wait_ge(added, it * BODY + j + 1)
                        pe.matmul(bank[j % 4][:, 0:H1], sel[:, j], rows[:, j], start=True, stop=True)\
                          .then_inc(tile_done, 1)
    moved.end(T // BODY)


def edge_scores(nc, name, k, moved, o, table_k, q, scores, top):
    with ExitStack() as ctx, nc.Block() as block:
        f = Phase(nc, ctx, name)
        nq = BODY // QUAD
        rows = f.sb("rows", [P, BODY, C])
        sel = f.sb("sel", [P, BODY, P])
        sel_t = f.sb("sel_t", [P, 2, QUAD, P])
        bar = f.sb("bar", [P, 2, QUAD, P])
        score = f.sb("score", [P, 2, QUAD * HEADS])
        masked = f.sb("masked", [P, HEADS, P])
        tile_top = f.sb("tile_top", [P, BODY, HEADS])
        turn = f.ps("turn", [P, QUAD, P])
        q_ps = [f.ps(f"q{s}", [P, 2, C]) for s in range(2)]
        wide = [f.ps(f"wide{s}", [P, HEADS, P]) for s in range(QUAD)]
        landed = moved.sems
        (sel_ready, turned, sel_t_ready, bar_ready, queries, multiplied, scored, kept, widened, tile_max,
         raised, passed_act, passed_dve) = (
            f.sem(n) for n in ("sel_ready", "turned", "sel_t_ready", "bar_ready", "queries", "multiplied",
                               "scored", "kept", "widened", "tile_max", "raised", "passed_act",
                               "passed_dve"))

        gather_rows_quads(f, block, o.other, table_k, rows, C, landed, scored, nq)

        @block.vector
        def _(dve):
            dve.sem_inc(scored, nq)
            dve.sem_inc(raised, 2 * QUAD)

            def dot(it, i):
                n = it * nq + i
                if i % 2 == 0:
                    dve.wait_ge(landed[i // 2], moved.after(it + 1))
                dve.wait_ge(queries, n + 1)
                for h in range(2):
                    j = i * QUAD + 2 * h
                    last = dve.tensor_tensor(rows[:, j:j + 2], rows[:, j:j + 2], q_ps[h][:, :, :], ALU.mult)
                last.then_inc(multiplied, 1)
                dve.wait_ge(multiplied, n + 1)
                dve.wait_ge(kept, n + 1)
                dve.tensor_reduce(score[:, i % 2], rows[:, i * QUAD:(i + 1) * QUAD].rearrange(
                    "p j (h d) -> p (j h) d", h=HEADS), AX, ALU.add).then_inc(scored, 1)

            def raise_top(it, i):
                regs = block_numbers(nc, DVE_ENGINE, o.block, it * BODY + i * QUAD, QUAD)
                dve.wait_ge(bar_ready, it * nq + i + 1)
                for t in range(QUAD):
                    n = it * BODY + i * QUAD + t
                    hold(dve, widened, n + 1, passed_dve)
                    for h in range(HEADS):
                        last = dve.tensor_tensor_reduce(
                            masked[:, h], wide[t][:, h], bar[:, i % 2, t], 1.0, -BIG, ALU.add, ALU.max,
                            tile_top[:, i * QUAD + t, h:h + 1])
                    last.then_inc(tile_max, 1)
                    dve.wait_ge(tile_max, n + 1)
                    dve.wait_ge(raised, n + 2 * QUAD)
                    to = top[:, bass.ds(regs[t] * HEADS, HEADS)]
                    dve.tensor_tensor(to, tile_top[:, i * QUAD + t], to, ALU.max).then_inc(raised, 1)

            with dve.Fori(0, T // BODY, 1) as it:
                for s in range(2):
                    select_matrix(dve, k, o, sel, it, s).then_inc(sel_ready, 1)
                dot(it, 0)
                for i in range(1, nq):
                    dot(it, i)
                    raise_top(it, i - 1)
                raise_top(it, nq - 1)

        @block.scalar
        def _(act):
            act.sem_inc(kept, 2)
            with act.Fori(0, T // BODY, 1) as it:
                def keep(i):
                    hold(act, scored, it * nq + i + nq + 1, passed_act)
                    act.copy(scores[:, bass.ds((it * nq + i) * (QUAD * HEADS), QUAD * HEADS)], score[:, i % 2])\
                       .then_inc(kept, 1)
                for i in range(nq):
                    act.wait_ge(turned, it * nq + i + 1)
                    act.copy(sel_t[:, i % 2], turn[:, :, :]).then_inc(sel_t_ready, 1)
                    act.wait_ge(raised, it * BODY + (i + 1) * QUAD)
                    act.activation(bar[:, i % 2], turn[:, :, :], ACT.Copy, bias=-BIG, scale=BIG)\
                       .then_inc(bar_ready, 1)
                    if i > 0:
                        keep(i - 1)
                keep(nq - 1)

        @block.tensor
        def _(pe):
            def query(it, i, regs):
                n = it * nq + i
                if i % 2 == 0:
                    pe.wait_ge(sel_ready, it * 2 + i // 2 + 1)
                pe.wait_ge(bar_ready, n)
                turn_select(pe, k, turn, sel, i * QUAD, QUAD).then_inc(turned, 1)
                pe.wait_ge(sel_t_ready, n + 1)
                pe.wait_ge(scored, n + nq)
                for t in range(QUAD):
                    last = pe.matmul(q_ps[t // 2][:, t % 2], sel_t[:, i % 2, t], q[:, bass.ds(regs[t] * C, C)],
                                     start=True, stop=True)
                last.then_inc(queries, 1)

            def widen(it, i):
                pe.wait_ge(scored, it * nq + i + nq + 1)
                for t in range(QUAD):
                    pe.wait_ge(raised, it * BODY + i * QUAD + t + QUAD + 1)
                    for h in range(HEADS):
                        last = pe.matmul(wide[t][:, h], score[:, i % 2, t * HEADS + h:t * HEADS + h + 1]
                                         .to_broadcast([P, P]), k.ident[:, :], start=True, stop=True)
                    last.then_inc(widened, 1)

            with pe.Fori(0, T // BODY, 1) as it:
                for i in range(nq):
                    regs = block_numbers(nc, PE_ENGINE, o.block, it * BODY + i * QUAD, QUAD)
                    query(it, i, regs)
                    if i > 0:
                        widen(it, i - 1)
                widen(it, nq - 1)
    moved.end(T // BODY)


def gather_rows_quads(f, block, index, table, rows, width, landed, scored, nq):
    slots = f.sb("slots", [P, 2, HALF], I32)
    staged = f.sem("staged")
    passed = f.sem("passed_pool")

    @block.gpsimd
    def _(pool):
        with pool.Fori(0, T // BODY, 1) as it:
            for s in range(2):
                hold(pool, scored, it * nq + 2 * (s + 1), passed)
                pool.tensor_copy(slots[:, s], index[:, bass.ds(it * BODY + s * HALF, HALF)]).then_inc(staged, 1)
                hold(pool, staged, it * 2 + s + 1, passed)
                for j in range(HALF):
                    pool.indirect_dma_start(rows[:, s * HALF + j, 0:width], None, table,
                                            bass.IndirectOffsetOnAxis(ap=slots[:, s, j:j + 1], axis=0))\
                        .then_inc(landed[s], 16)


def mix_values(nc, name, k, moved, o, table_v, scores, top, acc):
    with ExitStack() as ctx, nc.Block() as block:
        f = Phase(nc, ctx, name)
        nq = BODY // QUAD
        width = C + HEADS
        rows = f.sb("rows", [P, BODY, width])
        sel = f.sb("sel", [P, BODY, P])
        sel_t = f.sb("sel_t", [P, 2, QUAD, P])
        below = f.sb("below", [P, BODY, HEADS])
        turn = [f.ps(f"turn{s}", [P, QUAD, P]) for s in range(2)]
        top_ps = [f.ps(f"top{s}", [P, QUAD, HEADS]) for s in range(2)]
        bank = [f.ps(f"sum{j}", [P, 512]) for j in range(4)]
        landed = moved.sems
        (sel_ready, turned, sel_t_ready, tops, shifted, weights, weighted, tile_done, added) = (
            f.sem(n) for n in ("sel_ready", "turned", "sel_t_ready", "tops", "shifted", "weights", "weighted",
                               "tile_done", "added"))

        gather_rows(f, block, o.other, table_v, rows, C, landed, tile_done)

        @block.vector
        def _(dve):
            dve.sem_inc(added, 4)

            def shift(it, i):
                dve.wait_ge(tops, it * nq + i + 1)
                dve.tensor_tensor(below[:, i * QUAD:(i + 1) * QUAD].rearrange("p j h -> p (j h)"),
                                  scores[:, bass.ds((it * nq + i) * (QUAD * HEADS), QUAD * HEADS)],
                                  top_ps[i % 2][:, :, :].rearrange("p j h -> p (j h)"), ALU.subtract)\
                   .then_inc(shifted, 1)

            def weigh(it, i):
                if i % 2 == 0:
                    dve.wait_ge(landed[i // 2], moved.after(it + 1))
                dve.wait_ge(weights, it * nq + i + 1)
                tiles = slice(i * QUAD, (i + 1) * QUAD)
                v = rows[:, tiles, 0:C].rearrange("p j (h d) -> p j h d", h=HEADS)
                dve.tensor_tensor(v, v, rows[:, tiles, C:width].unsqueeze(3).to_broadcast([P, QUAD, HEADS, HD]),
                                  ALU.mult).then_inc(weighted, 1)

            def add(it, i):
                add_tiles(nc, dve, o, acc, width, lambda j: bank[j % 4], it, i * QUAD, QUAD,
                          tile_done, BODY, added, 4)

            with dve.Fori(0, T // BODY, 1) as it:
                for s in range(2):
                    select_matrix(dve, k, o, sel, it, s).then_inc(sel_ready, 1)
                shift(it, 0)
                shift(it, 1)
                weigh(it, 0)
                shift(it, 2)
                weigh(it, 1)
                add(it, 0)
                shift(it, 3)
                weigh(it, 2)
                add(it, 1)
                weigh(it, 3)
                add(it, 2)
                add(it, 3)

        @block.scalar
        def _(act):
            with act.Fori(0, T // BODY, 1) as it:
                def exponentials(i):
                    act.wait_ge(shifted, it * nq + i + 1)
                    act.activation(rows[:, i * QUAD:(i + 1) * QUAD, C:width], below[:, i * QUAD:(i + 1) * QUAD],
                                   ACT.Exp, scale=float(HD) ** -0.5).then_inc(weights, 1)
                for i in range(nq):
                    act.wait_ge(turned, it * nq + i + 1)
                    act.copy(sel_t[:, i % 2], turn[i % 2][:, :, :]).then_inc(sel_t_ready, 1)
                    if i > 0:
                        exponentials(i - 1)
                exponentials(nq - 1)

        @block.tensor
        def _(pe):
            pe.sem_inc(tile_done, BODY)

            def look_up(it, i):
                if i % 2 == 0:
                    pe.wait_ge(sel_ready, it * 2 + i // 2 + 1)
                turn_select(pe, k, turn[i % 2], sel, i * QUAD, QUAD).then_inc(turned, 1)
                regs = block_numbers(nc, PE_ENGINE, o.block, it * BODY + i * QUAD, QUAD)
                pe.wait_ge(sel_t_ready, it * nq + i + 1)
                for t in range(QUAD):
                    last = pe.matmul(top_ps[i % 2][:, t], sel_t[:, i % 2, t], top[:, bass.ds(regs[t] * HEADS, HEADS)],
                                     start=True, stop=True)
                last.then_inc(tops, 1)

            def add_up(it, i):
                pe.wait_ge(weighted, it * nq + i + 1)
                for j in range(i * QUAD, (i + 1) * QUAD):
                    pe.wait_ge(added, it * BODY + j + 1)
                    pe.matmul(bank[j % 4][:, 0:width], sel[:, j], rows[:, j], start=True, stop=True)\
                      .then_inc(tile_done, 1)

            with pe.Fori(0, T // BODY, 1) as it:
                look_up(it, 0)
                look_up(it, 1)
                look_up(it, 2)
                add_up(it, 0)
                look_up(it, 3)
                add_up(it, 1)
                add_up(it, 2)
                add_up(it, 3)
    moved.end(T // BODY)


def keep_largest(nc, name, src, dst):
    with ExitStack() as ctx, nc.Block() as block:
        f = Phase(nc, ctx, name)
        row = f.sb("row", [P, DB, C])
        left = f.sb("left", [P, DB, C])
        eight = f.sb("eight", [P, DB, 8])
        staged, found, struck, masked = f.sem("staged"), f.sem("found"), f.sem("struck"), f.sem("masked")
        passed, passed_dve = f.sem("passed_act"), f.sem("passed_dve")
        rounds = MAXK // 8

        @block.scalar
        def _(act):
            act.sem_inc(masked, 1)
            with act.Fori(0, NB // DB, 1) as it:
                hold(act, masked, it + 1, passed)
                for to in (row, left):
                    last = act.copy(to[:, :, :].rearrange("p j c -> p (j c)"), src[:, bass.ds(it * (DB * C), DB * C)])
                last.then_inc(staged, 1)

        @block.vector
        def _(dve):
            with dve.Fori(0, NB // DB, 1) as it:
                hold(dve, staged, it + 1, passed_dve)
                for r in range(rounds):
                    for j in range(DB):
                        if r > 0:
                            hold(dve, struck, it * (rounds * DB) + (r - 1) * DB + j + 1, passed_dve)
                        dve.max(eight[:, j], left[:, j]).then_inc(found, 1)
                    for j in range(DB):
                        n = it * (rounds * DB) + r * DB + j + 1
                        hold(dve, found, n, passed_dve)
                        dve.match_replace(left[:, j], eight[:, j], left[:, j], -BIG).then_inc(struck, 1)
                dve.wait_ge(struck, it * (rounds * DB) + rounds * DB)
                dve.scalar_tensor_tensor(dst[:, bass.ds(it * (DB * C), DB * C)],
                                         left[:, :, :].rearrange("p j c -> p (j c)"), -BIG,
                                         row[:, :, :].rearrange("p j c -> p (j c)"), ALU.is_equal, ALU.mult)\
                   .then_inc(masked, 1)


def batch_norm(nc, name, k, y, gamma, beta, x):
    with ExitStack() as ctx, nc.Block() as block:
        f = Phase(nc, ctx, name)
        sq = f.sb("sq", [P, NB * C])
        mean = f.sb("mean", [P, C])
        a = f.sb("a", [P, C])
        r = f.sb("r", [P, C])
        t = f.sb("t", [P, C])
        sum_ps = [f.ps(f"sum{s}", [P, C]) for s in range(2)]
        step, summed, centred, squared, var_ready, rooted = (f.sem(n) for n in (
            "step", "summed", "centred", "squared", "var_ready", "rooted"))
        y3, full = blocks(y), [P, NB, C]

        @block.tensor
        def _(pe):
            def column_sums(out, src):
                for b in range(NB):
                    rows = P if b < NB - 1 else TAIL
                    last = pe.matmul(out, k.ones[0:rows, :], src[0:rows, b * C:(b + 1) * C],
                                     start=(b == 0), stop=(b == NB - 1))
                last.then_inc(summed, 1)
            column_sums(sum_ps[0][:, :], y)
            pe.wait_ge(squared, 1)
            column_sums(sum_ps[1][:, :], sq)

        @block.vector
        def _(dve):
            ch = Chain(dve, step)
            dve.wait_ge(summed, 1)
            ch.done(dve.tensor_scalar(mean[:, :], sum_ps[0][:, :], 1.0 / N, None, ALU.mult))
            dve.tensor_tensor(y3, y3, repeat(mean[:, :], full), ALU.subtract).then_inc(centred, 1)
            dve.wait_ge(summed, 2)
            dve.tensor_scalar(a[:, :], sum_ps[1][:, :], 1.0 / N, BN_EPS, ALU.mult, ALU.add).then_inc(var_ready, 1)
            dve.wait_ge(rooted, 1)
            inverse_root(dve, ch, r[:, :], a[:, :], t[:, :])
            ch.done(dve.tensor_tensor(r[:, :], r[:, :], gamma[:, :], ALU.mult))
            ch.done(dve.tensor_tensor(y3, y3, repeat(r[:, :], full), ALU.mult))
            ch.done(dve.tensor_tensor(y3, y3, repeat(beta[:, :], full), ALU.add))
            ch.done(dve.scalar_tensor_tensor(y[:, :], y[:, :], SLOPE, y[:, :], ALU.mult, ALU.max))
            dve.tensor_tensor(x[:, :], x[:, :], y[:, :], ALU.add)

        @block.scalar
        def _(act):
            act.wait_ge(centred, 1)
            act.activation(sq[:, :], y[:, :], ACT.Square).then_inc(squared, 1)
            act.wait_ge(var_ready, 1)
            act.activation(r[:, :], a[:, :], ACT.Sqrt).then_inc(rooted, 1)


def store_table(nc, name, stores, work=None):
    with ExitStack() as ctx, nc.Block() as block:
        f = Phase(nc, ctx, name)
        stored, step = f.sem("stored"), f.sem("step")

        @block.sync
        def _(sp):
            for table, src, width in stores:
                sp.dma_start(table.rearrange("(b p) c -> p b c", p=P), blocks(src, width)).then_inc(stored, 16)
            sp.wait_ge(stored, 16 * len(stores))

        if work is not None:
            @block.vector
            def _(dve):
                work(dve, Chain(dve, step))


def vector_work(nc, name, work):
    with ExitStack() as ctx, nc.Block() as block:
        step = Phase(nc, ctx, name).sem("step")

        @block.vector
        def _(dve):
            work(dve, Chain(dve, step))


def load(nc, name, loads):
    with ExitStack() as ctx, nc.Block() as block:
        loaded = Phase(nc, ctx, name).sem("loaded")

        @block.sync
        def _(sp):
            for dst, src in loads:
                sp.dma_start(dst, src).then_inc(loaded, 16)
            sp.wait_ge(loaded, 16 * len(loads))


def clear_semaphores(nc):
    used = sorted(nc.released_uncleared_semaphores)
    with nc.Block() as block:
        @block.gpsimd
        def _(pool):
            first = used[0]
            for a, b in zip(used, used[1:] + [None]):
                if b != a + 1:
                    pool.sem_clear(range(first, a + 1))
                    first = b


def on_all(vector):
    return vector.partition_broadcast(P)


def build(nc, A, out):
    with ExitStack() as top:
        def sb(name, shape, dt=F32):
            return top.enter_context(nc.sbuf_tensor(name, shape, dt))

        def dram(name, shape, dt=F32):
            return nc.dram_tensor(name, shape, dt, kind="Internal").ap()

        k = make_consts(nc, top, sb)
        by_dst = Order(sb, dram, "dst")
        by_src = Order(sb, dram, "src")
        moved = IndirectCount(nc, top)
        x = sb("x_sb", [P, NB * C])
        root_d = sb("root_d", [P, NB])
        root_s = sb("root_s", [P, NB])
        mean_d = sb("mean_d", [P, NB])
        share = sb("share", [P, NB * NREL])
        table = dram("table", [NPAD, C])
        table_v = dram("table_v", [NPAD, C])
        table_r = dram("table_r", [NPAD * NREL, H1])

        with ExitStack() as ctx:
            def tmp(name, shape, dt):
                return ctx.enter_context(nc.sbuf_tensor(name, shape, dt))
            src_i = tmp("src_i", [EP, EC], I32)
            dst_i = tmp("dst_i", [EP, EC], I32)
            kind_i = tmp("kind_i", [EP, EC], I32)
            slot_d = tmp("slot_d", [EP, EC], I32)
            record_d = tmp("record_d", [EP, EC, 4], F32)
            slot_s = tmp("slot_s", [EP, EC], I32)
            record_s = tmp("record_s", [EP, EC, 4], F32)
            with ExitStack() as c:
                setup(nc, c, k, (by_dst, by_src), A["x"], x,
                      [(t[:, :], A[name].rearrange("(p t) -> p t", p=EP))
                       for t, name in ((src_i, "src"), (dst_i, "dst"), (kind_i, "edge_type_8"))])
            with ExitStack() as c, nc.Block() as block:
                rank_edges(nc, block, c, by_dst, dst_i, src_i, kind_i, k, slot_d, record_d)
            with ExitStack() as c, nc.Block() as block:
                scatter_records(nc, block, c, by_dst, slot_d, record_d, moved)
                rank_edges(nc, block, c, by_src, src_i, dst_i, kind_i, k, slot_s, record_s)
            with ExitStack() as c, nc.Block() as block:
                scatter_records(nc, block, c, by_src, slot_s, record_s, moved)
                fetch_records(nc, block, c, by_dst)
            with ExitStack() as c, nc.Block() as block:
                fetch_records(nc, block, c, by_src)
        degrees(nc, by_dst, by_src, root_d, root_s, mean_d)

        def finish():
            with ExitStack() as c, nc.Block() as block:
                stored = Phase(nc, c, "out").sem("stored")

                @block.sync
                def _(sp):
                    sp.dma_start(out[0:(NB - 1) * P, :].rearrange("(b p) c -> p b c", p=P),
                                 x[:, 0:(NB - 1) * C].rearrange("p (b c) -> p b c", b=NB - 1)).then_inc(stored, 16)
                    sp.dma_start(out[(NB - 1) * P:N, :], x[0:TAIL, (NB - 1) * C:NB * C]).then_inc(stored, 16)
                    sp.wait_ge(stored, 32)

        with ExitStack() as ctx:
            f = Phase(nc, ctx, "l0")
            acc = f.sb("acc", [P, NB * AW])
            g = f.sb("g", [P, NB * C])
            wide = f.sb("wide", [P, NB * CW])
            b1, gamma1, beta1 = (f.sb(n, [P, CW]) for n in ("b1", "gamma1", "beta1"))
            b2, gamma2, beta2 = (f.sb(n, [P, C]) for n in ("b2", "gamma2", "beta2"))
            load(nc, "l0_load", [(t[:, :], on_all(A[f"L0_gnn_{n}"])) for t, n in (
                (b1, "b1"), (gamma1, "gamma1"), (beta1, "beta1"), (b2, "b2"), (gamma2, "gamma2"), (beta2, "beta2"))])
            norm_relu(nc, "l0_in", x, g, C, scale=root_d)
            acc_k = blocks(acc, AW)

            def start_acc(dve, ch):
                dve.tensor_copy(acc_k[:, :, 0:C], blocks(g))
                dve.memset(acc_k[:, :, C:AW], 0.0)
            store_table(nc, "l0_t1", [(table, g, C)], start_acc)
            aggregate(nc, "l0_a1", k, moved, by_dst, table, acc, count_kinds=True)

            def end_acc(dve, ch):
                dve.tensor_tensor(blocks(g), acc_k[:, :, 0:C], spread(root_d[:, :], [P, NB, C]), ALU.mult)
                ch.done(dve.tensor_scalar(blocks(share, NREL), acc_k[:, :, C:AW], 1.0, None, ALU.max))
                dve.reciprocal(share[:, :], share[:, :])
            vector_work(nc, "l0_e1", end_acc)
            dense(nc, "l0_w1", k, g, C // P, CW, whole(A["L0_gnn_W1"]), [(0, CW, wide, b1)])
            norm_relu(nc, "l0_mid", wide, wide, CW, scale=root_d, gamma=gamma1, beta=beta1)
            dense(nc, "l0_w2", k, wide, CW // P, C, whole(A["L0_gnn_W2"]), [(0, C, acc, None)])
            store_table(nc, "l0_t2", [(table, acc, C)])
            aggregate(nc, "l0_a2", k, moved, by_dst, table, acc)

            def end_acc2(dve, ch):
                ch.done(dve.tensor_tensor(blocks(g), blocks(acc), spread(root_d[:, :], [P, NB, C]), ALU.mult))
                dve.tensor_tensor(blocks(g), blocks(g), repeat(b2[:, :], [P, NB, C]), ALU.add)
            vector_work(nc, "l0_e2", end_acc2)
            norm_relu(nc, "l0_out", g, g, C, gamma=gamma2, beta=beta2, add_to=x)

        with ExitStack() as ctx:
            f = Phase(nc, ctx, "l1")
            acc = f.sb("acc", [P, NB * C])
            g = f.sb("g", [P, NB * C])
            norm_relu(nc, "l1_in", x, g, C, scale=root_s)
            dense(nc, "l1_w", k, g, C // P, C, whole(A["L1_gnn_W"]), [(0, C, acc, None)])
            store_table(nc, "l1_t", [(table, acc, C)])
            aggregate(nc, "l1_a", k, moved, by_src, table, acc)

            def end_acc(dve, ch):
                ch.done(dve.tensor_tensor(blocks(acc), blocks(acc), spread(root_s[:, :], [P, NB, C]), ALU.mult))
                dve.tensor_tensor(x[:, :], x[:, :], acc[:, :], ALU.add)
            vector_work(nc, "l1_e", end_acc)

        clear_semaphores(nc)

        with ExitStack() as ctx:
            f = Phase(nc, ctx, "l2")
            h = f.sb("h", [P, NB * H1])
            with ExitStack() as inner:
                fi = Phase(nc, inner, "l2r")
                index = fi.sb("index", [P, T], I32)
                index_f = fi.sb("index_f", [P, T])
                with ExitStack() as dense_part:
                    fd = Phase(nc, dense_part, "l2d")
                    g = fd.sb("g", [P, NB * C])
                    norm_relu(nc, "l2_in", x, g, C)
                    xw = fd.sb("xw", [P, NB * NREL * H1])
                    bias = fd.sb("bias", [P, H1])
                    load(nc, "l2_load", [(bias[:, :], on_all(A["L2_gnn_rgcn_bias"]))])
                    wr = A["L2_gnn_rgcn_weight"]
                    dense(nc, "l2_xw", k, g, C // P, NREL * H1,
                          lambda w: [(w[:, c].rearrange("p (r h) -> p r h", r=NREL),
                                      wr[:, c * P:(c + 1) * P, :].rearrange("r p h -> p r h")) for c in range(C // P)],
                          [(0, NREL * H1, xw, None)])
                    dense(nc, "l2_root", k, g, C // P, H1, whole(A["L2_gnn_rgcn_root"]), [(0, H1, h, bias)])

                    def kind_rows(dve, ch):
                        ch.done(dve.tensor_copy(index_f[:, :], by_dst.other[:, :]))
                        dve.scalar_tensor_tensor(index[:, :], index_f[:, :], float(NREL), by_dst.kind[:, :],
                                                 ALU.mult, ALU.add)
                    store_table(nc, "l2_t", [(table_r.rearrange("(n r) h -> n (r h)", r=NREL), xw, NREL * H1)], kind_rows)
                aggregate_kinds(nc, "l2_a", k, moved, by_dst, index, table_r, share, h)
            q = f.sb("q", [P, NB * C])
            skip = f.sb("skip", [P, NB * C])
            with ExitStack() as inner:
                fi = Phase(nc, inner, "l2p")
                kk = fi.sb("kk", [P, NB * C])
                v = fi.sb("v", [P, NB * C])
                biases = [fi.sb(n, [P, C]) for n in ("bq", "bk", "bv", "bskip")]
                load(nc, "l2_load2", [(t[:, :], on_all(A[f"L2_gnn_{n}"])) for t, n in zip(
                    biases, ("bq", "bk", "bv", "bskip"))])
                dense(nc, "l2_qkv", k, h, 1, 4 * C,
                      lambda w: [(w[:, 0, i * C:(i + 1) * C], A[f"L2_gnn_{n}"]) for i, n in enumerate(
                          ("wq", "wk", "wv", "wskip"))],
                      [(i * C, C, t, b) for i, (t, b) in enumerate(zip((q, kk, v, skip), biases))])
                store_table(nc, "l2_t2", [(table, kk, C), (table_v, v, C)])
            scores = f.sb("scores", [P, T * HEADS])
            node_top = f.sb("node_top", [P, NB * HEADS])
            acc = f.sb("acc", [P, NB * (C + HEADS)])
            gamma = f.sb("gamma", [P, C])
            beta = f.sb("beta", [P, C])

            def start_acc(dve, ch):
                dve.memset(node_top[:, :], -BIG)
                dve.memset(acc[:, :], 0.0)
            vector_work(nc, "l2_s", start_acc)
            load(nc, "l2_load3", [(gamma[:, :], on_all(A["L2_gnn_bn_gamma"])), (beta[:, :], on_all(A["L2_gnn_bn_beta"]))])
            edge_scores(nc, "l2_sc", k, moved, by_dst, table, q, scores, node_top)
            mix_values(nc, "l2_mix", k, moved, by_dst, table_v, scores, node_top, acc)

            def end_acc(dve, ch):
                a3 = blocks(acc, C + HEADS)
                den = a3[:, :, C:C + HEADS]
                ch.done(dve.tensor_scalar(den, den, 1e-16, None, ALU.max))
                ch.done(dve.reciprocal(den, den))
                ch.done(dve.tensor_tensor(
                    blocks(q).rearrange("p b (h d) -> p b h d", h=HEADS),
                    a3[:, :, 0:C].rearrange("p b (h d) -> p b h d", h=HEADS),
                    den.unsqueeze(3).to_broadcast([P, NB, HEADS, HD]), ALU.mult))
                dve.tensor_tensor(q[:, :], q[:, :], skip[:, :], ALU.add)
            vector_work(nc, "l2_e", end_acc)
            batch_norm(nc, "l2_bn", k, q, gamma, beta, x)

        clear_semaphores(nc)

        with ExitStack() as ctx:
            f = Phase(nc, ctx, "l3")
            g = f.sb("g", [P, NB * C])
            own = f.sb("own", [P, NB * C])
            neigh = f.sb("neigh", [P, NB * C])
            acc = f.sb("acc", [P, NB * C])
            norm_relu(nc, "l3_in", x, g, C)
            dense(nc, "l3_w", k, g, C // P, 2 * C,
                  lambda w: [(w[:, :, 0:C], A["L3_gnn_W_self"].rearrange("(k p) n -> p k n", p=P)),
                             (w[:, :, C:2 * C], A["L3_gnn_W_neigh"].rearrange("(k p) n -> p k n", p=P))],
                  [(0, C, own, None), (C, C, neigh, None)])
            keep_largest(nc, "l3_k", neigh, g)

            def start_acc(dve, ch):
                dve.memset(acc[:, :], 0.0)
                dve.tensor_tensor(x[:, :], x[:, :], own[:, :], ALU.add)
            store_table(nc, "l3_t", [(table, g, C)], start_acc)
            aggregate(nc, "l3_a", k, moved, by_dst, table, acc)

            def end_acc(dve, ch):
                ch.done(dve.tensor_tensor(blocks(acc), blocks(acc), spread(mean_d[:, :], [P, NB, C]), ALU.mult))
                dve.tensor_tensor(x[:, :], x[:, :], acc[:, :], ALU.add)
            vector_work(nc, "l3_e", end_acc)
        finish()


_INS = ['x', 'src', 'dst', 'edge_type_8', 'L0_gnn_W1', 'L0_gnn_b1', 'L0_gnn_gamma1', 'L0_gnn_beta1', 'L0_gnn_W2',
        'L0_gnn_b2', 'L0_gnn_gamma2', 'L0_gnn_beta2', 'L1_gnn_W', 'L2_gnn_rgcn_weight', 'L2_gnn_rgcn_root',
        'L2_gnn_rgcn_bias', 'L2_gnn_wq', 'L2_gnn_bq', 'L2_gnn_wk', 'L2_gnn_bk', 'L2_gnn_wv', 'L2_gnn_bv',
        'L2_gnn_wskip', 'L2_gnn_bskip', 'L2_gnn_bn_gamma', 'L2_gnn_bn_beta', 'L3_gnn_W_self', 'L3_gnn_W_neigh']


def kernel(**inputs):
    import numpy as _np
    import concourse.bacc as _bacc
    from concourse import mybir as _mybir
    from concourse.bass_utils import run_bass_kernel_spmd as _run

    nc = _bacc.Bacc("TRN2", target_bir_lowering=False, num_devices=1)
    arrays, A = {}, {}
    for name in _INS:
        a = _np.asarray(inputs[name])
        if name == "L1_gnn_W":
            a = a.T
        a = _np.ascontiguousarray(a)
        arrays[f"in_{name}"] = a
        A[name] = nc.dram_tensor(f"in_{name}", a.shape, _mybir.dt.from_np(a.dtype), kind="ExternalInput").ap()
    out = nc.dram_tensor("out", (N, C), F32, kind="ExternalOutput").ap()
    build(nc, A, out)
    r = _run(nc, [arrays], core_ids=[0])
    return r.results[0]["out"]
```

```python
from contextlib import ExitStack

import concourse.bass as bass
from concourse import mybir

P = 128
N = 3125
C = 256
E = 50000
NB = -(-N // P)
TAIL = N - (NB - 1) * P
NPAD = NB * P
EP = 125
EC = E // EP
QUAD = 4
NQ = 4
BODY = NQ * QUAD
HALF = BODY // 2
T = -(-((E + NB * (P - 1)) // P) // BODY) * BODY
TP = -(-((E + NB * NB * (P - 1)) // P) // 512) * 512
HEADS = 4
HD = C // HEADS
NREL = 8
H1 = 128
CW = 512
MAXK = 32
HCH = 20
RCH = 8
DEPTH = 4
ROUND_512 = 1.5 * 2.0 ** 32
assert P * max(T, TP) <= 256 * 512
AW = C + NREL
BIG = 2.0 ** 127
LN_EPS = 1e-5
BN_EPS = 1e-5
SLOPE = 0.01

F32 = mybir.dt.float32
BF16 = mybir.dt.bfloat16
I32 = mybir.dt.int32
U16 = mybir.dt.uint16
ALU = mybir.AluOpType
ACT = mybir.ActivationFunctionType
AX = mybir.AxisListType.X
DVE_ENGINE = mybir.EngineType.DVE
PE_ENGINE = mybir.EngineType.PE


class Chain:

    def __init__(self, eng, sem):
        self.eng, self.sem, self.n = eng, sem, 0

    def done(self, ins):
        self.n += 1
        ins.then_inc(self.sem, 1)
        self.eng.wait_ge(self.sem, self.n)


def hold(eng, sem, value, passed):
    eng.wait_ge(sem, value)
    eng.sem_inc(passed, 1)


def spread(ap, shape):
    return ap.unsqueeze(2).to_broadcast(shape)


def repeat(ap, shape):
    return ap.unsqueeze(1).to_broadcast(shape)


def block_numbers(nc, engine, table, first, n):
    _, regs = nc.values_load_multi_w_load_instructions(
        table[0:1, bass.ds(first, n)], engines=(engine,), min_val=0, max_val=NB - 1,
        skip_runtime_bounds_check_because="counts of blocks that start at or before a tile, less one")
    return regs


def onehots_of(dve, k, out, key, at, width):
    parts, groups = out.shape[0], out.shape[1]
    full = [parts, groups, width, QUAD]
    return dve.tensor_tensor(
        out, k.iota_q[0:parts, 0:width, :].unsqueeze(1).to_broadcast(full),
        key[:, bass.ds(at, groups * QUAD)].rearrange("p (g j) -> p g j", j=QUAD).unsqueeze(2).to_broadcast(full),
        ALU.is_equal)


class IndirectCount:

    def __init__(self, nc, ctx):
        self.sems = [ctx.enter_context(nc.semaphore(f"indirect{i}")) for i in range(NQ)]
        self.before = 0

    def after(self, bodies):
        return bodies * (16 * QUAD) + self.before

    def end(self, bodies):
        self.before += 16 * QUAD * bodies


class Order:

    def __init__(self, sb, dram):
        self.block = sb("dst_block", [1, T], I32)
        self.other = sb("dst_other", [P, T], I32)
        self.low = sb("dst_low", [P, T], F32)
        self.kind = sb("dst_kind", [P, T], F32)
        self.key = sb("dst_key", [P, T], F32)
        self.records = dram("dst_records", [P * T, 4], F32)


def rank_edges(nc, block, ctx, n, low_b, high_b, low_width, tiles_n, k, slot_i, tile_group, count, by_node, extra):

    def sb(name, shape, dt):
        return ctx.enter_context(nc.sbuf_tensor(f"{n}_{name}", shape, dt))

    def ps(name, shape, dt):
        return ctx.enter_context(nc.psum_tensor(f"{n}_{name}", shape, dt))

    def sem(name):
        return ctx.enter_context(nc.semaphore(f"{n}_{name}"))

    W = low_width
    is_low = sb("is_low", [EP, 2, HCH // QUAD, W, QUAD], BF16)
    is_high = sb("is_high", [EP, 2, HCH // QUAD, NB, QUAD], BF16)
    step_low, step_high = (
        t.rearrange("p s g w j -> p (s g) w j")[:, 0:DEPTH * RCH // QUAD].rearrange("p (s g) w j -> p s g w j", s=DEPTH)
        for t in (is_low[:, :, :, :, :], is_high[:, :, :, :, :]))
    seen = sb("seen", [W, NB, EC + 1], F32)
    going = sb("going", [W, NB, EC + 1], BF16)
    low_t = sb("low_t", [W, DEPTH, RCH, EP], BF16)
    before = sb("before", [W, DEPTH, RCH, 2, NB], BF16)
    same = sb("same", [EP, 2, RCH, EP], BF16)
    picked = sb("picked", [EP, 2, RCH, 2, NB], F32)
    slot = sb("slot", [EP, EC], F32)
    part_i = sb("part_i", [EP, EC], I32)
    tile_i = sb("tile_i", [EP, EC], I32)
    part_f = sb("part_f", [EP, EC], F32)
    small_i = sb("small_i", [W, NB], I32)
    tiles = sb("tiles", [W, NB], F32)
    ends = sb("ends", [W, NB], F32)
    starts = sb("starts", [W, NB + 1], F32)
    groups_w = 1 if by_node else W
    starts_n = NB if by_node else NB + 1
    started = sb("started", [groups_w, starts_n, tiles_n], BF16)
    group_f = sb("group_f", [groups_w, tiles_n], F32)
    lefts = [sb(f"is_left{i}", [EP, 2, HCH // QUAD, P, QUAD], BF16) if e[0] is not low_b else is_low
             for i, e in enumerate(extra)]
    rights = [sb(f"is_right{i}", [EP, 2, HCH // QUAD, e[2], QUAD], BF16) for i, e in enumerate(extra)]
    nothing = sb("nothing", [P, 256], BF16)

    hist_ps = [ps(f"hist{s}", [P, 512], F32) for s in range(2)]
    turn_ps = [ps(f"turn{s}", [P, RCH, P], BF16) for s in range(2)]
    pair_ps = ps("pair", [EP, 2, 2, 512], F32)
    total_ps = hist_ps
    slot_ps = hist_ps
    extra_bank = [turn_ps[i][:, :, :].rearrange("p a b -> p (a b)").bitcast(F32) for i in range(len(extra))]

    (onehots, hist_done, hist_copied, passed_act, chain, totals_ready, totals_done, tiles_ready, prefix_ready,
     ranked_onehots, turned, turned_copied, paired, masked, looked_up, picked_done, ranks_done, nothing_ready,
     extra_taken, groups_ready, groups_done) = (sem(x) for x in (
         "onehots", "hist_done", "hist_copied", "passed_act", "chain", "totals_ready", "totals_done", "tiles_ready",
         "prefix_ready", "ranked_onehots", "turned", "turned_copied", "paired", "masked", "looked_up",
         "picked_done", "ranks_done", "nothing_ready", "extra_taken", "groups_ready", "groups_done"))

    def column(onehot, buffer, j):
        return onehot[:, buffer, j // QUAD, :, j % QUAD]

    def slots_by_high(b):
        return slot_ps[b % 2][0:EP, 0:RCH * 2 * NB].rearrange("p (j a h) -> p j a h", a=2, h=NB)

    steps = EC // RCH
    prologue, bodies = 1, (steps - 3) // DEPTH

    def each_step(eng, run):
        for r in range(prologue):
            run(r, r % DEPTH)
        with eng.Fori(0, bodies, 1) as it:
            for u in range(DEPTH):
                run(it * DEPTH + (prologue + u), (prologue + u) % DEPTH)
        for r in range(prologue + bodies * DEPTH, steps):
            run(r, r % DEPTH)

    def is_last(step, n):
        return isinstance(step, int) and step >= steps - n

    @block.vector
    def _(dve):
        ch = Chain(dve, chain)
        dve.sem_inc(hist_done, 2)
        dve.memset(nothing[:, :], 0.0).then_inc(nothing_ready, 1)
        with dve.Fori(0, EC // (2 * HCH), 1) as it:
            for s in range(2):
                at = it * (2 * HCH) + s * HCH
                dve.wait_ge(hist_done, it * 2 + s + 1)
                onehots_of(dve, k, is_low[:, s], low_b, at, W)
                for (left, right, width, _), l, r in zip(extra, lefts, rights):
                    if l is not is_low:
                        onehots_of(dve, k, l[:, s], left, at, P)
                    onehots_of(dve, k, r[:, s], right, at, width)
                onehots_of(dve, k, is_high[:, s], high_b, at, NB).then_inc(onehots, 1)
        dve.wait_ge(hist_copied, EC // HCH + 2)
        for (_, _, width, out), bank in zip(extra, extra_bank):
            last = dve.tensor_copy(out[:, :], bank[:, 0:width])
        if extra:
            last.then_inc(extra_taken, 1)
        if by_node:
            dve.tensor_reduce(count[:, :], seen[:, :, 1:EC + 1], AX, ALU.add).then_inc(totals_ready, 1)
            dve.wait_ge(totals_done, 1)
            ch.done(dve.tensor_scalar(small_i[:, :], total_ps[1][0:W, 0:NB], float(P - 1), None, ALU.add))
        else:
            ch.done(dve.tensor_reduce(tiles[:, :], seen[:, :, 1:EC + 1], AX, ALU.add))
            ch.done(dve.tensor_scalar(small_i[:, :], tiles[:, :], float(P - 1), None, ALU.add))
        ch.done(dve.tensor_scalar(small_i[:, :], small_i[:, :], 7, None, ALU.logical_shift_right))
        if by_node:
            ch.done(dve.tensor_copy(tiles[:, :], small_i[:, :]))
            ch.done(dve.tensor_tensor_scan(ends[:, :], k.ones[0:W, 0:NB], tiles[:, :], 0.0, ALU.mult, ALU.add))
            ch.done(dve.tensor_tensor(starts[:, 0:NB], ends[:, :], tiles[:, :], ALU.subtract))
            ch.done(dve.scalar_tensor_tensor(seen[:, :, 0], starts[:, 0:NB], float(P), total_ps[0][0:W, 0:NB],
                                             ALU.mult, ALU.add))
        else:
            dve.tensor_copy(tiles[:, :], small_i[:, :]).then_inc(totals_ready, 1)
            dve.wait_ge(totals_done, 1)
            ch.done(dve.tensor_copy(tiles[:, :], total_ps[1][0:W, 0:NB]))
            ch.done(dve.tensor_tensor_scan(ends[:, :], k.ones[0:W, 0:NB], tiles[:, :], 0.0, ALU.mult, ALU.add))
            dve.tensor_copy(starts[:, NB:NB + 1], ends[:, NB - 1:NB])
            ch.done(dve.tensor_tensor(starts[:, 0:NB], ends[:, :], tiles[:, :], ALU.subtract))
            ch.done(dve.tensor_tensor(starts[:, 0:NB], starts[:, 0:NB], total_ps[0][0:W, 0:NB], ALU.add))
            ch.done(dve.tensor_scalar(seen[:, :, 0], starts[:, 0:NB], float(P), None, ALU.mult))
        flat = seen[:, :, :].rearrange("p h t -> p (h t)")
        coarse = going[:, :, :].rearrange("p h t -> p (h t)")
        ch.done(dve.tensor_tensor_scan(flat, coarse, flat, 0.0, ALU.mult, ALU.add))
        ch.done(dve.tensor_scalar(coarse, flat, ROUND_512, ROUND_512, ALU.add, ALU.subtract))
        dve.tensor_tensor(flat, flat, coarse, ALU.subtract).then_inc(prefix_ready, 1)

        def compare(step, b):
            onehots_of(dve, k, step_low[:, b], low_b, step * RCH, W)
            onehots_of(dve, k, step_high[:, b], high_b, step * RCH, NB).then_inc(ranked_onehots, 1)

        def mask(step, b):
            dve.wait_ge(paired, step + 1)
            for q in range(2):
                last = dve.tensor_tensor(
                    same[:, b % 2, 4 * q:4 * q + 4],
                    pair_ps[:, b % 2, q, 0:4 * EP].rearrange("p (j e) -> p j e", j=4),
                    repeat(k.earlier[0:EP, 0:EP], [EP, 4, EP]), ALU.mult)
            last.then_inc(masked, 1)

        def pick(step, b):
            dve.wait_ge(looked_up, step + 1)
            for g in range(RCH // QUAD):
                last = dve.tensor_tensor(
                    picked[:, b % 2, g * QUAD:(g + 1) * QUAD],
                    slots_by_high(b)[:, g * QUAD:(g + 1) * QUAD],
                    step_high[:, b, g].rearrange("p h j -> p j h").unsqueeze(2).to_broadcast([EP, QUAD, 2, NB]), ALU.mult)
            last.then_inc(picked_done, 1)

        def total(step, b):
            dve.wait_ge(picked_done, step + 1)
            dve.tensor_reduce(slot[:, bass.ds(step * RCH, RCH)], picked[:, b % 2].rearrange("p j a h -> p j (a h)"),
                              AX, ALU.add).then_inc(ranks_done, 1)

        def run(step, b):
            if not is_last(step, 2):
                compare(step + 2, (b + 2) % DEPTH)
            if not (isinstance(step, int) and step == 0):
                pick(step - 1, (b - 1) % DEPTH)
            mask(step, b)
            if not (isinstance(step, int) and step == 0):
                total(step - 1, (b - 1) % DEPTH)

        compare(0, 0)
        compare(1, 1)
        each_step(dve, run)
        pick(steps - 1, (steps - 1) % DEPTH)
        total(steps - 1, (steps - 1) % DEPTH)
        dve.wait_ge(ranks_done, EC // RCH)
        ch.done(dve.tensor_copy(slot_i[:, :], slot[:, :]))
        dve.tensor_scalar(part_i[:, :], slot_i[:, :], P - 1, None, ALU.bitwise_and)
        ch.done(dve.tensor_scalar(tile_i[:, :], slot_i[:, :], 7, None, ALU.logical_shift_right))
        dve.tensor_copy(part_f[:, :], part_i[:, :])
        ch.done(dve.tensor_copy(slot[:, :], tile_i[:, :]))
        dve.scalar_tensor_tensor(slot_i[:, :], part_f[:, :], float(tiles_n), slot[:, :], ALU.mult, ALU.add)
        for h in range(starts_n):
            last = dve.tensor_scalar(started[:, h], k.iota_t[0:groups_w, 0:tiles_n], starts[0:groups_w, h:h + 1], None,
                                     ALU.is_ge)
        if by_node:
            ch.done(last)
            dve.tensor_reduce(group_f[:, :], started[:, :, :].rearrange("p h t -> p t h"), AX, ALU.add)\
               .then_inc(groups_ready, 1)
            dve.wait_ge(groups_ready, 1)
        else:
            last.then_inc(groups_ready, 1)
        if by_node:
            dve.tensor_scalar(tile_group[:, :], group_f[:, :], -1.0, None, ALU.add)
        else:
            dve.wait_ge(groups_done, 1)
            for c in range(0, tiles_n, 512):
                dve.tensor_scalar(tile_group[:, c:c + 512], pair_ps[0:1, 0, c // 512, :], -1.0, float(NB * NB),
                                  ALU.add, ALU.min)

    @block.tensor
    def _(pe):
        pe.wait_ge(nothing_ready, 1)
        for bank in extra_bank:
            pe.matmul(bank[:, 0:256], nothing[:, 0:P], nothing[:, :], start=True, stop=False, skip_group_check=True)
        with pe.Fori(0, EC // (2 * HCH), 1) as it:
            for s in range(2):
                pe.wait_ge(onehots, it * 2 + s + 1)
                pe.wait_ge(hist_copied, it * 2 + s + 1)
                for j in range(HCH):
                    for (_, _, width, _), l, r, bank in zip(extra, lefts, rights, extra_bank):
                        pe.matmul(bank[:, 0:width], column(l, s, j), column(r, s, j), start=False, stop=False,
                                  skip_group_check=True)
                    last = pe.matmul(hist_ps[s][0:W, j * NB:(j + 1) * NB], column(is_low, s, j),
                                     column(is_high, s, j), start=True, stop=True)
                last.then_inc(hist_done, 1)
        pe.wait_ge(totals_ready, 1)
        of = count if by_node else tiles
        pe.matmul(total_ps[0][0:W, 0:NB], k.earlier[0:W, 0:W], of[:, :], start=True, stop=True)
        pe.matmul(total_ps[1][0:W, 0:NB], k.ones[0:W, 0:W], of[:, :], start=True, stop=True)\
          .then_inc(totals_done, 1)
        pe.wait_ge(prefix_ready, 1)
        if extra:
            pe.wait_ge(extra_taken, 1)

        def turn(step, b):
            pe.wait_ge(ranked_onehots, step + 1)
            for j in range(RCH):
                last = pe.transpose(turn_ps[b % 2][0:W, j, 0:EP], column(step_low, b, j), k.ident_b[0:EP, 0:EP])
            last.then_inc(turned, 1)

        def pair(step, b):
            pe.wait_ge(turned_copied, step + 1)
            for j in range(RCH):
                last = pe.matmul(pair_ps[:, b % 2, j // 4, j % 4 * EP:(j % 4 + 1) * EP], low_t[:, b, j],
                                 low_t[:, b, j], start=True, stop=True)
            last.then_inc(paired, 1)

        def look_up(step, b):
            pe.wait_ge(masked, step + 1)
            for j in range(RCH):
                pe.matmul(slots_by_high(b)[:, j], low_t[:, b, j], before[:, b, j], start=True, stop=False)
                last = pe.matmul(slots_by_high(b)[:, j, 0], same[:, b % 2, j], column(step_high, b, j),
                                 start=False, stop=True)
            last.then_inc(looked_up, 1)

        def run(step, b):
            if not (isinstance(step, int) and step == 0):
                look_up(step - 1, (b - 1) % DEPTH)
            pair(step, b)
            if not is_last(step, 2):
                turn(step + 2, (b + 2) % DEPTH)

        turn(0, 0)
        turn(1, 1)
        each_step(pe, run)
        look_up(steps - 1, (steps - 1) % DEPTH)
        if not by_node:
            pe.wait_ge(groups_ready, 1)
            for c in range(0, tiles_n, 512):
                for h in range(starts_n):
                    last = pe.matmul(pair_ps[0:1, 0, c // 512, :], k.one_b[0:W, :], started[:, h, c:c + 512],
                                     start=(h == 0), stop=(h == starts_n - 1))
            last.then_inc(groups_done, 1)

    @block.scalar
    def _(act):
        act.sem_inc(hist_copied, 2)
        act.activation(going[:, :, :].rearrange("p h t -> p (h t)"),
                       k.iota_t[0:W, 0:1].to_broadcast([W, NB * (EC + 1)]), ACT.Copy, bias=1.0, scale=0.0)\
           .then_inc(passed_act, 1)
        act.wait_ge(passed_act, 1)
        act.activation(going[:, :, 0], k.iota_t[0:W, 0:NB], ACT.Copy, scale=0.0)
        with act.Fori(0, EC // (2 * HCH), 1) as it:
            for s in range(2):
                hold(act, hist_done, it * 2 + s + 3, passed_act)
                act.copy(seen[:, :, bass.ds(it * (2 * HCH) + s * HCH + 1, HCH)],
                         hist_ps[s][0:W, 0:HCH * NB].rearrange("p (t h) -> p h t", t=HCH)).then_inc(hist_copied, 1)

        def copy(step, b):
            if isinstance(step, int):
                act.wait_ge(turned, step + 1)
            else:
                hold(act, turned, step + 1, passed_act)
            for part, t in enumerate((seen, going)):
                act.copy(before[:, b, :, part], t[:, :, bass.ds(step * RCH, RCH)].rearrange("p h t -> p t h"))
            act.copy(low_t[:, b], turn_ps[b % 2][0:W, :, 0:EP]).then_inc(turned_copied, 1)

        act.wait_ge(prefix_ready, 1)
        each_step(act, copy)


def scatter_records(nc, block, ctx, n, records, slot_i, record, moved):
    slots = ctx.enter_context(nc.sbuf_tensor(f"{n}_slots", [EP, NQ, QUAD], I32))
    rows = ctx.enter_context(nc.sbuf_tensor(f"{n}_rows", [EP, NQ, QUAD, record.shape[2]], record.dtype))
    staged = ctx.enter_context(nc.semaphore(f"{n}_staged"))
    written = moved.sems
    passed = ctx.enter_context(nc.semaphore(f"{n}_passed_pool"))
    bodies = EC // BODY

    @block.gpsimd
    def _(pool):
        def stage(it, i, first):
            at = it * BODY + i * QUAD
            if not first:
                hold(pool, written[i], moved.after(it), passed)
            pool.tensor_copy(slots[:, i], slot_i[:, bass.ds(at, QUAD)])
            pool.tensor_copy(rows[:, i], record[:, bass.ds(at, QUAD), :]).then_inc(staged, 1)

        def body(it, first):
            stage(it, 0, first)
            for i in range(NQ):
                if i + 1 < NQ:
                    stage(it, i + 1, first)
                hold(pool, staged, it * NQ + i + 1, passed)
                for j in range(QUAD):
                    pool.indirect_dma_start(records, bass.IndirectOffsetOnAxis(ap=slots[:, i, j:j + 1], axis=0),
                                            rows[:, i, j], None).then_inc(written[i], 16)

        body(0, True)
        with pool.Fori(1, bodies, 1) as it:
            body(it, False)
        for i in range(NQ):
            pool.wait_ge(written[i], moved.after(bodies))

    moved.end(bodies)


def fetch_records(nc, block, ctx, o):
    got = ctx.enter_context(nc.sbuf_tensor("dst_got", [P, T, 4], F32))
    fetched = ctx.enter_context(nc.semaphore("dst_fetched"))

    @block.sync
    def _(sp):
        sp.dma_start(got[:, :, :], o.records.rearrange("(p t) c -> p t c", p=P)).then_inc(fetched, 16)

    @block.vector
    def _(dve):
        dve.wait_ge(fetched, 16)
        dve.tensor_copy(o.other[:, :], got[:, :, 0])
        dve.tensor_copy(o.low[:, :], got[:, :, 1])
        dve.tensor_copy(o.kind[:, :], got[:, :, 2])
        dve.tensor_copy(o.key[:, :], got[:, :, 3])


class Phase:

    def __init__(self, nc, ctx, name):
        self.nc, self.ctx, self.name = nc, ctx, name

    def sb(self, name, shape, dt=F32):
        return self.ctx.enter_context(self.nc.sbuf_tensor(f"{self.name}_{name}", shape, dt))

    def ps(self, name, shape, dt=F32):
        return self.ctx.enter_context(self.nc.psum_tensor(f"{self.name}_{name}", shape, dt))

    def sem(self, name):
        return self.ctx.enter_context(self.nc.semaphore(f"{self.name}_{name}"))


class Consts:
    pass


def make_consts(nc, ctx, sb):
    k = Consts()
    k.iota_t = sb("iota_t", [P, TP], F32)
    k.iota_q = sb("iota_q", [P, 2 * P, QUAD], BF16)
    k.ident = sb("ident", [P, P], F32)
    k.ident_b = sb("ident_b", [P, P], BF16)
    k.ones = sb("ones", [P, P], F32)
    k.one_b = sb("one_b", [P, 1], BF16)
    k.earlier = sb("earlier", [P, P], F32)
    return k


class Keys:

    def __init__(self, nc, ctx):
        def sb(name, shape, dt):
            return ctx.enter_context(nc.sbuf_tensor(name, shape, dt))
        self.src_low, self.src_high, self.dst_low, self.dst_high, self.dst_kind = (
            sb(n, [EP, EC], BF16) for n in ("key_src_low", "key_src_high", "key_dst_low", "key_dst_high", "key_dst_kind"))
        self.record = sb("record", [EP, EC, 4], F32)
        self.pair = sb("pair_record", [EP, EC, 2], BF16)
        self.slot_d = sb("slot_d", [EP, EC], I32)
        self.slot_p = sb("slot_p", [EP, EC], I32)


def setup(nc, ctx, k, e, A, records, pair_records):
    f = Phase(nc, ctx, "setup")
    iota_i = f.sb("iota_i", [P, TP], I32)
    filler = f.sb("filler", [P, T, 4])
    pair_filler = f.sb("pair_filler", [P, TP, 2], BF16)
    src_i, dst_i, kind_i, low_i, high_i = (f.sb(n, [EP, EC], I32) for n in ("src", "dst", "kind", "low", "high"))
    kind_f = f.sb("kind_f", [EP, EC])
    (loaded, pool_step, iota_ready, cleared, filler_ready, filled, step) = (f.sem(n) for n in (
        "loaded", "pool_step", "iota_ready", "cleared", "filler_ready", "filled", "step"))
    with nc.Block() as block:
        @block.sync
        def _(sp):
            for t, name in ((src_i, "src"), (dst_i, "dst"), (kind_i, "edge_type_8")):
                sp.dma_start(t[:, :], A[name].rearrange("(p t) -> p t", p=EP)).then_inc(loaded, 16)

        @block.scalar
        def _(act):
            act.wait_ge(filler_ready, 2)
            act.dma_start(records.rearrange("(p t) c -> p t c", p=P), filler[:, :, :]).then_inc(filled, 16)
            act.dma_start(pair_records.rearrange("(p t) c -> p t c", p=P), pair_filler[:, :, :]).then_inc(filled, 16)
            act.wait_ge(filled, 32)

        @block.gpsimd
        def _(pool):
            pool.iota(iota_i[:, :], [[1, TP]], base=0, channel_multiplier=0).then_inc(iota_ready, 1)
            pool.memset(k.ones[:, :], 1.0)
            pool.memset(k.one_b[:, :], 1.0)
            pool.memset(k.earlier[:, :], 1.0).then_inc(pool_step, 1)
            pool.memset(k.ident[:, :], 0.0).then_inc(pool_step, 1)
            pool.wait_ge(pool_step, 2)
            pool.affine_select(out=k.earlier[:, :], in_=k.earlier[:, :], compare_op=ALU.is_gt, fill=0.0,
                               base=0, pattern=[[1, P]], channel_multiplier=-1)
            pool.affine_select(out=k.ident[:, :], in_=k.ident[:, :], compare_op=ALU.not_equal, fill=1.0,
                               base=0, pattern=[[1, P]], channel_multiplier=-1).then_inc(pool_step, 1)

        @block.vector
        def _(dve):
            ch = Chain(dve, step)
            dve.memset(filler[:, :, :], 0.0).then_inc(cleared, 1)
            dve.memset(pair_filler[:, :, :], -1.0).then_inc(filler_ready, 1)
            dve.wait_ge(cleared, 1)
            dve.memset(filler[:, :, 1:2], -1.0).then_inc(filler_ready, 1)
            dve.wait_ge(iota_ready, 1)
            dve.tensor_copy(k.iota_t[:, :], iota_i[:, :])
            dve.tensor_copy(k.iota_q[:, :, :], spread(iota_i[:, 0:2 * P], [P, 2 * P, QUAD]))
            dve.wait_ge(pool_step, 3)
            dve.tensor_copy(k.ident_b[:, :], k.ident[:, :])
            dve.wait_ge(loaded, 48)
            for key, low, high, place in ((src_i, e.src_low, e.src_high, 0), (dst_i, e.dst_low, e.dst_high, 1)):
                dve.tensor_scalar(low_i[:, :], key[:, :], P - 1, None, ALU.bitwise_and)
                ch.done(dve.tensor_scalar(high_i[:, :], key[:, :], 7, None, ALU.logical_shift_right))
                dve.tensor_copy(low[:, :], low_i[:, :])
                dve.tensor_copy(e.pair[:, :, place], low_i[:, :])
                ch.done(dve.tensor_copy(high[:, :], high_i[:, :]))
            dve.tensor_copy(e.record[:, :, 0], src_i[:, :])
            dve.tensor_copy(e.record[:, :, 1], low_i[:, :])
            dve.tensor_copy(e.record[:, :, 2], kind_i[:, :])
            dve.tensor_scalar(e.record[:, :, 3], dst_i[:, :], 1.0, None, ALU.add)
            ch.done(dve.tensor_copy(kind_f[:, :], kind_i[:, :]))
            dve.scalar_tensor_tensor(e.dst_kind[:, :], high_i[:, :], float(NREL), kind_f[:, :], ALU.mult, ALU.add)


def blocks(t, width=C):
    return t[:, 0:NB * width].rearrange("p (b c) -> p b c", b=NB)


def inverse_root(dve, ch, y, a, t):
    ch.done(dve.reciprocal(y, y))
    ch.done(dve.tensor_tensor(t, y, y, ALU.mult))
    ch.done(dve.tensor_tensor(t, t, a, ALU.mult))
    ch.done(dve.tensor_scalar(t, t, -0.5, 1.5, ALU.mult, ALU.add))
    ch.done(dve.tensor_tensor(y, y, t, ALU.mult))


def degrees(nc, count_d, count_s, root_d, root_s, mean_d):
    with ExitStack() as ctx, nc.Block() as block:
        f = Phase(nc, ctx, "deg")
        a = f.sb("a", [P, 2, NB])
        y = f.sb("y", [P, 2, NB])
        t = f.sb("t", [P, 2, NB])
        step, added, rooted = f.sem("step"), f.sem("added"), f.sem("rooted")

        @block.vector
        def _(dve):
            ch = Chain(dve, step)
            dve.tensor_scalar(a[:, 0], count_d[:, :], 1.0, None, ALU.add)
            dve.tensor_scalar(a[:, 1], count_s[:, :], 1.0, None, ALU.add).then_inc(added, 1)
            ch.done(dve.tensor_scalar(mean_d[:, :], count_d[:, :], 1.0, None, ALU.max))
            ch.done(dve.reciprocal(mean_d[:, :], mean_d[:, :]))
            dve.wait_ge(rooted, 1)
            inverse_root(dve, ch, y[:, :, :], a[:, :, :], t[:, :, :])
            dve.tensor_copy(root_d[:, :], y[:, 0])
            dve.tensor_copy(root_s[:, :], y[:, 1])

        @block.scalar
        def _(act):
            act.wait_ge(added, 1)
            act.activation(y[:, :, :], a[:, :, :], ACT.Sqrt).then_inc(rooted, 1)


def norm_relu(nc, name, src, dst, width, scale=None, gamma=None, beta=None, add_to=None):
    with ExitStack() as ctx, nc.Block() as block:
        f = Phase(nc, ctx, name)
        sq = f.sb("sq", [P, NB * width])
        mean = f.sb("mean", [P, NB])
        a = f.sb("a", [P, NB])
        y = f.sb("y", [P, NB])
        t = f.sb("t", [P, NB])
        step, centred, squared, var_ready, rooted = (f.sem(n) for n in (
            "step", "centred", "squared", "var_ready", "rooted"))
        s3, d3, q3 = blocks(src, width), blocks(dst, width), blocks(sq, width)
        full = [P, NB, width]

        @block.vector
        def _(dve):
            ch = Chain(dve, step)
            ch.done(dve.tensor_reduce(mean[:, :], s3, AX, ALU.add))
            ch.done(dve.tensor_scalar(mean[:, :], mean[:, :], 1.0 / width, None, ALU.mult))
            dve.tensor_tensor(d3, s3, spread(mean[:, :], full), ALU.subtract).then_inc(centred, 1)
            dve.wait_ge(squared, 1)
            ch.done(dve.tensor_reduce(a[:, :], q3, AX, ALU.add))
            dve.tensor_scalar(a[:, :], a[:, :], 1.0 / width, LN_EPS, ALU.mult, ALU.add).then_inc(var_ready, 1)
            dve.wait_ge(rooted, 1)
            inverse_root(dve, ch, y[:, :], a[:, :], t[:, :])
            if gamma is None:
                if scale is not None:
                    ch.done(dve.tensor_tensor(y[:, :], y[:, :], scale[:, :], ALU.mult))
                ch.done(dve.scalar_tensor_tensor(d3, d3, 0.0, spread(y[:, :], full), ALU.max, ALU.mult))
                return
            ch.done(dve.tensor_tensor(d3, d3, spread(y[:, :], full), ALU.mult))
            ch.done(dve.tensor_tensor(d3, d3, repeat(gamma[:, :], full), ALU.mult))
            ch.done(dve.tensor_tensor(d3, d3, repeat(beta[:, :], full), ALU.add))
            if add_to is not None:
                ch.done(dve.scalar_tensor_tensor(blocks(add_to, width), d3, 0.0, blocks(add_to, width),
                                                 ALU.max, ALU.add))
            else:
                ch.done(dve.scalar_tensor_tensor(d3, d3, 0.0, spread(scale[:, :], full), ALU.max, ALU.mult))

        @block.scalar
        def _(act):
            act.wait_ge(centred, 1)
            act.activation(sq[:, :], dst[:, 0:NB * width], ACT.Square).then_inc(squared, 1)
            act.wait_ge(var_ready, 1)
            act.activation(y[:, :], a[:, :], ACT.Sqrt).then_inc(rooted, 1)


DB = 5


def dense(nc, name, k, src, kc, nout, weight_loads, outs):
    with ExitStack() as ctx, nc.Block() as block:
        f = Phase(nc, ctx, name)
        w = f.sb("w", [P, kc, nout])
        staged_rows = f.sb("staged_rows", [P, DB, kc * P])
        rows_t = f.sb("rows_t", [P, DB, kc, P])
        turn = [f.ps(f"turn{s}", [P, kc, P]) for s in range(2)]
        prod = [f.ps(f"prod{s}", [P, nout]) for s in range(2)]
        loaded, staged, turned, turned_copied, product, copied, passed_act, passed_dve = (f.sem(n) for n in (
            "loaded", "staged", "turned", "turned_copied", "product", "copied", "passed_act", "passed_dve"))
        loads = weight_loads(w)

        @block.sync
        def _(sp):
            for dst, s in loads:
                sp.dma_start(dst, s).then_inc(loaded, 16)

        @block.scalar
        def _(act):
            with act.Fori(0, NB // DB, 1) as it:
                act.copy(staged_rows[:, :, :].rearrange("p j c -> p (j c)"),
                         src[:, bass.ds(it * (DB * kc * P), DB * kc * P)]).then_inc(staged, 1)
                for j in range(DB):
                    act.wait_ge(turned, it * DB + j + 1)
                    act.copy(rows_t[:, j], turn[j % 2][:, :, :]).then_inc(turned_copied, 1)

        @block.tensor
        def _(pe):
            pe.wait_ge(loaded, 16 * len(loads))

            def product_of(it, j):
                pe.wait_ge(turned_copied, it * DB + j + 1)
                pe.wait_ge(copied, it * DB + j + (2 if j == 0 else 1))
                for c0 in range(0, nout, 512):
                    c1 = min(c0 + 512, nout)
                    for c in range(kc):
                        last = pe.matmul(prod[j % 2][:, c0:c1], rows_t[:, j, c], w[:, c, c0:c1],
                                         start=(c == 0), stop=(c == kc - 1))
                last.then_inc(product, 1)

            with pe.Fori(0, NB // DB, 1) as it:
                pe.wait_ge(staged, it + 1)
                for j in range(DB):
                    for c in range(kc):
                        last = pe.transpose(turn[j % 2][:, c], staged_rows[:, j, c * P:(c + 1) * P], k.ident[:, :])
                    last.then_inc(turned, 1)
                    if j > 0:
                        product_of(it, j - 1)
                product_of(it, DB - 1)

        @block.vector
        def _(dve):
            dve.sem_inc(copied, 2)
            with dve.Fori(0, NB // DB, 1) as it:
                for j in range(DB):
                    hold(dve, product, it * DB + j + 1, passed_dve)
                    for c0, width, dst, bias in outs:
                        for a in range(c0, c0 + width, 512):
                            n = min(512, c0 + width - a)
                            to = dst[:, bass.ds((it * DB + j) * width + (a - c0), n)]
                            if bias is None:
                                last = dve.tensor_copy(to, prod[j % 2][:, a:a + n])
                            else:
                                last = dve.tensor_tensor(to, prod[j % 2][:, a:a + n], bias[:, a - c0:a - c0 + n], ALU.add)
                    last.then_inc(copied, 1)


def whole(weight):
    return lambda w: [(w[:, :, :], weight.rearrange("(k p) n -> p k n", p=P))]


def gather_rows(f, block, index, table, rows, width, landed, used):
    slots = f.sb("slots", [P, NQ, QUAD], I32)
    staged = f.sem("staged")
    passed = f.sem("passed_pool")

    @block.gpsimd
    def _(pool):
        with pool.Fori(0, T // BODY, 1) as it:
            def stage(i):
                hold(pool, used, it * BODY + (i + 1) * QUAD, passed)
                pool.tensor_copy(slots[:, i], index[:, bass.ds(it * BODY + i * QUAD, QUAD)]).then_inc(staged, 1)

            stage(0)
            for i in range(NQ):
                hold(pool, staged, it * NQ + i + 1, passed)
                for j in range(QUAD):
                    if j == 2 and i + 1 < NQ:
                        stage(i + 1)
                    pool.indirect_dma_start(rows[:, i * QUAD + j, 0:width], None, table,
                                            bass.IndirectOffsetOnAxis(ap=slots[:, i, j:j + 1], axis=0))\
                        .then_inc(landed[i], 16)


def select_matrix(dve, k, o, sel, it, s):
    return dve.tensor_tensor(sel[:, s * HALF:(s + 1) * HALF], repeat(k.iota_t[:, 0:P], [P, HALF, P]),
                             spread(o.low[:, bass.ds(it * BODY + s * HALF, HALF)], [P, HALF, P]), ALU.is_equal)


def select_kind(dve, k, o, out, it, s):
    return dve.tensor_tensor(out, repeat(k.iota_t[:, 0:NREL], [P, HALF, NREL]),
                             spread(o.kind[:, bass.ds(it * BODY + s * HALF, HALF)], [P, HALF, NREL]), ALU.is_equal)


def add_tiles(nc, dve, o, accs, width, bank, it, first, n, done, done_start, added, lead):
    regs = block_numbers(nc, DVE_ENGINE, o.block, it * BODY + first, n)
    for i in range(n):
        tile = it * BODY + first + i
        dve.wait_ge(done, tile + done_start + 1)
        dve.wait_ge(added, tile + lead - 1)
        to = accs[i % 2][:, bass.ds(regs[i] * width, width)]
        dve.tensor_tensor(to, bank(first + i)[:, 0:width], to, ALU.add).then_inc(added, 1)


STREAM = TP // 2
assert STREAM > -(-E // P)


def build_adjacency(nc, block, ctx, k, places, tile_pair, adj):
    f = Phase(nc, ctx, "adj")
    onehot = f.sb("onehot", [P, 2, 2, 2, P, QUAD], BF16)
    bank = [[f.ps(f"count{s}{u}", [P, QUAD, P]) for u in range(2)] for s in range(2)]
    onehots, counted, added, cleared = f.sem("onehots"), f.sem("counted"), f.sem("added"), f.sem("cleared")

    @block.vector
    def _(dve):
        words = adj[:, :].bitcast(F32)
        dve.memset(words, 0.0).then_inc(cleared, 1)
        dve.sem_inc(added, 4 * QUAD)
        dve.wait_ge(cleared, 1)

        def compare(it, s):
            for u in range(2):
                for place in range(2):
                    last = onehots_of(dve, k, onehot[:, s, u, place:place + 1], places[:, place],
                                      it * (2 * QUAD) + (s * QUAD + u * STREAM), P)
            last.then_inc(onehots, 1)

        with dve.Fori(0, STREAM // (2 * QUAD), 1) as it:
            pairs = []
            for s in range(2):
                compare(it, s)
                pairs.append([nc.values_load_multi_w_load_instructions(
                    tile_pair[0:1, bass.ds(it * (2 * QUAD) + (s * QUAD + u * STREAM), QUAD)], engines=(DVE_ENGINE,),
                    min_val=0, max_val=NB * NB,
                    skip_runtime_bounds_check_because="counts of pairs of blocks, less one, cut to NB * NB")[1]
                    for u in range(2)])
            for s in range(2):
                dve.wait_ge(counted, it * 2 + s + 1)
                for j in range(QUAD):
                    for u in range(2):
                        dve.wait_ge(added, it * (4 * QUAD) + s * (2 * QUAD) + 2 * j + u + 4 * QUAD - 1)
                        to = adj[:, bass.ds(pairs[s][u][j] * P, P)]
                        dve.tensor_tensor(to, bank[s][u][:, j], to, ALU.add).then_inc(added, 1)

    @block.tensor
    def _(pe):
        with pe.Fori(0, STREAM // (2 * QUAD), 1) as it:
            for s in range(2):
                pe.wait_ge(onehots, it * 2 + s + 1)
                pe.wait_ge(added, it * (4 * QUAD) + (s + 1) * (2 * QUAD))
                for u in range(2):
                    for j in range(QUAD):
                        last = pe.matmul(bank[s][u][:, j], onehot[:, s, u, 0, :, j], onehot[:, s, u, 1, :, j],
                                         start=True, stop=True)
                last.then_inc(counted, 1)


def store_adjacency(nc, adj, adj_dram):
    with ExitStack() as ctx, nc.Block() as block:
        stored = Phase(nc, ctx, "adj_store").sem("stored")

        @block.sync
        def _(sp):
            for b in range(0, NB, DB):
                sp.dma_start(adj_dram[b:b + DB].rearrange("b p n -> p b n"),
                             adj[:, b * NPAD:(b + DB) * NPAD].rearrange("p (b n) -> p b n", b=DB)).then_inc(stored, 16)
            sp.wait_ge(stored, 16 * (NB // DB))


CH = 5


def neighbour_sums(nc, name, k, adj_dram, g, acc, turned=False):
    with ExitStack() as ctx, nc.Block() as block:
        f = Phase(nc, ctx, name)
        slab = f.sb("slab", [P, DB, NB, P], U16)
        count = f.sb("count", [P, CH, CH, P])
        count_t = f.sb("count_t", [P, CH, CH, P]) if turned else count
        bank = [f.ps(f"sum{s}", [P, 512]) for s in range(2)]
        turn = [f.ps(f"turn{s}", [P, 8, P]) for s in range(2)] if turned else []
        landed = [f.sem(f"landed{j}") for j in range(DB)]
        widened, summed, block_done, taken, passed_sp, passed_pool, flipped, flipped_copied = (f.sem(n) for n in (
            "widened", "summed", "block_done", "taken", "passed_sp", "passed_pool", "flipped", "flipped_copied"))
        chunks = NB // CH
        ready = flipped_copied if turned else widened

        @block.sync
        def _(sp):
            with sp.Fori(0, NB // DB, 1) as it:
                for j in range(DB):
                    sp.wait_ge(widened, (it * DB + j + 1) * chunks)
                    if turned:
                        src = adj_dram[:, :, bass.ds((it * DB + j) * P, P)].rearrange("b p n -> p b n")
                    else:
                        src = adj_dram[bass.ds(it * DB + j, 1)].rearrange("o p (b n) -> p (o b) n", n=P)
                    sp.dma_start(slab[:, j], src).then_inc(landed[j], 16)

        @block.gpsimd
        def _(pool):
            pool.sem_inc(widened, DB * chunks)
            with pool.Fori(0, NB // DB, 1) as it:
                for j in range(DB):
                    pool.wait_ge(landed[j], it * 16 + 16)
                    for c in range(chunks):
                        hold(pool, summed, (it * DB + j) * chunks + c + 1, passed_pool)
                        pool.tensor_copy(count[:, c], slab[:, j, c * CH:(c + 1) * CH]).then_inc(widened, 1)

        @block.tensor
        def _(pe):
            pe.sem_inc(summed, chunks)
            with pe.Fori(0, NB // DB, 1) as it:
                for j in range(DB):
                    pe.wait_ge(taken, it * DB + j + (2 if j == 0 else 1))

                    def flip(c):
                        n = (it * DB + j) * chunks + c
                        pe.wait_ge(widened, n + DB * chunks + 1)
                        for b in range(CH):
                            last = pe.transpose(turn[c % 2][:, b], count[:, c, b], k.ident[:, :])
                        last.then_inc(flipped, 1)

                    if turned:
                        flip(0)
                    for c in range(chunks):
                        n = (it * DB + j) * chunks + c
                        if turned:
                            if c + 1 < chunks:
                                flip(c + 1)
                            pe.wait_ge(flipped_copied, n + 1)
                        else:
                            pe.wait_ge(widened, n + DB * chunks + 1)
                        for b in range(CH):
                            last = pe.matmul(bank[j % 2][:, 0:C], count_t[:, c, b], g[:, (c * CH + b) * C:(c * CH + b + 1) * C],
                                             start=(c == 0 and b == 0), stop=(c == chunks - 1 and b == CH - 1))
                        last.then_inc(summed, 1)

        if turned:
            @block.scalar
            def _(act):
                with act.Fori(0, NB // DB, 1) as it:
                    for j in range(DB):
                        for c in range(chunks):
                            n = (it * DB + j) * chunks + c
                            act.wait_ge(flipped, n + 1)
                            act.copy(count_t[:, c], turn[c % 2][:, 0:CH]).then_inc(flipped_copied, 1)

        @block.vector
        def _(dve):
            dve.sem_inc(taken, 2)
            with dve.Fori(0, NB // DB, 1) as it:
                for j in range(DB):
                    dve.wait_ge(summed, (it * DB + j + 1) * chunks + chunks)
                    to = acc[:, bass.ds((it * DB + j) * C, C)]
                    dve.tensor_tensor(to, bank[j % 2][:, 0:C], to, ALU.add).then_inc(taken, 1)


def turn_select(pe, k, turn, sel, first, n):
    for i in range(n):
        last = pe.transpose(turn[:, i], sel[:, first + i], k.ident[:, :])
    return last


def aggregate_kinds(nc, name, k, moved, o, index, table, share, accs):
    with ExitStack() as ctx, nc.Block() as block:
        f = Phase(nc, ctx, name)
        rows = f.sb("rows", [P, BODY, H1])
        sel = f.sb("sel", [P, BODY, P])
        sel_t = f.sb("sel_t", [P, BODY, P])
        kinds = f.sb("kinds", [P, BODY, NREL])
        part = f.sb("part", [P, BODY, NREL])
        weight = f.sb("weight", [P, BODY])
        turn = [f.ps(f"turn{s}", [P, QUAD, P]) for s in range(2)]
        share_ps = [f.ps(f"share{s}", [P, QUAD, NREL]) for s in range(2)]
        bank = [f.ps(f"sum{j}", [P, 512]) for j in range(4)]
        landed = moved.sems
        (sel_ready, turned, turned_copied, shares, parted, weighed, scaled, tile_done, added) = (
            f.sem(n) for n in ("sel_ready", "turned", "turned_copied", "shares", "parted", "weighed",
                               "scaled", "tile_done", "added"))

        gather_rows(f, block, index, table, rows, H1, landed, tile_done)

        @block.vector
        def _(dve):
            dve.sem_inc(added, 4)

            def weigh(it, i):
                n = it * NQ + i + 1
                quad = slice(i * QUAD, (i + 1) * QUAD)
                dve.wait_ge(shares, n)
                dve.tensor_tensor(part[:, quad], share_ps[i % 2][:, :, :], kinds[:, quad], ALU.mult).then_inc(parted, 1)
                dve.wait_ge(parted, n)
                dve.tensor_reduce(weight[:, quad], part[:, quad], AX, ALU.add).then_inc(weighed, 1)
                dve.wait_ge(weighed, n)
                dve.wait_ge(landed[i], moved.after(it + 1))
                dve.tensor_tensor(rows[:, quad], rows[:, quad], spread(weight[:, quad], [P, QUAD, H1]),
                                  ALU.mult).then_inc(scaled, 1)

            def add(it, i):
                add_tiles(nc, dve, o, accs, H1, lambda j: bank[j % 4], it, i * QUAD, QUAD, tile_done, BODY, added, 4)

            with dve.Fori(0, T // BODY, 1) as it:
                for s in range(2):
                    select_kind(dve, k, o, kinds[:, s * HALF:(s + 1) * HALF], it, s)
                    select_matrix(dve, k, o, sel, it, s).then_inc(sel_ready, 1)
                weigh(it, 0)
                for i in range(1, NQ):
                    weigh(it, i)
                    add(it, i - 1)
                add(it, NQ - 1)

        @block.scalar
        def _(act):
            with act.Fori(0, T // BODY, 1) as it:
                for i in range(NQ):
                    act.wait_ge(turned, it * NQ + i + 1)
                    act.copy(sel_t[:, i * QUAD:(i + 1) * QUAD], turn[i % 2][:, :, :]).then_inc(turned_copied, 1)

        @block.tensor
        def _(pe):
            pe.sem_inc(tile_done, BODY)

            def flip(it, i):
                if i % 2 == 0:
                    pe.wait_ge(sel_ready, it * 2 + i // 2 + 1)
                turn_select(pe, k, turn[i % 2], sel, i * QUAD, QUAD).then_inc(turned, 1)

            def look_up(it, i):
                regs = block_numbers(nc, PE_ENGINE, o.block, it * BODY + i * QUAD, QUAD)
                pe.wait_ge(turned_copied, it * NQ + i + 1)
                for j in range(QUAD):
                    last = pe.matmul(share_ps[i % 2][:, j], sel_t[:, i * QUAD + j],
                                     share[:, bass.ds(regs[j] * NREL, NREL)], start=True, stop=True)
                last.then_inc(shares, 1)

            def add_up(it, i):
                pe.wait_ge(scaled, it * NQ + i + 1)
                for j in range(i * QUAD, (i + 1) * QUAD):
                    pe.wait_ge(added, it * BODY + j + 1)
                    pe.matmul(bank[j % 4][:, 0:H1], sel[:, j], rows[:, j], start=True, stop=True)\
                      .then_inc(tile_done, 1)

            with pe.Fori(0, T // BODY, 1) as it:
                flip(it, 0)
                flip(it, 1)
                look_up(it, 0)
                look_up(it, 1)
                for i in range(2, NQ):
                    flip(it, i)
                    add_up(it, i - 2)
                    look_up(it, i)
                add_up(it, NQ - 2)
                add_up(it, NQ - 1)

    moved.end(T // BODY)


def by_tile(t):
    return t[:, :].rearrange("p (h t) -> p t h", h=HEADS)


def edge_scores(nc, name, k, moved, o, table_k, q, scores):
    with ExitStack() as ctx, nc.Block() as block:
        f = Phase(nc, ctx, name)
        scores = by_tile(scores)
        rows = f.sb("rows", [P, BODY, C])
        sel = f.sb("sel", [P, BODY, P])
        sel_t = f.sb("sel_t", [P, 2, QUAD, P])
        turn = [f.ps(f"turn{s}", [P, QUAD, P]) for s in range(2)]
        q_ps = [[f.ps(f"q{s}{h}", [P, 2, C]) for h in range(2)] for s in range(2)]
        landed = moved.sems
        (sel_ready, turned, sel_t_ready, queries, multiplied, scored, passed_dve) = (f.sem(n) for n in (
            "sel_ready", "turned", "sel_t_ready", "queries", "multiplied", "scored", "passed_dve"))

        gather_rows(f, block, o.other, table_k, rows, C, landed, scored)

        @block.vector
        def _(dve):
            dve.sem_inc(scored, BODY)
            with dve.Fori(0, T // BODY, 1) as it:
                for s in range(2):
                    select_matrix(dve, k, o, sel, it, s).then_inc(sel_ready, 1)
                for i in range(NQ):
                    dve.wait_ge(landed[i], moved.after(it + 1))
                    dve.wait_ge(queries, it * NQ + i + 1)
                    for h in range(2):
                        j = i * QUAD + 2 * h
                        last = dve.tensor_tensor(rows[:, j:j + 2], rows[:, j:j + 2], q_ps[i % 2][h][:, :, :], ALU.mult)
                    last.then_inc(multiplied, 1)
                    hold(dve, multiplied, it * NQ + i + 1, passed_dve)
                    dve.tensor_reduce(scores[:, bass.ds(it * BODY + i * QUAD, QUAD), :],
                                      rows[:, i * QUAD:(i + 1) * QUAD].rearrange("p j (h d) -> p j h d", h=HEADS),
                                      AX, ALU.add).then_inc(scored, QUAD)

        @block.scalar
        def _(act):
            with act.Fori(0, T // BODY, 1) as it:
                for i in range(NQ):
                    act.wait_ge(turned, it * NQ + i + 1)
                    act.copy(sel_t[:, i % 2], turn[i % 2][:, :, :]).then_inc(sel_t_ready, 1)

        @block.tensor
        def _(pe):
            def flip(it, i):
                if i % 2 == 0:
                    pe.wait_ge(sel_ready, it * 2 + i // 2 + 1)
                turn_select(pe, k, turn[i % 2], sel, i * QUAD, QUAD).then_inc(turned, 1)

            with pe.Fori(0, T // BODY, 1) as it:
                flip(it, 0)
                for i in range(NQ):
                    if i + 1 < NQ:
                        flip(it, i + 1)
                    regs = block_numbers(nc, PE_ENGINE, o.block, it * BODY + i * QUAD, QUAD)
                    pe.wait_ge(sel_t_ready, it * NQ + i + 1)
                    pe.wait_ge(scored, it * BODY + i * QUAD + 3 * QUAD)
                    for t in range(QUAD):
                        last = pe.matmul(q_ps[i % 2][t // 2][:, t % 2], sel_t[:, i % 2, t], q[:, bass.ds(regs[t] * C, C)],
                                         start=True, stop=True)
                    last.then_inc(queries, 1)

    moved.end(T // BODY)


G = T * HEADS // P
LOW = 2.0 ** 126


def softmax_weights(nc, name, k, o, scores, ends_dram, carry_dram):
    with ExitStack() as ctx, nc.Block() as block:
        f = Phase(nc, ctx, name)
        N2 = G * P
        wide_key = f.sb("wide_key", [P, T * HEADS])
        st, kt, pen_f, pen_b, fwd, bwd, tmp = (f.sb(n, [P, N2]) for n in (
            "st", "kt", "pen_f", "pen_b", "fwd", "bwd", "tmp"))
        ends = f.sb("ends", [P, 4, G])
        ends_t = f.sb("ends_t", [4 * G, P])
        row = f.sb("row", [HEADS, 4, T])
        inner = f.sb("inner", [HEADS, T])
        joint = f.sb("joint", [HEADS, T + 1])
        go = f.sb("go", [HEADS, T])
        carried = f.sb("carried", [HEADS, T])
        carry = f.sb("carry", [HEADS, 2, T])
        carry_rows = f.sb("carry_rows", [2 * G, P])
        carry_t = f.sb("carry_t", [P, 2, G])
        bank = [f.ps(f"bank{i}", [P, 4, P]) for i in range(8)]
        (keys_ready, turned, copied, step, ends_ready, ends_turned, ends_copied, out_done, row_done, carry_ready,
         carry_out, carry_in, carry_turned, carry_copied, below, weights, turned_back) = (f.sem(n) for n in (
             "keys_ready", "turned", "copied", "step", "ends_ready", "ends_turned", "ends_copied", "out_done",
             "row_done", "carry_ready", "carry_out", "carry_in", "carry_turned", "carry_copied", "below",
             "weights", "turned_back"))

        def grouped(t):
            return t[:, :].rearrange("p (g e) -> p g e", g=G)

        @block.tensor
        def _(pe):
            for src, base in ((scores, 0), (wide_key, 4)):
                if base:
                    pe.wait_ge(keys_ready, 1)
                for g in range(G):
                    last = pe.transpose(bank[base + g // 4][:, g % 4], src[:, g * P:(g + 1) * P], k.ident[:, :])
                last.then_inc(turned, 1)
            pe.wait_ge(ends_ready, 1)
            pe.transpose(bank[0][0:4 * G, 0], ends[:, :, :].rearrange("p a g -> p (a g)"), k.ident[:, :])\
              .then_inc(ends_turned, 1)
            pe.wait_ge(carry_in, 16)
            pe.transpose(bank[1][:, 0, 0:2 * G], carry_rows[:, :], k.ident[0:2 * G, 0:2 * G]).then_inc(carry_turned, 1)
            pe.wait_ge(weights, 1)
            for g in range(G):
                last = pe.transpose(bank[g // 4][:, g % 4], st[:, g * P:(g + 1) * P], k.ident[:, :])
            last.then_inc(turned_back, 1)

        @block.scalar
        def _(act):
            for dst, base in ((st, 0), (kt, 4)):
                act.wait_ge(turned, 1 if base == 0 else 2)
                for b in range(0, G, 4):
                    n = min(4, G - b)
                    last = act.copy(grouped(dst)[:, b:b + n], bank[base + b // 4][:, 0:n])
                last.then_inc(copied, 1)
            act.wait_ge(ends_turned, 1)
            act.copy(ends_t[:, :], bank[0][0:4 * G, 0]).then_inc(ends_copied, 1)
            act.wait_ge(carry_turned, 1)
            act.copy(carry_t[:, :, :].rearrange("p a g -> p (a g)"), bank[1][:, 0, 0:2 * G]).then_inc(carry_copied, 1)
            act.wait_ge(below, 1)
            act.activation(st[:, :], tmp[:, :], ACT.Exp, scale=float(HD) ** -0.5).then_inc(weights, 1)
            act.wait_ge(turned_back, 1)
            for b in range(0, G, 4):
                n = min(4, G - b)
                act.copy(scores[:, b * P:(b + n) * P].rearrange("p (g e) -> p g e", g=n), bank[b // 4][:, 0:n])

        @block.vector
        def _(dve):
            ch = Chain(dve, step)
            dve.tensor_copy(wide_key[:, :].rearrange("p (h t) -> p h t", h=HEADS), repeat(o.key[:, :], [P, HEADS, T]))\
               .then_inc(keys_ready, 1)
            dve.wait_ge(copied, 2)
            for pen, lo, edge in ((pen_f, 1, 0), (pen_b, 0, P - 1)):
                ch.done(dve.tensor_tensor(pen[:, lo:lo + N2 - 1], kt[:, 1:N2], kt[:, 0:N2 - 1], ALU.is_equal))
                ch.done(dve.memset(grouped(pen)[:, :, edge:edge + 1], 0.0))
                ch.done(dve.tensor_scalar(pen[:, :], pen[:, :], LOW, -LOW, ALU.mult, ALU.add))
            dve.tensor_tensor_scan(fwd[:, :], pen_f[:, :], st[:, :], -LOW, ALU.add, ALU.max)
            ch.done(dve.tensor_tensor_scan(bwd[:, ::-1], pen_b[:, ::-1], st[:, ::-1], -LOW, ALU.add, ALU.max))
            for i, (t, e) in enumerate(((fwd, P - 1), (bwd, 0), (kt, 0), (kt, P - 1))):
                last = dve.tensor_copy(ends[:, i], grouped(t)[:, :, e])
            last.then_inc(ends_ready, 1)
            for pen, e in ((pen_f, 0), (pen_b, P - 1)):
                ch.done(dve.tensor_tensor(grouped(pen), grouped(kt), spread(grouped(kt)[:, :, e], [P, G, P]), ALU.is_equal))
                ch.done(dve.tensor_scalar(pen[:, :], pen[:, :], LOW, -LOW, ALU.mult, ALU.add))
            ch.done(dve.tensor_tensor(tmp[:, :], fwd[:, :], bwd[:, :], ALU.max))
            dve.wait_ge(row_done, 16)
            dve.tensor_tensor(inner[:, :], row[:, 2], row[:, 3], ALU.is_equal)
            dve.memset(joint[:, 0:1], 0.0)
            dve.memset(joint[:, T:T + 1], 0.0)
            ch.done(dve.tensor_tensor(joint[:, 1:T], row[:, 2, 1:T], row[:, 3, 0:T - 1], ALU.is_equal))
            ch.done(dve.tensor_tensor(go[:, :], inner[:, :], joint[:, 0:T], ALU.mult))
            ch.done(dve.tensor_scalar(go[:, :], go[:, :], LOW, -LOW, ALU.mult, ALU.add))
            ch.done(dve.tensor_tensor_scan(carried[:, :], go[:, :], row[:, 0], -LOW, ALU.add, ALU.max))
            dve.memset(carry[:, 0, 0:1], -LOW)
            ch.done(dve.tensor_scalar(carry[:, 0, 1:T], joint[:, 1:T], LOW, -LOW, ALU.mult, ALU.add))
            ch.done(dve.tensor_tensor(carry[:, 0, 1:T], carry[:, 0, 1:T], carried[:, 0:T - 1], ALU.add))
            ch.done(dve.tensor_tensor(go[:, :], inner[:, :], joint[:, 1:T + 1], ALU.mult))
            ch.done(dve.tensor_scalar(go[:, :], go[:, :], LOW, -LOW, ALU.mult, ALU.add))
            ch.done(dve.tensor_tensor_scan(carried[:, ::-1], go[:, ::-1], row[:, 1, ::-1], -LOW, ALU.add, ALU.max))
            dve.memset(carry[:, 1, T - 1:T], -LOW)
            ch.done(dve.tensor_scalar(carry[:, 1, 0:T - 1], joint[:, 1:T], LOW, -LOW, ALU.mult, ALU.add))
            dve.tensor_tensor(carry[:, 1, 0:T - 1], carry[:, 1, 0:T - 1], carried[:, 1:T], ALU.add).then_inc(carry_ready, 1)
            dve.wait_ge(carry_copied, 1)
            for i, pen in enumerate((pen_f, pen_b)):
                ch.done(dve.tensor_tensor(grouped(pen), grouped(pen), spread(carry_t[:, i], [P, G, P]), ALU.add))
                ch.done(dve.tensor_tensor(tmp[:, :], tmp[:, :], pen[:, :], ALU.max))
            dve.tensor_tensor(tmp[:, :], st[:, :], tmp[:, :], ALU.subtract).then_inc(below, 1)

        @block.sync
        def _(sp):
            sp.wait_ge(ends_copied, 1)
            sp.dma_start(ends_dram, ends_t[:, :]).then_inc(out_done, 16)
            sp.wait_ge(out_done, 16)
            sp.dma_start(row[:, :, :], ends_dram.rearrange("(a g) p -> a (g p)", a=4).rearrange("a (h t) -> h a t", h=HEADS))\
              .then_inc(row_done, 16)
            sp.wait_ge(carry_ready, 1)
            sp.dma_start(carry_dram.rearrange("(a g) p -> a (g p)", a=2).rearrange("a (h t) -> h a t", h=HEADS), carry[:, :, :])\
              .then_inc(carry_out, 16)
            sp.wait_ge(carry_out, 16)
            sp.dma_start(carry_rows[:, :], carry_dram).then_inc(carry_in, 16)


def mix_values(nc, name, k, moved, o, table_v, weights, accs):
    with ExitStack() as ctx, nc.Block() as block:
        f = Phase(nc, ctx, name)
        width = C + HEADS
        rows = f.sb("rows", [P, BODY, width])
        sel = f.sb("sel", [P, BODY, P])
        bank = [f.ps(f"sum{j}", [P, 512]) for j in range(8)]
        landed = moved.sems
        (sel_ready, copied, weighted, tile_done, added, passed_act) = (f.sem(n) for n in (
            "sel_ready", "copied", "weighted", "tile_done", "added", "passed_act"))

        gather_rows(f, block, o.other, table_v, rows, C, landed, tile_done)

        def weights_of(it, i):
            return by_tile(weights)[:, bass.ds(it * BODY + i * QUAD, QUAD), :]

        @block.vector
        def _(dve):
            dve.sem_inc(added, 8)

            def weigh(it, i):
                dve.wait_ge(landed[i], moved.after(it + 1))
                v = rows[:, i * QUAD:(i + 1) * QUAD, 0:C].rearrange("p j (h d) -> p j h d", h=HEADS)
                dve.tensor_tensor(v, v, weights_of(it, i).unsqueeze(3).to_broadcast([P, QUAD, HEADS, HD]),
                                  ALU.mult).then_inc(weighted, 1)

            def add(it, i):
                add_tiles(nc, dve, o, accs, width, lambda j: bank[j % 8], it, i * QUAD, QUAD,
                          tile_done, BODY, added, 8)

            with dve.Fori(0, T // BODY, 1) as it:
                for s in range(2):
                    select_matrix(dve, k, o, sel, it, s).then_inc(sel_ready, 1)
                weigh(it, 0)
                for i in range(1, NQ):
                    weigh(it, i)
                    add(it, i - 1)
                add(it, NQ - 1)

        @block.scalar
        def _(act):
            with act.Fori(0, T // BODY, 1) as it:
                for i in range(NQ):
                    hold(act, tile_done, it * BODY + (i + 1) * QUAD, passed_act)
                    act.copy(rows[:, i * QUAD:(i + 1) * QUAD, C:width], weights_of(it, i)).then_inc(copied, 1)

        @block.tensor
        def _(pe):
            pe.sem_inc(tile_done, BODY)
            with pe.Fori(0, T // BODY, 1) as it:
                for i in range(NQ):
                    if i % 2 == 0:
                        pe.wait_ge(sel_ready, it * 2 + i // 2 + 1)
                    pe.wait_ge(copied, it * NQ + i + 1)
                    pe.wait_ge(weighted, it * NQ + i + 1)
                    for j in range(i * QUAD, (i + 1) * QUAD):
                        pe.wait_ge(added, it * BODY + j + 1)
                        pe.matmul(bank[j % 8][:, 0:width], sel[:, j], rows[:, j], start=True, stop=True)\
                          .then_inc(tile_done, 1)

    moved.end(T // BODY)


def keep_largest(nc, name, src, dst):
    with ExitStack() as ctx, nc.Block() as block:
        f = Phase(nc, ctx, name)
        row = f.sb("row", [P, DB, C])
        left = f.sb("left", [P, DB, C])
        eight = f.sb("eight", [P, DB, 8])
        staged, found, struck, masked = f.sem("staged"), f.sem("found"), f.sem("struck"), f.sem("masked")
        passed, passed_dve = f.sem("passed_act"), f.sem("passed_dve")
        rounds = MAXK // 8

        @block.scalar
        def _(act):
            act.sem_inc(masked, 1)
            with act.Fori(0, NB // DB, 1) as it:
                hold(act, masked, it + 1, passed)
                for to in (row, left):
                    last = act.copy(to[:, :, :].rearrange("p j c -> p (j c)"), src[:, bass.ds(it * (DB * C), DB * C)])
                last.then_inc(staged, 1)

        @block.vector
        def _(dve):
            with dve.Fori(0, NB // DB, 1) as it:
                hold(dve, staged, it + 1, passed_dve)
                for r in range(rounds):
                    for j in range(DB):
                        if r > 0:
                            hold(dve, struck, it * (rounds * DB) + (r - 1) * DB + j + 1, passed_dve)
                        dve.max(eight[:, j], left[:, j]).then_inc(found, 1)
                    for j in range(DB):
                        n = it * (rounds * DB) + r * DB + j + 1
                        hold(dve, found, n, passed_dve)
                        dve.match_replace(left[:, j], eight[:, j], left[:, j], -BIG).then_inc(struck, 1)
                dve.wait_ge(struck, it * (rounds * DB) + rounds * DB)
                dve.scalar_tensor_tensor(dst[:, bass.ds(it * (DB * C), DB * C)],
                                         left[:, :, :].rearrange("p j c -> p (j c)"), -BIG,
                                         row[:, :, :].rearrange("p j c -> p (j c)"), ALU.is_equal, ALU.mult)\
                   .then_inc(masked, 1)


def batch_norm(nc, name, k, y, gamma, beta, x):
    with ExitStack() as ctx, nc.Block() as block:
        f = Phase(nc, ctx, name)
        sq = f.sb("sq", [P, NB * C])
        mean = f.sb("mean", [P, C])
        a = f.sb("a", [P, C])
        r = f.sb("r", [P, C])
        t = f.sb("t", [P, C])
        sum_ps = [f.ps(f"sum{s}", [P, C]) for s in range(2)]
        step, summed, centred, squared, var_ready, rooted = (f.sem(n) for n in (
            "step", "summed", "centred", "squared", "var_ready", "rooted"))
        y3, full = blocks(y), [P, NB, C]

        @block.tensor
        def _(pe):
            def column_sums(out, src):
                for b in range(NB):
                    rows = P if b < NB - 1 else TAIL
                    last = pe.matmul(out, k.ones[0:rows, :], src[0:rows, b * C:(b + 1) * C],
                                     start=(b == 0), stop=(b == NB - 1))
                last.then_inc(summed, 1)
            column_sums(sum_ps[0][:, :], y)
            pe.wait_ge(squared, 1)
            column_sums(sum_ps[1][:, :], sq)

        @block.vector
        def _(dve):
            ch = Chain(dve, step)
            dve.wait_ge(summed, 1)
            ch.done(dve.tensor_scalar(mean[:, :], sum_ps[0][:, :], 1.0 / N, None, ALU.mult))
            dve.tensor_tensor(y3, y3, repeat(mean[:, :], full), ALU.subtract).then_inc(centred, 1)
            dve.wait_ge(summed, 2)
            dve.tensor_scalar(a[:, :], sum_ps[1][:, :], 1.0 / N, BN_EPS, ALU.mult, ALU.add).then_inc(var_ready, 1)
            dve.wait_ge(rooted, 1)
            inverse_root(dve, ch, r[:, :], a[:, :], t[:, :])
            ch.done(dve.tensor_tensor(r[:, :], r[:, :], gamma[:, :], ALU.mult))
            ch.done(dve.tensor_tensor(y3, y3, repeat(r[:, :], full), ALU.mult))
            ch.done(dve.tensor_tensor(y3, y3, repeat(beta[:, :], full), ALU.add))
            ch.done(dve.scalar_tensor_tensor(y[:, :], y[:, :], SLOPE, y[:, :], ALU.mult, ALU.max))
            dve.tensor_tensor(x[:, :], x[:, :], y[:, :], ALU.add)

        @block.scalar
        def _(act):
            act.wait_ge(centred, 1)
            act.activation(sq[:, :], y[:, :], ACT.Square).then_inc(squared, 1)
            act.wait_ge(var_ready, 1)
            act.activation(r[:, :], a[:, :], ACT.Sqrt).then_inc(rooted, 1)


def store_table(nc, name, stores, work=None):
    with ExitStack() as ctx, nc.Block() as block:
        f = Phase(nc, ctx, name)
        stored, step = f.sem("stored"), f.sem("step")

        @block.sync
        def _(sp):
            for table, src, width in stores:
                sp.dma_start(table.rearrange("(b p) c -> p b c", p=P), blocks(src, width)).then_inc(stored, 16)
            sp.wait_ge(stored, 16 * len(stores))

        if work is not None:
            @block.vector
            def _(dve):
                work(dve, Chain(dve, step))


def vector_work(nc, name, work):
    with ExitStack() as ctx, nc.Block() as block:
        step = Phase(nc, ctx, name).sem("step")

        @block.vector
        def _(dve):
            work(dve, Chain(dve, step))


def load(nc, name, loads):
    with ExitStack() as ctx, nc.Block() as block:
        loaded = Phase(nc, ctx, name).sem("loaded")

        @block.sync
        def _(sp):
            for dst, src in loads:
                sp.dma_start(dst, src).then_inc(loaded, 16)
            sp.wait_ge(loaded, 16 * len(loads))


def clear_semaphores(nc):
    used = sorted(nc.released_uncleared_semaphores)
    with nc.Block() as block:
        @block.gpsimd
        def _(pool):
            first = used[0]
            for a, b in zip(used, used[1:] + [None]):
                if b != a + 1:
                    pool.sem_clear(range(first, a + 1))
                    first = b


def on_all(vector):
    return vector.partition_broadcast(P)


def build(nc, A, out):
    with ExitStack() as top:
        def sb(name, shape, dt=F32):
            return top.enter_context(nc.sbuf_tensor(name, shape, dt))

        def dram(name, shape, dt=F32):
            return nc.dram_tensor(name, shape, dt, kind="Internal").ap()

        k = make_consts(nc, top, sb)
        by_dst = Order(sb, dram)
        moved = IndirectCount(nc, top)
        count_d = sb("count_d", [P, NB])
        count_s = sb("count_s", [P, NB])
        root_d = sb("root_d", [P, NB])
        root_s = sb("root_s", [P, NB])
        mean_d = sb("mean_d", [P, NB])
        share = sb("share", [P, NB * NREL])
        table = dram("table", [NPAD, C])
        table_v = dram("table_v", [NPAD, C])
        table_r = dram("table_r", [NPAD * NREL, H1])
        ends_dram = dram("ends_dram", [4 * G, P])
        carry_dram = dram("carry_dram", [2 * G, P])
        adj_dram = dram("adj_dram", [NB, P, NPAD], U16)
        pair_records = dram("pair_records", [P * TP, 2], BF16)

        with ExitStack() as ctx:
            pair_block = ctx.enter_context(nc.sbuf_tensor("pair_block", [1, TP], I32))
            places = ctx.enter_context(nc.sbuf_tensor("places", [P, 2, TP], BF16))
            e = Keys(nc, ctx)
            with ExitStack() as c:
                setup(nc, c, k, e, A, by_dst.records, pair_records)
            with ExitStack() as c, nc.Block() as block:
                rank_edges(nc, block, c, "pair", e.src_high, e.dst_high, NB, TP, k, e.slot_p, pair_block, None, False, [])
            with ExitStack() as c, nc.Block() as block:
                scatter_records(nc, block, c, "pair", pair_records, e.slot_p, e.pair, moved)
                rank_edges(nc, block, c, "dst", e.dst_low, e.dst_high, P, T, k, e.slot_d, by_dst.block, count_d, True,
                           [(e.dst_low, e.dst_kind, NB * NREL, share), (e.src_low, e.src_high, NB, count_s)])
            with ExitStack() as c:
                places_in = c.enter_context(nc.sbuf_tensor("places_in", [P, TP, 2], BF16))
                load(nc, "places_load", [(places_in[:, :, :], pair_records.rearrange("(p t) c -> p t c", p=P))])
                vector_work(nc, "places_split", lambda dve, ch: dve.tensor_copy(
                    places[:, :, :], places_in[:, :, :].rearrange("p t c -> p c t")))
            with ExitStack() as c:
                adj = c.enter_context(nc.sbuf_tensor("adj", [P, NB * NPAD + P], U16))
                with ExitStack() as c2, nc.Block() as block:
                    scatter_records(nc, block, c2, "dst", by_dst.records, e.slot_d, e.record, moved)
                    build_adjacency(nc, block, c2, k, places, pair_block, adj)
                store_adjacency(nc, adj, adj_dram)
        x = sb("x_sb", [P, NB * C])
        with ExitStack() as c, nc.Block() as block:
            fetch_records(nc, block, c, by_dst)
            f = Phase(nc, c, "x_load")
            tail_zero, loaded = f.sem("tail_zero"), f.sem("loaded")

            @block.scalar
            def _(act):
                act.dma_start(x[:, 0:(NB - 1) * C].rearrange("p (b c) -> p b c", b=NB - 1),
                              A["x"][0:(NB - 1) * P, :].rearrange("(b p) c -> p b c", p=P)).then_inc(loaded, 16)
                act.wait_ge(tail_zero, 1)
                act.dma_start(x[0:TAIL, (NB - 1) * C:NB * C], A["x"][(NB - 1) * P:N, :]).then_inc(loaded, 16)
                act.wait_ge(loaded, 32)

            @block.gpsimd
            def _(pool):
                pool.memset(x[:, (NB - 1) * C:NB * C], 0.0).then_inc(tail_zero, 1)
        degrees(nc, count_d, count_s, root_d, root_s, mean_d)

        def finish():
            with ExitStack() as c, nc.Block() as block:
                stored = Phase(nc, c, "out").sem("stored")

                @block.sync
                def _(sp):
                    sp.dma_start(out[0:(NB - 1) * P, :].rearrange("(b p) c -> p b c", p=P),
                                 x[:, 0:(NB - 1) * C].rearrange("p (b c) -> p b c", b=NB - 1)).then_inc(stored, 16)
                    sp.dma_start(out[(NB - 1) * P:N, :], x[0:TAIL, (NB - 1) * C:NB * C]).then_inc(stored, 16)
                    sp.wait_ge(stored, 32)

        with ExitStack() as ctx:
            f = Phase(nc, ctx, "l0")
            acc = f.sb("acc", [P, NB * C])
            g = f.sb("g", [P, NB * C])
            wide = f.sb("wide", [P, NB * CW])
            b1, gamma1, beta1 = (f.sb(n, [P, CW]) for n in ("b1", "gamma1", "beta1"))
            b2, gamma2, beta2 = (f.sb(n, [P, C]) for n in ("b2", "gamma2", "beta2"))
            load(nc, "l0_load", [(t[:, :], on_all(A[f"L0_gnn_{n}"])) for t, n in (
                (b1, "b1"), (gamma1, "gamma1"), (beta1, "beta1"), (b2, "b2"), (gamma2, "gamma2"), (beta2, "beta2"))])
            norm_relu(nc, "l0_in", x, g, C, scale=root_d)

            def start_acc(dve, ch):
                dve.tensor_copy(acc[:, :], g[:, :])
            vector_work(nc, "l0_s1", start_acc)
            neighbour_sums(nc, "l0_a1", k, adj_dram, g, acc)

            def end_acc(dve, ch):
                dve.tensor_tensor(blocks(g), blocks(acc), spread(root_d[:, :], [P, NB, C]), ALU.mult)
                ch.done(dve.tensor_scalar(share[:, :], share[:, :], 1.0, None, ALU.max))
                dve.reciprocal(share[:, :], share[:, :])
            vector_work(nc, "l0_e1", end_acc)
            dense(nc, "l0_w1", k, g, C // P, CW, whole(A["L0_gnn_W1"]), [(0, CW, wide, b1)])
            norm_relu(nc, "l0_mid", wide, wide, CW, scale=root_d, gamma=gamma1, beta=beta1)
            dense(nc, "l0_w2", k, wide, CW // P, C, whole(A["L0_gnn_W2"]), [(0, C, acc, None)])
            vector_work(nc, "l0_s2", lambda dve, ch: dve.tensor_copy(g[:, :], acc[:, :]))
            neighbour_sums(nc, "l0_a2", k, adj_dram, g, acc)

            def end_acc2(dve, ch):
                ch.done(dve.tensor_tensor(blocks(g), blocks(acc), spread(root_d[:, :], [P, NB, C]), ALU.mult))
                dve.tensor_tensor(blocks(g), blocks(g), repeat(b2[:, :], [P, NB, C]), ALU.add)
            vector_work(nc, "l0_e2", end_acc2)
            norm_relu(nc, "l0_out", g, g, C, gamma=gamma2, beta=beta2, add_to=x)

        clear_semaphores(nc)

        with ExitStack() as ctx:
            f = Phase(nc, ctx, "l1")
            acc = f.sb("acc", [P, NB * C])
            g = f.sb("g", [P, NB * C])
            norm_relu(nc, "l1_in", x, g, C, scale=root_s)
            dense(nc, "l1_w", k, g, C // P, C, whole(A["L1_gnn_W"]), [(0, C, acc, None)])
            vector_work(nc, "l1_s", lambda dve, ch: dve.tensor_copy(g[:, :], acc[:, :]))
            neighbour_sums(nc, "l1_a", k, adj_dram, g, acc, turned=True)

            def end_acc(dve, ch):
                ch.done(dve.tensor_tensor(blocks(acc), blocks(acc), spread(root_s[:, :], [P, NB, C]), ALU.mult))
                dve.tensor_tensor(x[:, :], x[:, :], acc[:, :], ALU.add)
            vector_work(nc, "l1_e", end_acc)

        clear_semaphores(nc)

        with ExitStack() as ctx:
            f = Phase(nc, ctx, "l2")
            h = f.sb("h", [P, NB * H1])
            with ExitStack() as inner:
                fi = Phase(nc, inner, "l2r")
                index = fi.sb("index", [P, T], I32)
                index_f = fi.sb("index_f", [P, T])
                with ExitStack() as dense_part:
                    fd = Phase(nc, dense_part, "l2d")
                    g = fd.sb("g", [P, NB * C])
                    norm_relu(nc, "l2_in", x, g, C)
                    xw = fd.sb("xw", [P, NB * NREL * H1])
                    bias = fd.sb("bias", [P, H1])
                    load(nc, "l2_load", [(bias[:, :], on_all(A["L2_gnn_rgcn_bias"]))])
                    wr = A["L2_gnn_rgcn_weight"]
                    dense(nc, "l2_xw", k, g, C // P, NREL * H1,
                          lambda w: [(w[:, c].rearrange("p (r h) -> p r h", r=NREL),
                                      wr[:, c * P:(c + 1) * P, :].rearrange("r p h -> p r h")) for c in range(C // P)],
                          [(0, NREL * H1, xw, None)])
                    dense(nc, "l2_root", k, g, C // P, H1, whole(A["L2_gnn_rgcn_root"]), [(0, H1, h, bias)])

                    def kind_rows(dve, ch):
                        ch.done(dve.tensor_copy(index_f[:, :], by_dst.other[:, :]))
                        dve.scalar_tensor_tensor(index[:, :], index_f[:, :], float(NREL), by_dst.kind[:, :],
                                                 ALU.mult, ALU.add)
                    store_table(nc, "l2_t", [(table_r.rearrange("(n r) h -> n (r h)", r=NREL), xw, NREL * H1)], kind_rows)
                h_odd = fi.sb("h_odd", [P, NB * H1])
                vector_work(nc, "l2_z", lambda dve, ch: dve.memset(h_odd[:, :], 0.0))
                aggregate_kinds(nc, "l2_a", k, moved, by_dst, index, table_r, share, (h, h_odd))
                vector_work(nc, "l2_y", lambda dve, ch: dve.tensor_tensor(h[:, :], h[:, :], h_odd[:, :], ALU.add))
            q = f.sb("q", [P, NB * C])
            skip = f.sb("skip", [P, NB * C])
            with ExitStack() as inner:
                fi = Phase(nc, inner, "l2p")
                kk = fi.sb("kk", [P, NB * C])
                v = fi.sb("v", [P, NB * C])
                biases = [fi.sb(n, [P, C]) for n in ("bq", "bk", "bv", "bskip")]
                load(nc, "l2_load2", [(t[:, :], on_all(A[f"L2_gnn_{n}"])) for t, n in zip(
                    biases, ("bq", "bk", "bv", "bskip"))])
                dense(nc, "l2_qkv", k, h, 1, 4 * C,
                      lambda w: [(w[:, 0, i * C:(i + 1) * C], A[f"L2_gnn_{n}"]) for i, n in enumerate(
                          ("wq", "wk", "wv", "wskip"))],
                      [(i * C, C, t, b) for i, (t, b) in enumerate(zip((q, kk, v, skip), biases))])
                store_table(nc, "l2_t2", [(table, kk, C), (table_v, v, C)])
            scores = f.sb("scores", [P, T * HEADS])
            edge_scores(nc, "l2_sc", k, moved, by_dst, table, q, scores)
            softmax_weights(nc, "l2_sm", k, by_dst, scores, ends_dram, carry_dram)
            acc = f.sb("acc", [P, NB * (C + HEADS)])
            acc_odd = f.sb("acc_odd", [P, NB * (C + HEADS)])
            gamma = f.sb("gamma", [P, C])
            beta = f.sb("beta", [P, C])
            load(nc, "l2_load3", [(gamma[:, :], on_all(A["L2_gnn_bn_gamma"])), (beta[:, :], on_all(A["L2_gnn_bn_beta"]))])

            def start_acc(dve, ch):
                dve.memset(acc_odd[:, :], 0.0)
                dve.memset(acc[:, :], 0.0)
            vector_work(nc, "l2_s", start_acc)
            mix_values(nc, "l2_mix", k, moved, by_dst, table_v, scores, (acc, acc_odd))

            def end_acc(dve, ch):
                a3 = blocks(acc, C + HEADS)
                den = a3[:, :, C:C + HEADS]
                ch.done(dve.tensor_tensor(acc[:, :], acc[:, :], acc_odd[:, :], ALU.add))
                ch.done(dve.tensor_scalar(den, den, 1e-16, None, ALU.max))
                ch.done(dve.reciprocal(den, den))
                ch.done(dve.tensor_tensor(
                    blocks(q).rearrange("p b (h d) -> p b h d", h=HEADS),
                    a3[:, :, 0:C].rearrange("p b (h d) -> p b h d", h=HEADS),
                    den.unsqueeze(3).to_broadcast([P, NB, HEADS, HD]), ALU.mult))
                dve.tensor_tensor(q[:, :], q[:, :], skip[:, :], ALU.add)
            vector_work(nc, "l2_e", end_acc)
            batch_norm(nc, "l2_bn", k, q, gamma, beta, x)

        clear_semaphores(nc)

        with ExitStack() as ctx:
            f = Phase(nc, ctx, "l3")
            g = f.sb("g", [P, NB * C])
            own = f.sb("own", [P, NB * C])
            neigh = f.sb("neigh", [P, NB * C])
            acc = f.sb("acc", [P, NB * C])
            norm_relu(nc, "l3_in", x, g, C)
            dense(nc, "l3_w", k, g, C // P, 2 * C,
                  lambda w: [(w[:, :, 0:C], A["L3_gnn_W_self"].rearrange("(k p) n -> p k n", p=P)),
                             (w[:, :, C:2 * C], A["L3_gnn_W_neigh"].rearrange("(k p) n -> p k n", p=P))],
                  [(0, C, own, None), (C, C, neigh, None)])
            keep_largest(nc, "l3_k", neigh, g)

            def start_acc(dve, ch):
                dve.memset(acc[:, :], 0.0)
                dve.tensor_tensor(x[:, :], x[:, :], own[:, :], ALU.add)
            vector_work(nc, "l3_s", start_acc)
            neighbour_sums(nc, "l3_a", k, adj_dram, g, acc)

            def end_acc(dve, ch):
                ch.done(dve.tensor_tensor(blocks(acc), blocks(acc), spread(mean_d[:, :], [P, NB, C]), ALU.mult))
                dve.tensor_tensor(x[:, :], x[:, :], acc[:, :], ALU.add)
            vector_work(nc, "l3_e", end_acc)
        finish()


_INS = ['x', 'src', 'dst', 'edge_type_8', 'L0_gnn_W1', 'L0_gnn_b1', 'L0_gnn_gamma1', 'L0_gnn_beta1', 'L0_gnn_W2',
        'L0_gnn_b2', 'L0_gnn_gamma2', 'L0_gnn_beta2', 'L1_gnn_W', 'L2_gnn_rgcn_weight', 'L2_gnn_rgcn_root',
        'L2_gnn_rgcn_bias', 'L2_gnn_wq', 'L2_gnn_bq', 'L2_gnn_wk', 'L2_gnn_bk', 'L2_gnn_wv', 'L2_gnn_bv',
        'L2_gnn_wskip', 'L2_gnn_bskip', 'L2_gnn_bn_gamma', 'L2_gnn_bn_beta', 'L3_gnn_W_self', 'L3_gnn_W_neigh']


def kernel(**inputs):
    import numpy as _np
    import concourse.bacc as _bacc
    from concourse import mybir as _mybir
    from concourse.bass_utils import run_bass_kernel_spmd as _run

    nc = _bacc.Bacc("TRN2", target_bir_lowering=False, num_devices=1)
    arrays, A = {}, {}
    for name in _INS:
        a = _np.asarray(inputs[name])
        if name == "L1_gnn_W":
            a = a.T
        a = _np.ascontiguousarray(a)
        arrays[f"in_{name}"] = a
        A[name] = nc.dram_tensor(f"in_{name}", a.shape, _mybir.dt.from_np(a.dtype), kind="ExternalInput").ap()
    out = nc.dram_tensor("out", (N, C), F32, kind="ExternalOutput").ap()
    build(nc, A, out)
    r = _run(nc, [arrays], core_ids=[0])
    return r.results[0]["out"]
```

```python
from contextlib import ExitStack

import concourse.bass as bass
from concourse import mybir

P = 128
N = 3125
C = 256
E = 50000
NB = -(-N // P)
TAIL = N - (NB - 1) * P
NPAD = NB * P
EP = 125
EC = E // EP
QUAD = 4
NQ = 4
BODY = NQ * QUAD
HALF = BODY // 2
T = -(-((E + NB * (P - 1)) // P) // BODY) * BODY
TP = -(-((E + NB * NB * (P - 1)) // P) // 512) * 512
HEADS = 4
HD = C // HEADS
NREL = 8
H1 = 128
CW = 512
MAXK = 32
HCH = 20
RCH = 8
DEPTH = 4
ROUND_512 = 1.5 * 2.0 ** 32
assert P * max(T, TP) <= 256 * 512
BIG = 2.0 ** 127
LN_EPS = 1e-5
BN_EPS = 1e-5
SLOPE = 0.01

F32 = mybir.dt.float32
BF16 = mybir.dt.bfloat16
I32 = mybir.dt.int32
U16 = mybir.dt.uint16
ALU = mybir.AluOpType
ACT = mybir.ActivationFunctionType
AX = mybir.AxisListType.X
DVE_ENGINE = mybir.EngineType.DVE
PE_ENGINE = mybir.EngineType.PE


class Chain:

    def __init__(self, eng, sem):
        self.eng, self.sem, self.n = eng, sem, 0

    def done(self, ins):
        self.n += 1
        ins.then_inc(self.sem, 1)
        self.eng.wait_ge(self.sem, self.n)


class LoopChain:

    def __init__(self, eng, sem, it, steps, passed):
        self.eng, self.sem, self.before, self.steps, self.passed, self.n = eng, sem, it * steps, steps, passed, 0

    def done(self, ins):
        self.n += 1
        ins.then_inc(self.sem, 1)
        hold(self.eng, self.sem, self.before + self.n, self.passed)

    def end(self):
        assert self.n == self.steps


def hold(eng, sem, value, passed):
    eng.wait_ge(sem, value)
    eng.sem_inc(passed, 1)


def spread(ap, shape):
    return ap.unsqueeze(2).to_broadcast(shape)


def repeat(ap, shape):
    return ap.unsqueeze(1).to_broadcast(shape)


def block_numbers(nc, engine, table, first, n):
    _, regs = nc.values_load_multi_w_load_instructions(
        table[0:1, bass.ds(first, n)], engines=(engine,), min_val=0, max_val=NB - 1,
        skip_runtime_bounds_check_because="counts of blocks that start at or before a tile, less one")
    return regs


def onehots_of(dve, k, out, key, at, width):
    parts, groups = out.shape[0], out.shape[1]
    full = [parts, groups, width, QUAD]
    return dve.tensor_tensor(
        out, k.iota_q[0:parts, 0:width, :].unsqueeze(1).to_broadcast(full),
        key[:, bass.ds(at, groups * QUAD)].rearrange("p (g j) -> p g j", j=QUAD).unsqueeze(2).to_broadcast(full),
        ALU.is_equal)


class IndirectCount:

    def __init__(self, nc, ctx):
        self.sems = [ctx.enter_context(nc.semaphore(f"indirect{i}")) for i in range(NQ)]
        self.before = 0

    def after(self, bodies):
        return bodies * (16 * QUAD) + self.before

    def end(self, bodies):
        self.before += 16 * QUAD * bodies


class Order:

    def __init__(self, sb, dram):
        self.block = sb("dst_block", [1, T], I32)
        self.other = sb("dst_other", [P, T], I32)
        self.low = sb("dst_low", [P, T], F32)
        self.kind = sb("dst_kind", [P, T], F32)
        self.key = sb("dst_key", [P, T], F32)
        self.records = dram("dst_records", [P * T, 4], F32)


def rank_edges(nc, block, ctx, n, low_b, high_b, low_width, tiles_n, k, slot_i, tile_group, count, by_node, extra):

    def sb(name, shape, dt):
        return ctx.enter_context(nc.sbuf_tensor(f"{n}_{name}", shape, dt))

    def ps(name, shape, dt):
        return ctx.enter_context(nc.psum_tensor(f"{n}_{name}", shape, dt))

    def sem(name):
        return ctx.enter_context(nc.semaphore(f"{n}_{name}"))

    W = low_width
    is_low = sb("is_low", [EP, 2, HCH // QUAD, W, QUAD], BF16)
    is_high = sb("is_high", [EP, 2, HCH // QUAD, NB, QUAD], BF16)
    step_low, step_high = (
        t.rearrange("p s g w j -> p (s g) w j")[:, 0:DEPTH * RCH // QUAD].rearrange("p (s g) w j -> p s g w j", s=DEPTH)
        for t in (is_low[:, :, :, :, :], is_high[:, :, :, :, :]))
    seen = sb("seen", [W, NB, EC + 1], F32)
    going = sb("going", [W, NB, EC + 1], BF16)
    low_t = sb("low_t", [W, DEPTH, RCH, EP], BF16)
    before = sb("before", [W, DEPTH, RCH, 2, NB], BF16)
    same = sb("same", [EP, 2, RCH, EP], BF16)
    picked = sb("picked", [EP, 2, RCH, 2, NB], F32)
    slot = sb("slot", [EP, EC], F32)
    part_i = sb("part_i", [EP, EC], I32)
    tile_i = sb("tile_i", [EP, EC], I32)
    part_f = sb("part_f", [EP, EC], F32)
    small_i = sb("small_i", [W, NB], I32)
    tiles = sb("tiles", [W, NB], F32)
    ends = sb("ends", [W, NB], F32)
    starts = sb("starts", [W, NB + 1], F32)
    groups_w = 1 if by_node else W
    starts_n = NB if by_node else NB + 1
    started = sb("started", [groups_w, starts_n, tiles_n], BF16)
    group_f = sb("group_f", [groups_w, tiles_n], F32)
    lefts = [sb(f"is_left{i}", [EP, 2, HCH // QUAD, P, QUAD], BF16) if e[0] is not low_b else is_low
             for i, e in enumerate(extra)]
    rights = [sb(f"is_right{i}", [EP, 2, HCH // QUAD, e[2], QUAD], BF16) for i, e in enumerate(extra)]
    nothing = sb("nothing", [P, 256], BF16)

    hist_ps = [ps(f"hist{s}", [P, 512], F32) for s in range(2)]
    turn_ps = [ps(f"turn{s}", [P, RCH, P], BF16) for s in range(2)]
    pair_ps = ps("pair", [EP, 2, 2, 512], F32)
    total_ps = hist_ps
    slot_ps = hist_ps
    extra_bank = [turn_ps[i][:, :, :].rearrange("p a b -> p (a b)").bitcast(F32) for i in range(len(extra))]

    (onehots, hist_done, hist_copied, passed_act, chain, totals_ready, totals_done, prefix_ready,
     ranked_onehots, turned, turned_copied, paired, masked, looked_up, picked_done, ranks_done, nothing_ready,
     extra_taken, groups_ready, groups_done) = (sem(x) for x in (
         "onehots", "hist_done", "hist_copied", "passed_act", "chain", "totals_ready", "totals_done",
         "prefix_ready", "ranked_onehots", "turned", "turned_copied", "paired", "masked", "looked_up",
         "picked_done", "ranks_done", "nothing_ready", "extra_taken", "groups_ready", "groups_done"))

    def column(onehot, buffer, j):
        return onehot[:, buffer, j // QUAD, :, j % QUAD]

    def slots_by_high(b):
        return slot_ps[b % 2][0:EP, 0:RCH * 2 * NB].rearrange("p (j a h) -> p j a h", a=2, h=NB)

    steps = EC // RCH
    prologue, bodies = 1, (steps - 3) // DEPTH

    def each_step(eng, run):
        for r in range(prologue):
            run(r, r % DEPTH)
        with eng.Fori(0, bodies, 1) as it:
            for u in range(DEPTH):
                run(it * DEPTH + (prologue + u), (prologue + u) % DEPTH)
        for r in range(prologue + bodies * DEPTH, steps):
            run(r, r % DEPTH)

    def is_last(step, n):
        return isinstance(step, int) and step >= steps - n

    @block.vector
    def _(dve):
        ch = Chain(dve, chain)
        dve.sem_inc(hist_done, 2)
        dve.memset(nothing[:, :], 0.0).then_inc(nothing_ready, 1)
        with dve.Fori(0, EC // (2 * HCH), 1) as it:
            for s in range(2):
                at = it * (2 * HCH) + s * HCH
                dve.wait_ge(hist_done, it * 2 + s + 1)
                onehots_of(dve, k, is_low[:, s], low_b, at, W)
                for (left, right, width, _), l, r in zip(extra, lefts, rights):
                    if l is not is_low:
                        onehots_of(dve, k, l[:, s], left, at, P)
                    onehots_of(dve, k, r[:, s], right, at, width)
                onehots_of(dve, k, is_high[:, s], high_b, at, NB).then_inc(onehots, 1)
        dve.wait_ge(hist_copied, EC // HCH + 2)
        for (_, _, width, out), bank in zip(extra, extra_bank):
            last = dve.tensor_copy(out[:, :], bank[:, 0:width])
        if extra:
            last.then_inc(extra_taken, 1)
        if by_node:
            dve.tensor_reduce(count[:, :], seen[:, :, 1:EC + 1], AX, ALU.add).then_inc(totals_ready, 1)
            dve.wait_ge(totals_done, 1)
            ch.done(dve.tensor_scalar(small_i[:, :], total_ps[1][0:W, 0:NB], float(P - 1), None, ALU.add))
        else:
            ch.done(dve.tensor_reduce(tiles[:, :], seen[:, :, 1:EC + 1], AX, ALU.add))
            ch.done(dve.tensor_scalar(small_i[:, :], tiles[:, :], float(P - 1), None, ALU.add))
        ch.done(dve.tensor_scalar(small_i[:, :], small_i[:, :], 7, None, ALU.logical_shift_right))
        if by_node:
            ch.done(dve.tensor_copy(tiles[:, :], small_i[:, :]))
            ch.done(dve.tensor_tensor_scan(ends[:, :], k.ones[0:W, 0:NB], tiles[:, :], 0.0, ALU.mult, ALU.add))
            ch.done(dve.tensor_tensor(starts[:, 0:NB], ends[:, :], tiles[:, :], ALU.subtract))
            ch.done(dve.scalar_tensor_tensor(seen[:, :, 0], starts[:, 0:NB], float(P), total_ps[0][0:W, 0:NB],
                                             ALU.mult, ALU.add))
        else:
            dve.tensor_copy(tiles[:, :], small_i[:, :]).then_inc(totals_ready, 1)
            dve.wait_ge(totals_done, 1)
            ch.done(dve.tensor_copy(tiles[:, :], total_ps[1][0:W, 0:NB]))
            ch.done(dve.tensor_tensor_scan(ends[:, :], k.ones[0:W, 0:NB], tiles[:, :], 0.0, ALU.mult, ALU.add))
            dve.tensor_copy(starts[:, NB:NB + 1], ends[:, NB - 1:NB])
            ch.done(dve.tensor_tensor(starts[:, 0:NB], ends[:, :], tiles[:, :], ALU.subtract))
            ch.done(dve.tensor_tensor(starts[:, 0:NB], starts[:, 0:NB], total_ps[0][0:W, 0:NB], ALU.add))
            ch.done(dve.tensor_scalar(seen[:, :, 0], starts[:, 0:NB], float(P), None, ALU.mult))
        flat = seen[:, :, :].rearrange("p h t -> p (h t)")
        coarse = going[:, :, :].rearrange("p h t -> p (h t)")
        ch.done(dve.tensor_tensor_scan(flat, coarse, flat, 0.0, ALU.mult, ALU.add))
        ch.done(dve.tensor_scalar(coarse, flat, ROUND_512, ROUND_512, ALU.add, ALU.subtract))
        dve.tensor_tensor(flat, flat, coarse, ALU.subtract).then_inc(prefix_ready, 1)

        def compare(step, b):
            onehots_of(dve, k, step_low[:, b], low_b, step * RCH, W)
            onehots_of(dve, k, step_high[:, b], high_b, step * RCH, NB).then_inc(ranked_onehots, 1)

        def mask(step, b):
            dve.wait_ge(paired, step + 1)
            for q in range(2):
                last = dve.tensor_tensor(
                    same[:, b % 2, 4 * q:4 * q + 4],
                    pair_ps[:, b % 2, q, 0:4 * EP].rearrange("p (j e) -> p j e", j=4),
                    repeat(k.earlier[0:EP, 0:EP], [EP, 4, EP]), ALU.mult)
            last.then_inc(masked, 1)

        def pick(step, b):
            dve.wait_ge(looked_up, step + 1)
            for g in range(RCH // QUAD):
                last = dve.tensor_tensor(
                    picked[:, b % 2, g * QUAD:(g + 1) * QUAD],
                    slots_by_high(b)[:, g * QUAD:(g + 1) * QUAD],
                    step_high[:, b, g].rearrange("p h j -> p j h").unsqueeze(2).to_broadcast([EP, QUAD, 2, NB]), ALU.mult)
            last.then_inc(picked_done, 1)

        def total(step, b):
            dve.wait_ge(picked_done, step + 1)
            dve.tensor_reduce(slot[:, bass.ds(step * RCH, RCH)], picked[:, b % 2].rearrange("p j a h -> p j (a h)"),
                              AX, ALU.add).then_inc(ranks_done, 1)

        def run(step, b):
            if not is_last(step, 2):
                compare(step + 2, (b + 2) % DEPTH)
            mask(step, b)
            if not (isinstance(step, int) and step == 0):
                pick(step - 1, (b - 1) % DEPTH)
                total(step - 1, (b - 1) % DEPTH)

        compare(0, 0)
        compare(1, 1)
        each_step(dve, run)
        pick(steps - 1, (steps - 1) % DEPTH)
        total(steps - 1, (steps - 1) % DEPTH)
        dve.wait_ge(ranks_done, EC // RCH)
        ch.done(dve.tensor_copy(slot_i[:, :], slot[:, :]))
        dve.tensor_scalar(part_i[:, :], slot_i[:, :], P - 1, None, ALU.bitwise_and)
        ch.done(dve.tensor_scalar(tile_i[:, :], slot_i[:, :], 7, None, ALU.logical_shift_right))
        dve.tensor_copy(part_f[:, :], part_i[:, :])
        ch.done(dve.tensor_copy(slot[:, :], tile_i[:, :]))
        dve.scalar_tensor_tensor(slot_i[:, :], part_f[:, :], float(tiles_n), slot[:, :], ALU.mult, ALU.add)
        for h in range(starts_n):
            last = dve.tensor_scalar(started[:, h], k.iota_t[0:groups_w, 0:tiles_n], starts[0:groups_w, h:h + 1], None,
                                     ALU.is_ge)
        if by_node:
            ch.done(last)
            dve.tensor_reduce(group_f[:, :], started[:, :, :].rearrange("p h t -> p t h"), AX, ALU.add)\
               .then_inc(groups_ready, 1)
            dve.wait_ge(groups_ready, 1)
        else:
            last.then_inc(groups_ready, 1)
        if by_node:
            dve.tensor_scalar(tile_group[:, :], group_f[:, :], -1.0, None, ALU.add)
        else:
            dve.wait_ge(groups_done, 1)
            for c in range(0, tiles_n, 512):
                last = dve.tensor_scalar(group_f[0:1, c:c + 512], pair_ps[0:1, 0, c // 512, :], -1.0, float(NB * NB),
                                         ALU.add, ALU.min)
            ch.done(last)
            dve.tensor_scalar(tile_group[:, :], group_f[0:1, :], float(P), None, ALU.mult)

    @block.tensor
    def _(pe):
        pe.wait_ge(nothing_ready, 1)
        for bank in extra_bank:
            pe.matmul(bank[:, 0:256], nothing[:, 0:P], nothing[:, :], start=True, stop=False, skip_group_check=True)
        with pe.Fori(0, EC // (2 * HCH), 1) as it:
            for s in range(2):
                pe.wait_ge(onehots, it * 2 + s + 1)
                pe.wait_ge(hist_copied, it * 2 + s + 1)
                for j in range(HCH):
                    for (_, _, width, _), l, r, bank in zip(extra, lefts, rights, extra_bank):
                        pe.matmul(bank[:, 0:width], column(l, s, j), column(r, s, j), start=False, stop=False,
                                  skip_group_check=True)
                    last = pe.matmul(hist_ps[s][0:W, j * NB:(j + 1) * NB], column(is_low, s, j),
                                     column(is_high, s, j), start=True, stop=True)
                last.then_inc(hist_done, 1)
        pe.wait_ge(totals_ready, 1)
        of = count if by_node else tiles
        pe.matmul(total_ps[0][0:W, 0:NB], k.earlier[0:W, 0:W], of[:, :], start=True, stop=True)
        pe.matmul(total_ps[1][0:W, 0:NB], k.ones[0:W, 0:W], of[:, :], start=True, stop=True)\
          .then_inc(totals_done, 1)
        pe.wait_ge(prefix_ready, 1)
        if extra:
            pe.wait_ge(extra_taken, 1)

        def turn(step, b):
            pe.wait_ge(ranked_onehots, step + 1)
            for j in range(RCH):
                last = pe.transpose(turn_ps[b % 2][0:W, j, 0:EP], column(step_low, b, j), k.ident_b[0:EP, 0:EP])
            last.then_inc(turned, 1)

        def pair(step, b):
            pe.wait_ge(turned_copied, step + 1)
            for j in range(RCH):
                last = pe.matmul(pair_ps[:, b % 2, j // 4, j % 4 * EP:(j % 4 + 1) * EP], low_t[:, b, j],
                                 low_t[:, b, j], start=True, stop=True)
            last.then_inc(paired, 1)

        def look_up(step, b):
            pe.wait_ge(masked, step + 1)
            for j in range(RCH):
                pe.matmul(slots_by_high(b)[:, j], low_t[:, b, j], before[:, b, j], start=True, stop=False)
                last = pe.matmul(slots_by_high(b)[:, j, 0], same[:, b % 2, j], column(step_high, b, j),
                                 start=False, stop=True)
            last.then_inc(looked_up, 1)

        def run(step, b):
            pair(step, b)
            if not (isinstance(step, int) and step == 0):
                look_up(step - 1, (b - 1) % DEPTH)
            if not is_last(step, 2):
                turn(step + 2, (b + 2) % DEPTH)

        turn(0, 0)
        turn(1, 1)
        each_step(pe, run)
        look_up(steps - 1, (steps - 1) % DEPTH)
        if not by_node:
            pe.wait_ge(groups_ready, 1)
            for c in range(0, tiles_n, 512):
                for h in range(starts_n):
                    last = pe.matmul(pair_ps[0:1, 0, c // 512, :], k.one_b[0:W, :], started[:, h, c:c + 512],
                                     start=(h == 0), stop=(h == starts_n - 1))
            last.then_inc(groups_done, 1)

    @block.scalar
    def _(act):
        act.sem_inc(hist_copied, 2)
        act.activation(going[:, :, :].rearrange("p h t -> p (h t)"),
                       k.iota_t[0:W, 0:1].to_broadcast([W, NB * (EC + 1)]), ACT.Copy, bias=1.0, scale=0.0)\
           .then_inc(passed_act, 1)
        act.wait_ge(passed_act, 1)
        act.activation(going[:, :, 0], k.iota_t[0:W, 0:NB], ACT.Copy, scale=0.0)
        with act.Fori(0, EC // (2 * HCH), 1) as it:
            for s in range(2):
                hold(act, hist_done, it * 2 + s + 3, passed_act)
                act.copy(seen[:, :, bass.ds(it * (2 * HCH) + s * HCH + 1, HCH)],
                         hist_ps[s][0:W, 0:HCH * NB].rearrange("p (t h) -> p h t", t=HCH)).then_inc(hist_copied, 1)

        def copy(step, b):
            if isinstance(step, int):
                act.wait_ge(turned, step + 1)
            else:
                hold(act, turned, step + 1, passed_act)
            for part, t in enumerate((seen, going)):
                act.copy(before[:, b, :, part], t[:, :, bass.ds(step * RCH, RCH)].rearrange("p h t -> p t h"))
            act.copy(low_t[:, b], turn_ps[b % 2][0:W, :, 0:EP]).then_inc(turned_copied, 1)

        act.wait_ge(prefix_ready, 1)
        each_step(act, copy)


def scatter_records(nc, block, ctx, n, records, slot_i, record, moved):
    slots = ctx.enter_context(nc.sbuf_tensor(f"{n}_slots", [EP, NQ, QUAD], I32))
    rows = ctx.enter_context(nc.sbuf_tensor(f"{n}_rows", [EP, NQ, QUAD, record.shape[2]], record.dtype))
    staged = ctx.enter_context(nc.semaphore(f"{n}_staged"))
    written = moved.sems
    passed = ctx.enter_context(nc.semaphore(f"{n}_passed_pool"))
    bodies = EC // BODY

    @block.gpsimd
    def _(pool):
        def stage(it, i, first):
            at = it * BODY + i * QUAD
            if not first:
                hold(pool, written[i], moved.after(it), passed)
            pool.tensor_copy(slots[:, i], slot_i[:, bass.ds(at, QUAD)])
            pool.tensor_copy(rows[:, i], record[:, bass.ds(at, QUAD), :]).then_inc(staged, 1)

        def body(it, first):
            stage(it, 0, first)
            for i in range(NQ):
                if i + 1 < NQ:
                    stage(it, i + 1, first)
                hold(pool, staged, it * NQ + i + 1, passed)
                for j in range(QUAD):
                    pool.indirect_dma_start(records, bass.IndirectOffsetOnAxis(ap=slots[:, i, j:j + 1], axis=0),
                                            rows[:, i, j], None).then_inc(written[i], 16)

        body(0, True)
        with pool.Fori(1, bodies, 1) as it:
            body(it, False)
        for i in range(NQ):
            pool.wait_ge(written[i], moved.after(bodies))

    moved.end(bodies)


def fetch_records(nc, block, ctx, o):
    got = ctx.enter_context(nc.sbuf_tensor("dst_got", [P, T, 4], F32))
    fetched = ctx.enter_context(nc.semaphore("dst_fetched"))

    @block.sync
    def _(sp):
        sp.dma_start(got[:, :, :], o.records.rearrange("(p t) c -> p t c", p=P)).then_inc(fetched, 16)

    @block.vector
    def _(dve):
        dve.wait_ge(fetched, 16)
        dve.tensor_copy(o.other[:, :], got[:, :, 0])
        dve.tensor_copy(o.low[:, :], got[:, :, 1])
        dve.tensor_copy(o.kind[:, :], got[:, :, 2])
        dve.tensor_copy(o.key[:, :], got[:, :, 3])


class Phase:

    def __init__(self, nc, ctx, name):
        self.nc, self.ctx, self.name = nc, ctx, name

    def sb(self, name, shape, dt=F32):
        return self.ctx.enter_context(self.nc.sbuf_tensor(f"{self.name}_{name}", shape, dt))

    def ps(self, name, shape, dt=F32):
        return self.ctx.enter_context(self.nc.psum_tensor(f"{self.name}_{name}", shape, dt))

    def sem(self, name):
        return self.ctx.enter_context(self.nc.semaphore(f"{self.name}_{name}"))


class Consts:
    pass


def make_consts(nc, ctx, sb):
    k = Consts()
    k.iota_t = sb("iota_t", [P, TP], F32)
    k.iota_q = sb("iota_q", [P, 2 * P, QUAD], BF16)
    k.ident = sb("ident", [P, P], F32)
    k.ident_b = sb("ident_b", [P, P], BF16)
    k.ones = sb("ones", [P, P], F32)
    k.one_b = sb("one_b", [P, 1], BF16)
    k.earlier = sb("earlier", [P, P], F32)
    return k


class Keys:

    def __init__(self, nc, ctx):
        def sb(name, shape, dt):
            return ctx.enter_context(nc.sbuf_tensor(name, shape, dt))
        self.src_low, self.src_high, self.dst_low, self.dst_high, self.dst_kind = (
            sb(n, [EP, EC], BF16) for n in ("key_src_low", "key_src_high", "key_dst_low", "key_dst_high", "key_dst_kind"))
        self.record = sb("record", [EP, EC, 4], F32)
        self.pair = sb("pair_record", [EP, EC, 2], BF16)
        self.slot_d = sb("slot_d", [EP, EC], I32)
        self.slot_p = sb("slot_p", [EP, EC], I32)


def setup(nc, ctx, k, e, A, records, pair_records):
    f = Phase(nc, ctx, "setup")
    iota_i = f.sb("iota_i", [P, TP], I32)
    filler = f.sb("filler", [P, T, 4])
    pair_filler = f.sb("pair_filler", [P, TP, 2], BF16)
    src_i, dst_i, kind_i, low_i, high_i = (f.sb(n, [EP, EC], I32) for n in ("src", "dst", "kind", "low", "high"))
    kind_f = f.sb("kind_f", [EP, EC])
    (loaded, pool_step, iota_ready, cleared, filler_ready, filled, step) = (f.sem(n) for n in (
        "loaded", "pool_step", "iota_ready", "cleared", "filler_ready", "filled", "step"))
    with nc.Block() as block:
        @block.sync
        def _(sp):
            for t, name in ((src_i, "src"), (dst_i, "dst"), (kind_i, "edge_type_8")):
                sp.dma_start(t[:, :], A[name].rearrange("(p t) -> p t", p=EP)).then_inc(loaded, 16)

        @block.scalar
        def _(act):
            act.wait_ge(filler_ready, 2)
            act.dma_start(records.rearrange("(p t) c -> p t c", p=P), filler[:, :, :]).then_inc(filled, 16)
            act.dma_start(pair_records.rearrange("(p t) c -> p t c", p=P), pair_filler[:, :, :]).then_inc(filled, 16)
            act.wait_ge(filled, 32)

        @block.gpsimd
        def _(pool):
            pool.iota(iota_i[:, :], [[1, TP]], base=0, channel_multiplier=0).then_inc(iota_ready, 1)
            pool.memset(k.ones[:, :], 1.0)
            pool.memset(k.one_b[:, :], 1.0)
            pool.memset(k.earlier[:, :], 1.0).then_inc(pool_step, 1)
            pool.memset(k.ident[:, :], 0.0).then_inc(pool_step, 1)
            pool.wait_ge(pool_step, 2)
            pool.affine_select(out=k.earlier[:, :], in_=k.earlier[:, :], compare_op=ALU.is_gt, fill=0.0,
                               base=0, pattern=[[1, P]], channel_multiplier=-1)
            pool.affine_select(out=k.ident[:, :], in_=k.ident[:, :], compare_op=ALU.not_equal, fill=1.0,
                               base=0, pattern=[[1, P]], channel_multiplier=-1).then_inc(pool_step, 1)

        @block.vector
        def _(dve):
            ch = Chain(dve, step)
            dve.memset(filler[:, :, :], 0.0).then_inc(cleared, 1)
            dve.memset(pair_filler[:, :, :], -1.0).then_inc(filler_ready, 1)
            dve.wait_ge(cleared, 1)
            dve.memset(filler[:, :, 1:2], -1.0).then_inc(filler_ready, 1)
            dve.wait_ge(iota_ready, 1)
            dve.tensor_copy(k.iota_t[:, :], iota_i[:, :])
            dve.tensor_copy(k.iota_q[:, :, :], spread(iota_i[:, 0:2 * P], [P, 2 * P, QUAD]))
            dve.wait_ge(pool_step, 3)
            dve.tensor_copy(k.ident_b[:, :], k.ident[:, :])
            dve.wait_ge(loaded, 48)
            for key, low, high, place in ((src_i, e.src_low, e.src_high, 0), (dst_i, e.dst_low, e.dst_high, 1)):
                dve.tensor_scalar(low_i[:, :], key[:, :], P - 1, None, ALU.bitwise_and)
                ch.done(dve.tensor_scalar(high_i[:, :], key[:, :], 7, None, ALU.logical_shift_right))
                dve.tensor_copy(low[:, :], low_i[:, :])
                dve.tensor_copy(e.pair[:, :, place], low_i[:, :])
                ch.done(dve.tensor_copy(high[:, :], high_i[:, :]))
            dve.tensor_copy(e.record[:, :, 0], src_i[:, :])
            dve.tensor_copy(e.record[:, :, 1], low_i[:, :])
            dve.tensor_copy(e.record[:, :, 2], kind_i[:, :])
            dve.tensor_scalar(e.record[:, :, 3], dst_i[:, :], 1.0, None, ALU.add)
            ch.done(dve.tensor_copy(kind_f[:, :], kind_i[:, :]))
            dve.scalar_tensor_tensor(e.dst_kind[:, :], high_i[:, :], float(NREL), kind_f[:, :], ALU.mult, ALU.add)


def blocks(t, width=C):
    return t[:, 0:NB * width].rearrange("p (b c) -> p b c", b=NB)


def inverse_root(dve, ch, y, a, t):
    ch.done(dve.reciprocal(y, y))
    ch.done(dve.tensor_tensor(t, y, y, ALU.mult))
    ch.done(dve.tensor_tensor(t, t, a, ALU.mult))
    ch.done(dve.tensor_scalar(t, t, -0.5, 1.5, ALU.mult, ALU.add))
    ch.done(dve.tensor_tensor(y, y, t, ALU.mult))


def degrees(nc, count_d, count_s, root_d, root_s, mean_d):
    with ExitStack() as ctx, nc.Block() as block:
        f = Phase(nc, ctx, "deg")
        a = f.sb("a", [P, 2, NB])
        y = f.sb("y", [P, 2, NB])
        t = f.sb("t", [P, 2, NB])
        step, added, rooted = f.sem("step"), f.sem("added"), f.sem("rooted")

        @block.vector
        def _(dve):
            ch = Chain(dve, step)
            dve.tensor_scalar(a[:, 0], count_d[:, :], 1.0, None, ALU.add)
            dve.tensor_scalar(a[:, 1], count_s[:, :], 1.0, None, ALU.add).then_inc(added, 1)
            ch.done(dve.tensor_scalar(mean_d[:, :], count_d[:, :], 1.0, None, ALU.max))
            ch.done(dve.reciprocal(mean_d[:, :], mean_d[:, :]))
            dve.wait_ge(rooted, 1)
            inverse_root(dve, ch, y[:, :, :], a[:, :, :], t[:, :, :])
            dve.tensor_copy(root_d[:, :], y[:, 0])
            dve.tensor_copy(root_s[:, :], y[:, 1])

        @block.scalar
        def _(act):
            act.wait_ge(added, 1)
            act.activation(y[:, :, :], a[:, :, :], ACT.Sqrt).then_inc(rooted, 1)


def norm_relu(nc, name, src, dst, scale=None):
    with ExitStack() as ctx, nc.Block() as block:
        f = Phase(nc, ctx, name)
        stats = f.sb("stats", [P, NB, 6])
        moments = f.sb("moments", [P, NB, 2])
        a, y, t, shift = (f.sb(n, [P, NB]) for n in ("a", "y", "t", "shift"))
        step, var_ready, rooted, ready = (f.sem(n) for n in ("step", "var_ready", "rooted", "ready"))
        s3, d3 = blocks(src), blocks(dst)
        mine = range(0, NB, 2)

        @block.vector
        def _(dve):
            ch = Chain(dve, step)
            for b in range(NB):
                last = dve.bn_stats(stats[:, b], s3[:, b])
            ch.done(last)
            for b in range(NB):
                last = dve.bn_aggr(moments[:, b], stats[:, b])
            ch.done(last)
            dve.tensor_scalar(a[:, :], moments[:, :, 1], LN_EPS, None, ALU.add).then_inc(var_ready, 1)
            dve.wait_ge(rooted, 1)
            inverse_root(dve, ch, y[:, :], a[:, :], t[:, :])
            if scale is not None:
                ch.done(dve.tensor_tensor(y[:, :], y[:, :], scale[:, :], ALU.mult))
            dve.scalar_tensor_tensor(shift[:, :], moments[:, :, 0], -1.0, y[:, :], ALU.mult, ALU.mult).then_inc(ready, 1)
            for b in mine:
                last = dve.tensor_scalar(d3[:, b], s3[:, b], moments[:, b, 0:1], y[:, b:b + 1], ALU.subtract, ALU.mult)
            ch.done(last)
            for b in mine:
                dve.tensor_scalar(d3[:, b], d3[:, b], 0.0, None, ALU.max)

        @block.scalar
        def _(act):
            act.wait_ge(var_ready, 1)
            act.activation(y[:, :], a[:, :], ACT.Sqrt).then_inc(rooted, 1)
            act.wait_ge(ready, 1)
            for b in range(NB):
                if b not in mine:
                    act.activation(d3[:, b], s3[:, b], ACT.Relu, bias=shift[:, b:b + 1], scale=y[:, b:b + 1])


DB = 5


ADD = "add"


def scalar_bodies(act, finish, steps):
    def body(it, first):
        for j in range(DB):
            if j == 2 and not first:
                finish.scalar(act, it - 1)
            steps(it, j)

    body(0, True)
    with act.Fori(1, NB // DB, 1) as it:
        body(it, False)
    finish.scalar(act, NB // DB - 1)


def free_bank(it, j, banks):
    if j >= banks:
        return it * DB + (DB + j - banks + 1)
    return it * DB + (max(i for i in range(DB) if i % banks == j) + 1)


def of_body(t, it, width=C):
    return t[:, bass.ds(it * (DB * width), DB * width)].rearrange("p (b c) -> p b c", b=DB)


def per_row(t, it, width=C):
    return spread(t[:, bass.ds(it * DB, DB)], [P, DB, width])


class BodyNorm:

    STEPS = 9

    def __init__(self, f, name):
        self.stats = f.sb(f"{name}_stats", [P, DB, 6])
        self.moments = f.sb(f"{name}_moments", [P, DB, 2])
        self.a, self.y, self.t = (f.sb(f"{name}_{n}", [P, DB]) for n in ("a", "y", "t"))
        self.var_ready, self.rooted = f.sem(f"{name}_var_ready"), f.sem(f"{name}_rooted")

    def vector(self, dve, ch, it, z):
        for j in range(DB):
            last = dve.bn_stats(self.stats[:, j], z[:, j])
        ch.done(last)
        for j in range(DB):
            last = dve.bn_aggr(self.moments[:, j], self.stats[:, j])
        ch.done(last)
        ch.done(dve.tensor_scalar(self.a[:, :], self.moments[:, :, 1], LN_EPS, None, ALU.add))
        dve.sem_inc(self.var_ready, 1)
        hold(dve, self.rooted, it + 1, ch.passed)
        inverse_root(dve, ch, self.y[:, :], self.a[:, :], self.t[:, :])
        for j in range(DB):
            last = dve.tensor_scalar(z[:, j], z[:, j], self.moments[:, j, 0:1], self.y[:, j:j + 1],
                                     ALU.subtract, ALU.mult)
        ch.done(last)

    def scalar(self, act, it):
        act.wait_ge(self.var_ready, it + 1)
        act.activation(self.y[:, :], self.a[:, :], ACT.Sqrt).then_inc(self.rooted, 1)


def dense(nc, name, k, src, kc, nout, weight_loads, outs, finish=None, stores=()):
    with ExitStack() as ctx, nc.Block() as block:
        f = Phase(nc, ctx, name)
        if finish is not None:
            finish.place(f)
        w = f.sb("w", [P, kc, nout])
        staged_rows = f.sb("staged_rows", [P, DB, kc * P])
        rows_t = f.sb("rows_t", [P, DB, kc, P])
        turn = [f.ps(f"turn{s}", [P, kc, P]) for s in range(2)]
        banks = 4 if nout <= 512 else 2
        prod = [f.ps(f"prod{s}", [P, nout]) for s in range(banks)]
        stored = f.sem("stored")
        loaded, staged, turned, turned_copied, product, copied, passed_act, passed_dve = (f.sem(n) for n in (
            "loaded", "staged", "turned", "turned_copied", "product", "copied", "passed_act", "passed_dve"))
        loads = weight_loads(w)

        @block.sync
        def _(sp):
            for dst, s in loads:
                sp.dma_start(dst, s).then_inc(loaded, 16)
            if not stores:
                return
            with sp.Fori(0, NB // DB, 1) as it:
                sp.wait_ge(copied, it * DB + 2 * DB)
                for src, width, table in stores:
                    sp.dma_start(table.rearrange("(b p) c -> p b c", p=P)[:, bass.ds(it * DB, DB)],
                                 of_body(src, it, width)).then_inc(stored, 16)
            sp.wait_ge(stored, 16 * len(stores) * (NB // DB))

        @block.scalar
        def _(act):
            def steps(it, j):
                if j == 0:
                    act.copy(staged_rows[:, :, :].rearrange("p j c -> p (j c)"),
                             src[:, bass.ds(it * (DB * kc * P), DB * kc * P)]).then_inc(staged, 1)
                act.wait_ge(turned, it * DB + j + 1)
                act.copy(rows_t[:, j], turn[j % 2][:, :, :]).then_inc(turned_copied, 1)

            scalar_bodies(act, finish or Finish(), steps)

        @block.tensor
        def _(pe):
            pe.wait_ge(loaded, 16 * len(loads))

            def product_of(it, j):
                pe.wait_ge(turned_copied, it * DB + j + 1)
                pe.wait_ge(copied, free_bank(it, j, banks))
                for c0 in range(0, nout, 512):
                    c1 = min(c0 + 512, nout)
                    for c in range(kc):
                        last = pe.matmul(prod[j % banks][:, c0:c1], rows_t[:, j, c], w[:, c, c0:c1],
                                         start=(c == 0), stop=(c == kc - 1))
                last.then_inc(product, 1)

            with pe.Fori(0, NB // DB, 1) as it:
                pe.wait_ge(staged, it + 1)
                for j in range(DB):
                    for c in range(kc):
                        last = pe.transpose(turn[j % 2][:, c], staged_rows[:, j, c * P:(c + 1) * P], k.ident[:, :])
                    last.then_inc(turned, 1)
                    if j > 0:
                        product_of(it, j - 1)
                product_of(it, DB - 1)

        @block.vector
        def _(dve):
            dve.sem_inc(copied, DB)
            with dve.Fori(0, NB // DB, 1) as it:
                for j in range(DB):
                    hold(dve, product, it * DB + j + 1, passed_dve)
                    for c0, width, dst, bias in outs:
                        for a in range(c0, c0 + width, 512):
                            n = min(512, c0 + width - a)
                            if dst is None:
                                to = finish.z[:, j, a - c0:a - c0 + n]
                            else:
                                to = dst[:, bass.ds((it * DB + j) * width + (a - c0), n)]
                            if bias is ADD:
                                last = dve.tensor_tensor(to, prod[j % banks][:, a:a + n], to, ALU.add)
                            elif bias is None:
                                last = dve.tensor_copy(to, prod[j % banks][:, a:a + n])
                            else:
                                last = dve.tensor_tensor(to, prod[j % banks][:, a:a + n], bias[:, a - c0:a - c0 + n], ALU.add)
                    last.then_inc(copied, 1)
                if finish is not None:
                    dve.wait_ge(copied, it * DB + 2 * DB)
                    finish.vector(dve, it)


def whole(weight):
    return lambda w: [(w[:, :, :], weight.rearrange("(k p) n -> p k n", p=P))]


def gather_rows(f, block, index, table, rows, width, landed, used):
    slots = f.sb("slots", [P, NQ, QUAD], I32)
    staged = f.sem("staged")
    passed = f.sem("passed_pool")

    @block.gpsimd
    def _(pool):
        with pool.Fori(0, T // BODY, 1) as it:
            def stage(i):
                hold(pool, used, it * BODY + (i + 1) * QUAD, passed)
                pool.tensor_copy(slots[:, i], index[:, bass.ds(it * BODY + i * QUAD, QUAD)]).then_inc(staged, 1)

            stage(0)
            for i in range(NQ):
                hold(pool, staged, it * NQ + i + 1, passed)
                for j in range(QUAD):
                    if j == 2 and i + 1 < NQ:
                        stage(i + 1)
                    pool.indirect_dma_start(rows[:, i * QUAD + j, 0:width], None, table,
                                            bass.IndirectOffsetOnAxis(ap=slots[:, i, j:j + 1], axis=0))\
                        .then_inc(landed[i], 16)


def select_matrix(dve, k, o, sel, it, s):
    return dve.tensor_tensor(sel[:, s * HALF:(s + 1) * HALF], repeat(k.iota_t[:, 0:P], [P, HALF, P]),
                             spread(o.low[:, bass.ds(it * BODY + s * HALF, HALF)], [P, HALF, P]), ALU.is_equal)


def select_kind(dve, k, o, out, it, s):
    return dve.tensor_tensor(out, repeat(k.iota_t[:, 0:NREL], [P, HALF, NREL]),
                             spread(o.kind[:, bass.ds(it * BODY + s * HALF, HALF)], [P, HALF, NREL]), ALU.is_equal)


def add_tiles(nc, dve, o, accs, width, bank, it, first, n, done, done_start, added, lead):
    regs = block_numbers(nc, DVE_ENGINE, o.block, it * BODY + first, n)
    for i in range(n):
        tile = it * BODY + first + i
        dve.wait_ge(done, tile + done_start + 1)
        dve.wait_ge(added, tile + lead - 1)
        to = accs[i % 2][:, bass.ds(regs[i] * width, width)]
        dve.tensor_tensor(to, bank(first + i)[:, 0:width], to, ALU.add).then_inc(added, 1)


STREAM = TP // 2
assert STREAM > -(-E // P)


def build_adjacency(nc, block, ctx, k, places, tile_pair, adj):
    f = Phase(nc, ctx, "adj")
    onehot = f.sb("onehot", [P, 2, 2, 2, P, QUAD], BF16)
    bank = [[f.ps(f"count{s}{u}", [P, QUAD, P]) for u in range(2)] for s in range(2)]
    onehots, counted, added, cleared = f.sem("onehots"), f.sem("counted"), f.sem("added"), f.sem("cleared")

    @block.vector
    def _(dve):
        words = adj[:, :].bitcast(F32)
        dve.memset(words, 0.0).then_inc(cleared, 1)
        dve.sem_inc(added, 4 * QUAD)
        dve.wait_ge(cleared, 1)

        def compare(it, s):
            for u in range(2):
                for place in range(2):
                    last = onehots_of(dve, k, onehot[:, s, u, place:place + 1], places[:, place],
                                      it * (2 * QUAD) + (s * QUAD + u * STREAM), P)
            last.then_inc(onehots, 1)

        with dve.Fori(0, STREAM // (2 * QUAD), 1) as it:
            pairs = []
            for s in range(2):
                compare(it, s)
                pairs.append([nc.values_load_multi_w_load_instructions(
                    tile_pair[0:1, bass.ds(it * (2 * QUAD) + (s * QUAD + u * STREAM), QUAD)], engines=(DVE_ENGINE,),
                    min_val=0, max_val=NB * NB * P,
                    skip_runtime_bounds_check_because="P times counts of pairs of blocks, less one, cut to NB * NB")[1]
                    for u in range(2)])
            for s in range(2):
                dve.wait_ge(counted, it * 2 + s + 1)
                for j in range(QUAD):
                    for u in range(2):
                        dve.wait_ge(added, it * (4 * QUAD) + s * (2 * QUAD) + 2 * j + u + 4 * QUAD - 1)
                        to = adj[:, bass.ds(pairs[s][u][j], P)]
                        dve.tensor_tensor(to, bank[s][u][:, j], to, ALU.add).then_inc(added, 1)

    @block.tensor
    def _(pe):
        with pe.Fori(0, STREAM // (2 * QUAD), 1) as it:
            for s in range(2):
                pe.wait_ge(onehots, it * 2 + s + 1)
                pe.wait_ge(added, it * (4 * QUAD) + (s + 1) * (2 * QUAD))
                for u in range(2):
                    for j in range(QUAD):
                        last = pe.matmul(bank[s][u][:, j], onehot[:, s, u, 0, :, j], onehot[:, s, u, 1, :, j],
                                         start=True, stop=True)
                last.then_inc(counted, 1)


def store_adjacency(nc, adj, adj_dram):
    with ExitStack() as ctx, nc.Block() as block:
        stored = Phase(nc, ctx, "adj_store").sem("stored")

        @block.sync
        def _(sp):
            for b in range(0, NB, DB):
                sp.dma_start(adj_dram[b:b + DB].rearrange("b p n -> p b n"),
                             adj[:, b * NPAD:(b + DB) * NPAD].rearrange("p (b n) -> p b n", b=DB)).then_inc(stored, 16)
            sp.wait_ge(stored, 16 * (NB // DB))


CH = 5
SHARED_FROM = 2


def neighbour_sums(nc, name, k, adj_dram, g, finish, loops=True, turned=False):
    with ExitStack() as ctx, nc.Block() as block:
        f = Phase(nc, ctx, name)
        finish.place(f)
        slab = f.sb("slab", [P, DB, NB, P], U16)
        count = f.sb("count", [P, CH, CH, P])
        count_t = f.sb("count_t", [P, CH, CH, P]) if turned else count
        banks = 4
        bank = [f.ps(f"sum{s}", [P, 512]) for s in range(banks)]
        turn = [f.ps(f"turn{s}", [P, 8, P]) for s in range(2)] if turned else []
        landed = [f.sem(f"landed{j}") for j in range(DB)]
        widened, summed, taken, passed_sp, passed_pool, flipped, flipped_copied = (f.sem(n) for n in (
            "widened", "summed", "taken", "passed_sp", "passed_pool", "flipped", "flipped_copied"))
        chunks = NB // CH
        widened_act, passed_act = f.sem("widened_act"), f.sem("passed_act")

        def by_act(j, c):
            return not turned and j >= SHARED_FROM and c == chunks - 1

        def before(j, c):
            return sum(not by_act(a, b) for a in range(DB) for b in range(chunks) if (a, b) < (j, c))

        per_body = before(DB, 0)

        @block.sync
        def _(sp):
            with sp.Fori(0, NB // DB, 1) as it:
                for j in range(DB):
                    hold(sp, widened, it * per_body + before(j + 1, 0), passed_sp)
                    if by_act(j, chunks - 1):
                        sp.wait_ge(widened_act, it * (DB - SHARED_FROM) + (j - SHARED_FROM + 1))
                    if turned:
                        src = adj_dram[:, :, bass.ds((it * DB + j) * P, P)].rearrange("b p n -> p b n")
                    else:
                        src = adj_dram[bass.ds(it * DB + j, 1)].rearrange("o p (b n) -> p (o b) n", n=P)
                    sp.dma_start(slab[:, j], src).then_inc(landed[j], 16)

        @block.gpsimd
        def _(pool):
            pool.sem_inc(widened, per_body)
            pool.sem_inc(widened_act, DB - SHARED_FROM)
            with pool.Fori(0, NB // DB, 1) as it:
                for j in range(DB):
                    pool.wait_ge(landed[j], it * 16 + 16)
                    for c in range(chunks):
                        if by_act(j, c):
                            continue
                        hold(pool, flipped if turned else summed, (it * DB + j) * chunks + c + 1, passed_pool)
                        pool.tensor_copy(count[:, c], slab[:, j, c * CH:(c + 1) * CH]).then_inc(widened, 1)

        @block.tensor
        def _(pe):
            pe.sem_inc(summed, chunks)
            pe.sem_inc(flipped, chunks)
            with pe.Fori(0, NB // DB, 1) as it:
                def flip(i):
                    pe.wait_ge(widened, it * per_body + (i + per_body + 1))
                    for b in range(CH):
                        last = pe.transpose(turn[i % 2][:, b], count[:, i % chunks, b], k.ident[:, :])
                    last.then_inc(flipped, 1)

                if turned:
                    flip(0)
                for j in range(DB):
                    pe.wait_ge(taken, free_bank(it, j, banks))
                    for c in range(chunks):
                        n = (it * DB + j) * chunks + c
                        if turned:
                            if j * chunks + c + 1 < DB * chunks:
                                flip(j * chunks + c + 1)
                            pe.wait_ge(flipped_copied, n + 1)
                        else:
                            if by_act(j, c):
                                pe.wait_ge(widened_act, it * (DB - SHARED_FROM) + (j + DB - 2 * SHARED_FROM + 1))
                            else:
                                pe.wait_ge(widened, it * per_body + (per_body + before(j, c) + 1))
                        for b in range(CH):
                            last = pe.matmul(bank[j % banks][:, 0:C], count_t[:, c, b], g[:, (c * CH + b) * C:(c * CH + b + 1) * C],
                                             start=(c == 0 and b == 0), stop=(c == chunks - 1 and b == CH - 1))
                        last.then_inc(summed, 1)

        @block.scalar
        def _(act):
            def steps(it, j):
                if turned:
                    for c in range(chunks):
                        n = (it * DB + j) * chunks + c
                        act.wait_ge(summed, n + 1)
                        act.wait_ge(flipped, n + chunks + 1)
                        act.copy(count_t[:, c], turn[(j * chunks + c) % 2][:, 0:CH]).then_inc(flipped_copied, 1)
                elif by_act(j, chunks - 1):
                    c = chunks - 1
                    hold(act, landed[j], it * 16 + 16, passed_act)
                    act.wait_ge(summed, (it * DB + j) * chunks + c + 1)
                    act.copy(count[:, c], slab[:, j, c * CH:(c + 1) * CH]).then_inc(widened_act, 1)

            scalar_bodies(act, finish, steps)

        @block.vector
        def _(dve):
            dve.sem_inc(taken, DB)
            with dve.Fori(0, NB // DB, 1) as it:
                for j in range(DB):
                    dve.wait_ge(summed, (it * DB + j + 1) * chunks + chunks)
                    if loops:
                        dve.tensor_tensor(finish.z[:, j], bank[j % banks][:, 0:C], g[:, bass.ds((it * DB + j) * C, C)],
                                          ALU.add).then_inc(taken, 1)
                    else:
                        dve.tensor_copy(finish.z[:, j], bank[j % banks][:, 0:C]).then_inc(taken, 1)
                dve.wait_ge(taken, it * DB + 2 * DB)
                finish.vector(dve, it)


class Finish:

    STEPS = 0
    WIDTH = C

    def place(self, f):
        self.z = f.sb("z", [P, DB, self.WIDTH])
        self.step = f.sem("finish_step")
        self.passed = f.sem("passed_finish")
        self.place_more(f)

    def place_more(self, f):
        pass

    def vector(self, dve, it):
        ch = LoopChain(dve, self.step, it, self.STEPS, self.passed)
        self.steps(dve, ch, it, self.z[:, :, :])
        ch.end()

    def scalar(self, act, it):
        pass


class Scaled(Finish):

    STEPS = 1

    def __init__(self, scale, out):
        self.scale, self.out = scale, out

    def steps(self, dve, ch, it, z):
        ch.done(dve.tensor_tensor(of_body(self.out, it), z, per_row(self.scale, it), ALU.mult))


class HiddenNorm(Finish):

    WIDTH = CW
    STEPS = BodyNorm.STEPS + 3

    def __init__(self, gamma, beta, scale, out):
        self.gamma, self.beta, self.scale, self.out = gamma, beta, scale, out

    def place_more(self, f):
        self.norm = BodyNorm(f, "norm")

    def steps(self, dve, ch, it, z):
        full = [P, DB, CW]
        self.norm.vector(dve, ch, it, z)
        ch.done(dve.tensor_tensor(z, z, repeat(self.gamma[:, :], full), ALU.mult))
        ch.done(dve.tensor_tensor(z, z, repeat(self.beta[:, :], full), ALU.add))
        ch.done(dve.scalar_tensor_tensor(of_body(self.out, it, CW), z, 0.0, per_row(self.scale, it, CW),
                                         ALU.max, ALU.mult))

    def scalar(self, act, it):
        self.norm.scalar(act, it)


class ToStream(Finish):

    def __init__(self, scale, x, own=None, out=None, out_scale=None):
        self.scale, self.x, self.own, self.out, self.out_scale = scale, x, own, out, out_scale
        self.STEPS = 3
        if own is not None:
            self.STEPS += 1 + BodyNorm.STEPS + 2
        if out is not None:
            self.STEPS += BodyNorm.STEPS

    def place_more(self, f):
        if self.own is not None:
            self.own_norm = BodyNorm(f, "own")
        if self.out is not None:
            self.next_norm = BodyNorm(f, "next")

    def steps(self, dve, ch, it, z):
        full = [P, DB, C]
        x = of_body(self.x, it)
        ch.done(dve.tensor_tensor(z, z, per_row(self.scale, it), ALU.mult))
        if self.own is not None:
            bias, gamma, beta = self.own
            ch.done(dve.tensor_tensor(z, z, repeat(bias[:, :], full), ALU.add))
            self.own_norm.vector(dve, ch, it, z)
            ch.done(dve.tensor_tensor(z, z, repeat(gamma[:, :], full), ALU.mult))
            ch.done(dve.tensor_tensor(z, z, repeat(beta[:, :], full), ALU.add))
            ch.done(dve.scalar_tensor_tensor(z, z, 0.0, x, ALU.max, ALU.add))
        else:
            ch.done(dve.tensor_tensor(z, z, x, ALU.add))
        last = dve.tensor_scalar(x, z, 1.0, None, ALU.mult)
        if self.out is None:
            ch.done(last)
            return
        self.next_norm.vector(dve, ch, it, z)
        out = of_body(self.out, it)
        if self.out_scale is None:
            ch.done(dve.tensor_scalar(out, z, 0.0, None, ALU.max))
        else:
            ch.done(dve.scalar_tensor_tensor(out, z, 0.0, per_row(self.out_scale, it), ALU.max, ALU.mult))

    def scalar(self, act, it):
        if self.own is not None:
            self.own_norm.scalar(act, it)
        if self.out is not None:
            self.next_norm.scalar(act, it)


def turn_select(pe, k, turn, sel, first, n):
    for i in range(n):
        last = pe.transpose(turn[:, i], sel[:, first + i], k.ident[:, :])
    return last


def aggregate_kinds(nc, name, k, moved, o, index, table, share, accs):
    with ExitStack() as ctx, nc.Block() as block:
        f = Phase(nc, ctx, name)
        rows = f.sb("rows", [P, BODY, H1])
        sel = f.sb("sel", [P, BODY, P])
        sel_t = f.sb("sel_t", [P, BODY, P])
        kinds = f.sb("kinds", [P, BODY, NREL])
        part = f.sb("part", [P, BODY, NREL])
        weight = f.sb("weight", [P, BODY])
        turn = [f.ps(f"turn{s}", [P, QUAD, P]) for s in range(2)]
        share_ps = [f.ps(f"share{s}", [P, QUAD, NREL]) for s in range(2)]
        bank = [f.ps(f"sum{j}", [P, 512]) for j in range(4)]
        landed = moved.sems
        (sel_ready, turned, turned_copied, shares, parted, weighed, scaled, tile_done, added) = (
            f.sem(n) for n in ("sel_ready", "turned", "turned_copied", "shares", "parted", "weighed",
                               "scaled", "tile_done", "added"))

        gather_rows(f, block, index, table, rows, H1, landed, tile_done)

        @block.vector
        def _(dve):
            dve.sem_inc(added, 4)

            def weigh(it, i):
                n = it * NQ + i + 1
                quad = slice(i * QUAD, (i + 1) * QUAD)
                dve.wait_ge(shares, n)
                dve.tensor_tensor(part[:, quad], share_ps[i % 2][:, :, :], kinds[:, quad], ALU.mult).then_inc(parted, 1)
                dve.wait_ge(parted, n)
                dve.tensor_reduce(weight[:, quad], part[:, quad], AX, ALU.add).then_inc(weighed, 1)
                dve.wait_ge(weighed, n)
                dve.wait_ge(landed[i], moved.after(it + 1))
                dve.tensor_tensor(rows[:, quad], rows[:, quad], spread(weight[:, quad], [P, QUAD, H1]),
                                  ALU.mult).then_inc(scaled, 1)

            def add(it, i):
                add_tiles(nc, dve, o, accs, H1, lambda j: bank[j % 4], it, i * QUAD, QUAD, tile_done, BODY, added, 4)

            with dve.Fori(0, T // BODY, 1) as it:
                for s in range(2):
                    select_kind(dve, k, o, kinds[:, s * HALF:(s + 1) * HALF], it, s)
                    select_matrix(dve, k, o, sel, it, s).then_inc(sel_ready, 1)
                weigh(it, 0)
                for i in range(1, NQ):
                    weigh(it, i)
                    add(it, i - 1)
                add(it, NQ - 1)

        @block.scalar
        def _(act):
            with act.Fori(0, T // BODY, 1) as it:
                for i in range(NQ):
                    act.wait_ge(turned, it * NQ + i + 1)
                    act.copy(sel_t[:, i * QUAD:(i + 1) * QUAD], turn[i % 2][:, :, :]).then_inc(turned_copied, 1)

        @block.tensor
        def _(pe):
            pe.sem_inc(tile_done, BODY)

            def flip(it, i):
                if i % 2 == 0:
                    pe.wait_ge(sel_ready, it * 2 + i // 2 + 1)
                turn_select(pe, k, turn[i % 2], sel, i * QUAD, QUAD).then_inc(turned, 1)

            def look_up(it, i):
                regs = block_numbers(nc, PE_ENGINE, o.block, it * BODY + i * QUAD, QUAD)
                pe.wait_ge(turned_copied, it * NQ + i + 1)
                for j in range(QUAD):
                    last = pe.matmul(share_ps[i % 2][:, j], sel_t[:, i * QUAD + j],
                                     share[:, bass.ds(regs[j] * NREL, NREL)], start=True, stop=True)
                last.then_inc(shares, 1)

            def add_up(it, i):
                pe.wait_ge(scaled, it * NQ + i + 1)
                for j in range(i * QUAD, (i + 1) * QUAD):
                    pe.wait_ge(added, it * BODY + j + 1)
                    pe.matmul(bank[j % 4][:, 0:H1], sel[:, j], rows[:, j], start=True, stop=True)\
                      .then_inc(tile_done, 1)

            with pe.Fori(0, T // BODY, 1) as it:
                flip(it, 0)
                flip(it, 1)
                look_up(it, 0)
                look_up(it, 1)
                for i in range(2, NQ):
                    flip(it, i)
                    add_up(it, i - 2)
                    look_up(it, i)
                add_up(it, NQ - 2)
                add_up(it, NQ - 1)

    moved.end(T // BODY)


def by_tile(t):
    return t[:, :].rearrange("p (h t) -> p t h", h=HEADS)


def edge_scores(nc, name, k, moved, o, table_k, q, scores):
    with ExitStack() as ctx, nc.Block() as block:
        f = Phase(nc, ctx, name)
        scores = by_tile(scores)
        rows = f.sb("rows", [P, BODY, C])
        sel = f.sb("sel", [P, BODY, P])
        sel_t = f.sb("sel_t", [P, 2, QUAD, P])
        turn = [f.ps(f"turn{s}", [P, QUAD, P]) for s in range(2)]
        q_ps = [[f.ps(f"q{s}{h}", [P, 2, C]) for h in range(2)] for s in range(2)]
        landed = moved.sems
        (sel_ready, turned, sel_t_ready, queries, multiplied, scored, passed_dve) = (f.sem(n) for n in (
            "sel_ready", "turned", "sel_t_ready", "queries", "multiplied", "scored", "passed_dve"))

        gather_rows(f, block, o.other, table_k, rows, C, landed, scored)

        @block.vector
        def _(dve):
            dve.sem_inc(scored, BODY)
            with dve.Fori(0, T // BODY, 1) as it:
                for s in range(2):
                    select_matrix(dve, k, o, sel, it, s).then_inc(sel_ready, 1)
                for i in range(NQ):
                    dve.wait_ge(landed[i], moved.after(it + 1))
                    dve.wait_ge(queries, it * NQ + i + 1)
                    for h in range(2):
                        j = i * QUAD + 2 * h
                        last = dve.tensor_tensor(rows[:, j:j + 2], rows[:, j:j + 2], q_ps[i % 2][h][:, :, :], ALU.mult)
                    last.then_inc(multiplied, 1)
                    hold(dve, multiplied, it * NQ + i + 1, passed_dve)
                    dve.tensor_reduce(scores[:, bass.ds(it * BODY + i * QUAD, QUAD), :],
                                      rows[:, i * QUAD:(i + 1) * QUAD].rearrange("p j (h d) -> p j h d", h=HEADS),
                                      AX, ALU.add).then_inc(scored, QUAD)

        @block.scalar
        def _(act):
            with act.Fori(0, T // BODY, 1) as it:
                for i in range(NQ):
                    act.wait_ge(turned, it * NQ + i + 1)
                    act.copy(sel_t[:, i % 2], turn[i % 2][:, :, :]).then_inc(sel_t_ready, 1)

        @block.tensor
        def _(pe):
            def flip(it, i):
                if i % 2 == 0:
                    pe.wait_ge(sel_ready, it * 2 + i // 2 + 1)
                turn_select(pe, k, turn[i % 2], sel, i * QUAD, QUAD).then_inc(turned, 1)

            with pe.Fori(0, T // BODY, 1) as it:
                flip(it, 0)
                for i in range(NQ):
                    if i + 1 < NQ:
                        flip(it, i + 1)
                    regs = block_numbers(nc, PE_ENGINE, o.block, it * BODY + i * QUAD, QUAD)
                    pe.wait_ge(sel_t_ready, it * NQ + i + 1)
                    pe.wait_ge(scored, it * BODY + i * QUAD + 3 * QUAD)
                    for t in range(QUAD):
                        last = pe.matmul(q_ps[i % 2][t // 2][:, t % 2], sel_t[:, i % 2, t], q[:, bass.ds(regs[t] * C, C)],
                                         start=True, stop=True)
                    last.then_inc(queries, 1)

    moved.end(T // BODY)


G = T * HEADS // P
LOW = 2.0 ** 126


def softmax_weights(nc, name, k, o, scores, ends_dram, carry_dram):
    with ExitStack() as ctx, nc.Block() as block:
        f = Phase(nc, ctx, name)
        N2 = G * P
        wide_key = f.sb("wide_key", [P, T * HEADS])
        st, kt, pen_f, pen_b, fwd, bwd, tmp = (f.sb(n, [P, N2]) for n in (
            "st", "kt", "pen_f", "pen_b", "fwd", "bwd", "tmp"))
        ends = f.sb("ends", [P, 4, G])
        ends_t = f.sb("ends_t", [4 * G, P])
        row = f.sb("row", [HEADS, 4, T])
        inner = f.sb("inner", [HEADS, T])
        joint = f.sb("joint", [HEADS, T + 1])
        go = f.sb("go", [HEADS, T])
        carried = f.sb("carried", [HEADS, T])
        carry = f.sb("carry", [HEADS, 2, T])
        carry_rows = f.sb("carry_rows", [2 * G, P])
        carry_t = f.sb("carry_t", [P, 2, G])
        bank = [f.ps(f"bank{i}", [P, 4, P]) for i in range(8)]
        (keys_ready, turned, copied, step, ends_ready, ends_turned, ends_copied, out_done, row_done, carry_ready,
         carry_out, carry_in, carry_turned, carry_copied, below, weights, turned_back) = (f.sem(n) for n in (
             "keys_ready", "turned", "copied", "step", "ends_ready", "ends_turned", "ends_copied", "out_done",
             "row_done", "carry_ready", "carry_out", "carry_in", "carry_turned", "carry_copied", "below",
             "weights", "turned_back"))

        def grouped(t):
            return t[:, :].rearrange("p (g e) -> p g e", g=G)

        @block.tensor
        def _(pe):
            for src, base in ((scores, 0), (wide_key, 4)):
                if base:
                    pe.wait_ge(keys_ready, 1)
                for g in range(G):
                    last = pe.transpose(bank[base + g // 4][:, g % 4], src[:, g * P:(g + 1) * P], k.ident[:, :])
                last.then_inc(turned, 1)
            pe.wait_ge(ends_ready, 1)
            pe.transpose(bank[0][0:4 * G, 0], ends[:, :, :].rearrange("p a g -> p (a g)"), k.ident[:, :])\
              .then_inc(ends_turned, 1)
            pe.wait_ge(carry_in, 16)
            pe.transpose(bank[1][:, 0, 0:2 * G], carry_rows[:, :], k.ident[0:2 * G, 0:2 * G]).then_inc(carry_turned, 1)
            pe.wait_ge(weights, 1)
            for g in range(G):
                last = pe.transpose(bank[g // 4][:, g % 4], st[:, g * P:(g + 1) * P], k.ident[:, :])
            last.then_inc(turned_back, 1)

        @block.scalar
        def _(act):
            for dst, base in ((st, 0), (kt, 4)):
                act.wait_ge(turned, 1 if base == 0 else 2)
                for b in range(0, G, 4):
                    n = min(4, G - b)
                    last = act.copy(grouped(dst)[:, b:b + n], bank[base + b // 4][:, 0:n])
                last.then_inc(copied, 1)
            act.wait_ge(ends_turned, 1)
            act.copy(ends_t[:, :], bank[0][0:4 * G, 0]).then_inc(ends_copied, 1)
            act.wait_ge(carry_turned, 1)
            act.copy(carry_t[:, :, :].rearrange("p a g -> p (a g)"), bank[1][:, 0, 0:2 * G]).then_inc(carry_copied, 1)
            act.wait_ge(below, 1)
            act.activation(st[:, :], tmp[:, :], ACT.Exp, scale=float(HD) ** -0.5).then_inc(weights, 1)
            act.wait_ge(turned_back, 1)
            for b in range(0, G, 4):
                n = min(4, G - b)
                act.copy(scores[:, b * P:(b + n) * P].rearrange("p (g e) -> p g e", g=n), bank[b // 4][:, 0:n])

        @block.vector
        def _(dve):
            ch = Chain(dve, step)
            dve.tensor_copy(wide_key[:, :].rearrange("p (h t) -> p h t", h=HEADS), repeat(o.key[:, :], [P, HEADS, T]))\
               .then_inc(keys_ready, 1)
            dve.wait_ge(copied, 2)
            for pen, lo, edge in ((pen_f, 1, 0), (pen_b, 0, P - 1)):
                ch.done(dve.tensor_tensor(pen[:, lo:lo + N2 - 1], kt[:, 1:N2], kt[:, 0:N2 - 1], ALU.is_equal))
                ch.done(dve.memset(grouped(pen)[:, :, edge:edge + 1], 0.0))
                ch.done(dve.tensor_scalar(pen[:, :], pen[:, :], LOW, -LOW, ALU.mult, ALU.add))
            dve.tensor_tensor_scan(fwd[:, :], pen_f[:, :], st[:, :], -LOW, ALU.add, ALU.max)
            ch.done(dve.tensor_tensor_scan(bwd[:, ::-1], pen_b[:, ::-1], st[:, ::-1], -LOW, ALU.add, ALU.max))
            for i, (t, e) in enumerate(((fwd, P - 1), (bwd, 0), (kt, 0), (kt, P - 1))):
                last = dve.tensor_copy(ends[:, i], grouped(t)[:, :, e])
            last.then_inc(ends_ready, 1)
            for pen, e in ((pen_f, 0), (pen_b, P - 1)):
                ch.done(dve.tensor_tensor(grouped(pen), grouped(kt), spread(grouped(kt)[:, :, e], [P, G, P]), ALU.is_equal))
                ch.done(dve.tensor_scalar(pen[:, :], pen[:, :], LOW, -LOW, ALU.mult, ALU.add))
            ch.done(dve.tensor_tensor(tmp[:, :], fwd[:, :], bwd[:, :], ALU.max))
            dve.wait_ge(row_done, 16)
            dve.tensor_tensor(inner[:, :], row[:, 2], row[:, 3], ALU.is_equal)
            dve.memset(joint[:, 0:1], 0.0)
            dve.memset(joint[:, T:T + 1], 0.0)
            ch.done(dve.tensor_tensor(joint[:, 1:T], row[:, 2, 1:T], row[:, 3, 0:T - 1], ALU.is_equal))
            ch.done(dve.tensor_tensor(go[:, :], inner[:, :], joint[:, 0:T], ALU.mult))
            ch.done(dve.tensor_scalar(go[:, :], go[:, :], LOW, -LOW, ALU.mult, ALU.add))
            ch.done(dve.tensor_tensor_scan(carried[:, :], go[:, :], row[:, 0], -LOW, ALU.add, ALU.max))
            dve.memset(carry[:, 0, 0:1], -LOW)
            ch.done(dve.tensor_scalar(carry[:, 0, 1:T], joint[:, 1:T], LOW, -LOW, ALU.mult, ALU.add))
            ch.done(dve.tensor_tensor(carry[:, 0, 1:T], carry[:, 0, 1:T], carried[:, 0:T - 1], ALU.add))
            ch.done(dve.tensor_tensor(go[:, :], inner[:, :], joint[:, 1:T + 1], ALU.mult))
            ch.done(dve.tensor_scalar(go[:, :], go[:, :], LOW, -LOW, ALU.mult, ALU.add))
            ch.done(dve.tensor_tensor_scan(carried[:, ::-1], go[:, ::-1], row[:, 1, ::-1], -LOW, ALU.add, ALU.max))
            dve.memset(carry[:, 1, T - 1:T], -LOW)
            ch.done(dve.tensor_scalar(carry[:, 1, 0:T - 1], joint[:, 1:T], LOW, -LOW, ALU.mult, ALU.add))
            dve.tensor_tensor(carry[:, 1, 0:T - 1], carry[:, 1, 0:T - 1], carried[:, 1:T], ALU.add).then_inc(carry_ready, 1)
            dve.wait_ge(carry_copied, 1)
            for i, pen in enumerate((pen_f, pen_b)):
                ch.done(dve.tensor_tensor(grouped(pen), grouped(pen), spread(carry_t[:, i], [P, G, P]), ALU.add))
                ch.done(dve.tensor_tensor(tmp[:, :], tmp[:, :], pen[:, :], ALU.max))
            dve.tensor_tensor(tmp[:, :], st[:, :], tmp[:, :], ALU.subtract).then_inc(below, 1)

        @block.sync
        def _(sp):
            sp.wait_ge(ends_copied, 1)
            sp.dma_start(ends_dram, ends_t[:, :]).then_inc(out_done, 16)
            sp.wait_ge(out_done, 16)
            sp.dma_start(row[:, :, :], ends_dram.rearrange("(a g) p -> a (g p)", a=4).rearrange("a (h t) -> h a t", h=HEADS))\
              .then_inc(row_done, 16)
            sp.wait_ge(carry_ready, 1)
            sp.dma_start(carry_dram.rearrange("(a g) p -> a (g p)", a=2).rearrange("a (h t) -> h a t", h=HEADS), carry[:, :, :])\
              .then_inc(carry_out, 16)
            sp.wait_ge(carry_out, 16)
            sp.dma_start(carry_rows[:, :], carry_dram).then_inc(carry_in, 16)


def mix_values(nc, name, k, moved, o, table_v, weights, accs):
    with ExitStack() as ctx, nc.Block() as block:
        f = Phase(nc, ctx, name)
        width = C + HEADS
        rows = f.sb("rows", [P, BODY, width])
        sel = f.sb("sel", [P, BODY, P])
        bank = [f.ps(f"sum{j}", [P, 512]) for j in range(8)]
        landed = moved.sems
        (sel_ready, copied, weighted, tile_done, added, passed_act) = (f.sem(n) for n in (
            "sel_ready", "copied", "weighted", "tile_done", "added", "passed_act"))

        gather_rows(f, block, o.other, table_v, rows, C, landed, tile_done)

        def weights_of(it, i):
            return by_tile(weights)[:, bass.ds(it * BODY + i * QUAD, QUAD), :]

        @block.vector
        def _(dve):
            dve.sem_inc(added, 8)

            def weigh(it, i):
                dve.wait_ge(landed[i], moved.after(it + 1))
                v = rows[:, i * QUAD:(i + 1) * QUAD, 0:C].rearrange("p j (h d) -> p j h d", h=HEADS)
                dve.tensor_tensor(v, v, weights_of(it, i).unsqueeze(3).to_broadcast([P, QUAD, HEADS, HD]),
                                  ALU.mult).then_inc(weighted, 1)

            def add(it, i):
                add_tiles(nc, dve, o, accs, width, lambda j: bank[j % 8], it, i * QUAD, QUAD,
                          tile_done, BODY, added, 8)

            with dve.Fori(0, T // BODY, 1) as it:
                for s in range(2):
                    select_matrix(dve, k, o, sel, it, s).then_inc(sel_ready, 1)
                weigh(it, 0)
                for i in range(1, NQ):
                    weigh(it, i)
                    add(it, i - 1)
                add(it, NQ - 1)

        @block.scalar
        def _(act):
            with act.Fori(0, T // BODY, 1) as it:
                for i in range(NQ):
                    hold(act, tile_done, it * BODY + (i + 1) * QUAD, passed_act)
                    act.copy(rows[:, i * QUAD:(i + 1) * QUAD, C:width], weights_of(it, i)).then_inc(copied, 1)

        @block.tensor
        def _(pe):
            pe.sem_inc(tile_done, BODY)
            with pe.Fori(0, T // BODY, 1) as it:
                for i in range(NQ):
                    if i % 2 == 0:
                        pe.wait_ge(sel_ready, it * 2 + i // 2 + 1)
                    pe.wait_ge(copied, it * NQ + i + 1)
                    pe.wait_ge(weighted, it * NQ + i + 1)
                    for j in range(i * QUAD, (i + 1) * QUAD):
                        pe.wait_ge(added, it * BODY + j + 1)
                        pe.matmul(bank[j % 8][:, 0:width], sel[:, j], rows[:, j], start=True, stop=True)\
                          .then_inc(tile_done, 1)

    moved.end(T // BODY)


class KeepLargest(Finish):

    STEPS = 2 + 2 * (MAXK // 8)

    def __init__(self, out):
        self.out = out

    def place_more(self, f):
        self.left = f.sb("left", [P, DB, C])
        self.eight = f.sb("eight", [P, DB, 8])

    def steps(self, dve, ch, it, z):
        ch.done(dve.tensor_copy(self.left[:, :, :], z))
        for _ in range(MAXK // 8):
            for j in range(DB):
                last = dve.max(self.eight[:, j], self.left[:, j])
            ch.done(last)
            for j in range(DB):
                last = dve.match_replace(self.left[:, j], self.eight[:, j], self.left[:, j], -BIG)
            ch.done(last)
        ch.done(dve.scalar_tensor_tensor(of_body(self.out, it), self.left[:, :, :], -BIG, z, ALU.is_equal, ALU.mult))


def batch_norm(nc, name, k, prepare, y, gamma, beta, x):
    with ExitStack() as ctx, nc.Block() as block:
        f = Phase(nc, ctx, name)
        sq = f.sb("sq", [P, NB * C])
        mean = f.sb("mean", [P, C])
        a = f.sb("a", [P, C])
        r = f.sb("r", [P, C])
        t = f.sb("t", [P, C])
        sum_ps = [f.ps(f"sum{s}", [P, C]) for s in range(2)]
        prepared, step, summed, centred, squared, var_ready, rooted = (f.sem(n) for n in (
            "prepared", "step", "summed", "centred", "squared", "var_ready", "rooted"))
        y3, full = blocks(y), [P, NB, C]
        chunks = NB // DB

        @block.tensor
        def _(pe):
            def column_sums(out, src, ready):
                for b in range(NB):
                    if b % DB == 0:
                        pe.wait_ge(ready, b // DB + 1)
                    rows = P if b < NB - 1 else TAIL
                    last = pe.matmul(out, k.ones[0:rows, :], src[0:rows, b * C:(b + 1) * C],
                                     start=(b == 0), stop=(b == NB - 1))
                last.then_inc(summed, 1)
            column_sums(sum_ps[0][:, :], y, prepared)
            column_sums(sum_ps[1][:, :], sq, squared)

        @block.vector
        def _(dve):
            ch = Chain(dve, step)
            for c in range(chunks):
                prepare(dve, ch, c).then_inc(prepared, 1)
            dve.wait_ge(summed, 1)
            ch.done(dve.tensor_scalar(mean[:, :], sum_ps[0][:, :], 1.0 / N, None, ALU.mult))
            for c in range(chunks):
                yc = y3[:, c * DB:(c + 1) * DB]
                dve.tensor_tensor(yc, yc, repeat(mean[:, :], [P, DB, C]), ALU.subtract).then_inc(centred, 1)
            dve.wait_ge(summed, 2)
            dve.tensor_scalar(a[:, :], sum_ps[1][:, :], 1.0 / N, BN_EPS, ALU.mult, ALU.add).then_inc(var_ready, 1)
            dve.wait_ge(rooted, 1)
            inverse_root(dve, ch, r[:, :], a[:, :], t[:, :])
            ch.done(dve.tensor_tensor(r[:, :], r[:, :], gamma[:, :], ALU.mult))
            ch.done(dve.tensor_tensor(y3, y3, repeat(r[:, :], full), ALU.mult))
            ch.done(dve.tensor_tensor(y3, y3, repeat(beta[:, :], full), ALU.add))
            ch.done(dve.scalar_tensor_tensor(y[:, :], y[:, :], SLOPE, y[:, :], ALU.mult, ALU.max))
            dve.tensor_tensor(x[:, :], x[:, :], y[:, :], ALU.add)

        @block.scalar
        def _(act):
            for c in range(chunks):
                part = slice(c * DB * C, (c + 1) * DB * C)
                act.wait_ge(centred, c + 1)
                act.activation(sq[:, part], y[:, part], ACT.Square).then_inc(squared, 1)
            act.wait_ge(var_ready, 1)
            act.activation(r[:, :], a[:, :], ACT.Sqrt).then_inc(rooted, 1)


def vector_work(nc, name, work):
    with ExitStack() as ctx, nc.Block() as block:
        step = Phase(nc, ctx, name).sem("step")

        @block.vector
        def _(dve):
            work(dve, Chain(dve, step))


def load(nc, name, loads, work=None):
    with ExitStack() as ctx, nc.Block() as block:
        f = Phase(nc, ctx, name)
        loaded, step = f.sem("loaded"), f.sem("step")

        @block.sync
        def _(sp):
            for dst, src in loads:
                sp.dma_start(dst, src).then_inc(loaded, 16)
            sp.wait_ge(loaded, 16 * len(loads))

        if work is not None:
            @block.vector
            def _(dve):
                work(dve, Chain(dve, step))


def clear_semaphores(nc):
    used = sorted(nc.released_uncleared_semaphores)
    with nc.Block() as block:
        @block.gpsimd
        def _(pool):
            first = used[0]
            for a, b in zip(used, used[1:] + [None]):
                if b != a + 1:
                    pool.sem_clear(range(first, a + 1))
                    first = b


def on_all(vector):
    return vector.partition_broadcast(P)


def build(nc, A, out):
    with ExitStack() as top:
        def sb(name, shape, dt=F32):
            return top.enter_context(nc.sbuf_tensor(name, shape, dt))

        def dram(name, shape, dt=F32):
            return nc.dram_tensor(name, shape, dt, kind="Internal").ap()

        k = make_consts(nc, top, sb)
        by_dst = Order(sb, dram)
        moved = IndirectCount(nc, top)
        count_d = sb("count_d", [P, NB])
        count_s = sb("count_s", [P, NB])
        root_d = sb("root_d", [P, NB])
        root_s = sb("root_s", [P, NB])
        mean_d = sb("mean_d", [P, NB])
        share = sb("share", [P, NB * NREL])
        table = dram("table", [NPAD, C])
        table_v = dram("table_v", [NPAD, C])
        table_r = dram("table_r", [NPAD * NREL, H1])
        ends_dram = dram("ends_dram", [4 * G, P])
        carry_dram = dram("carry_dram", [2 * G, P])
        adj_dram = dram("adj_dram", [NB, P, NPAD], U16)
        pair_records = dram("pair_records", [P * TP, 2], BF16)

        with ExitStack() as ctx:
            pair_block = ctx.enter_context(nc.sbuf_tensor("pair_block", [1, TP], I32))
            places = ctx.enter_context(nc.sbuf_tensor("places", [P, 2, TP], BF16))
            e = Keys(nc, ctx)
            with ExitStack() as c:
                setup(nc, c, k, e, A, by_dst.records, pair_records)
            with ExitStack() as c, nc.Block() as block:
                rank_edges(nc, block, c, "pair", e.src_high, e.dst_high, NB, TP, k, e.slot_p, pair_block, None, False, [])
            with ExitStack() as c, nc.Block() as block:
                scatter_records(nc, block, c, "pair", pair_records, e.slot_p, e.pair, moved)
                rank_edges(nc, block, c, "dst", e.dst_low, e.dst_high, P, T, k, e.slot_d, by_dst.block, count_d, True,
                           [(e.dst_low, e.dst_kind, NB * NREL, share), (e.src_low, e.src_high, NB, count_s)])
            with ExitStack() as c:
                places_in = c.enter_context(nc.sbuf_tensor("places_in", [P, TP, 2], BF16))
                load(nc, "places_load", [(places_in[:, :, :], pair_records.rearrange("(p t) c -> p t c", p=P))])
                vector_work(nc, "places_split", lambda dve, ch: dve.tensor_copy(
                    places[:, :, :], places_in[:, :, :].rearrange("p t c -> p c t")))
            with ExitStack() as c:
                adj = c.enter_context(nc.sbuf_tensor("adj", [P, NB * NPAD + P], U16))
                with ExitStack() as c2, nc.Block() as block:
                    scatter_records(nc, block, c2, "dst", by_dst.records, e.slot_d, e.record, moved)
                    build_adjacency(nc, block, c2, k, places, pair_block, adj)
                store_adjacency(nc, adj, adj_dram)
        x = sb("x_sb", [P, NB * C])
        with ExitStack() as c, nc.Block() as block:
            fetch_records(nc, block, c, by_dst)
            f = Phase(nc, c, "x_load")
            tail_zero, loaded = f.sem("tail_zero"), f.sem("loaded")

            @block.scalar
            def _(act):
                act.dma_start(x[:, 0:(NB - 1) * C].rearrange("p (b c) -> p b c", b=NB - 1),
                              A["x"][0:(NB - 1) * P, :].rearrange("(b p) c -> p b c", p=P)).then_inc(loaded, 16)
                act.wait_ge(tail_zero, 1)
                act.dma_start(x[0:TAIL, (NB - 1) * C:NB * C], A["x"][(NB - 1) * P:N, :]).then_inc(loaded, 16)
                act.wait_ge(loaded, 32)

            @block.gpsimd
            def _(pool):
                pool.memset(x[:, (NB - 1) * C:NB * C], 0.0).then_inc(tail_zero, 1)
        degrees(nc, count_d, count_s, root_d, root_s, mean_d)

        def finish():
            with ExitStack() as c, nc.Block() as block:
                stored = Phase(nc, c, "out").sem("stored")

                @block.sync
                def _(sp):
                    sp.dma_start(out[0:(NB - 1) * P, :].rearrange("(b p) c -> p b c", p=P),
                                 x[:, 0:(NB - 1) * C].rearrange("p (b c) -> p b c", b=NB - 1)).then_inc(stored, 16)
                    sp.dma_start(out[(NB - 1) * P:N, :], x[0:TAIL, (NB - 1) * C:NB * C]).then_inc(stored, 16)
                    sp.wait_ge(stored, 32)

        h = sb("h", [P, NB * H1])
        normed_ctx = ExitStack()
        normed = normed_ctx.enter_context(nc.sbuf_tensor("normed", [P, NB * C], F32))
        with ExitStack() as ctx:
            f = Phase(nc, ctx, "l0")
            g = f.sb("g", [P, NB * C])
            b1, gamma1, beta1 = (f.sb(n, [P, CW]) for n in ("b1", "gamma1", "beta1"))
            b2, gamma2, beta2 = (f.sb(n, [P, C]) for n in ("b2", "gamma2", "beta2"))
            load(nc, "l0_load", [(t[:, :], on_all(A[f"L0_gnn_{n}"])) for t, n in (
                (b1, "b1"), (gamma1, "gamma1"), (beta1, "beta1"), (b2, "b2"), (gamma2, "gamma2"), (beta2, "beta2"))])
            norm_relu(nc, "l0_in", x, g, scale=root_d)
            neighbour_sums(nc, "l0_a1", k, adj_dram, g, Scaled(root_d, normed))
            with ExitStack() as c:
                wide = c.enter_context(nc.sbuf_tensor("l0_wide", [P, NB * CW], F32))
                dense(nc, "l0_w1", k, normed, C // P, CW, whole(A["L0_gnn_W1"]), [(0, CW, None, b1)],
                      HiddenNorm(gamma1, beta1, root_d, wide))
                dense(nc, "l0_w2", k, wide, CW // P, C, whole(A["L0_gnn_W2"]), [(0, C, g, None)])
            neighbour_sums(nc, "l0_a2", k, adj_dram, g,
                           ToStream(root_d, x, own=(b2, gamma2, beta2), out=normed, out_scale=root_s))

        clear_semaphores(nc)

        with ExitStack() as ctx:
            g = Phase(nc, ctx, "l1").sb("g", [P, NB * C])
            dense(nc, "l1_w", k, normed, C // P, C, whole(A["L1_gnn_W"]), [(0, C, g, None)])
            neighbour_sums(nc, "l1_a", k, adj_dram, g, ToStream(root_s, x, out=normed), turned=True)

        clear_semaphores(nc)

        with ExitStack() as ctx:
            f = Phase(nc, ctx, "l2")
            with normed_ctx, ExitStack() as inner:
                fi = Phase(nc, inner, "l2r")
                index = fi.sb("index", [P, T], I32)
                index_f = fi.sb("index_f", [P, T])
                with ExitStack() as dense_part:
                    fd = Phase(nc, dense_part, "l2d")
                    xw = fd.sb("xw", [P, NB * NREL * H1])
                    bias = fd.sb("bias", [P, H1])
                    def kind_rows(dve, ch):
                        ch.done(dve.tensor_scalar(share[:, :], share[:, :], 1.0, None, ALU.max))
                        dve.reciprocal(share[:, :], share[:, :])
                        ch.done(dve.tensor_copy(index_f[:, :], by_dst.other[:, :]))
                        dve.scalar_tensor_tensor(index[:, :], index_f[:, :], float(NREL), by_dst.kind[:, :],
                                                 ALU.mult, ALU.add)
                    load(nc, "l2_load", [(bias[:, :], on_all(A["L2_gnn_rgcn_bias"]))], kind_rows)
                    wr = A["L2_gnn_rgcn_weight"]
                    by_kind = NREL * H1
                    dense(nc, "l2_w", k, normed, C // P, by_kind + H1,
                          lambda w: [(w[:, c, 0:by_kind].rearrange("p (r h) -> p r h", r=NREL),
                                      wr[:, c * P:(c + 1) * P, :].rearrange("r p h -> p r h")) for c in range(C // P)]
                          + [(w[:, :, by_kind:by_kind + H1], A["L2_gnn_rgcn_root"].rearrange("(k p) n -> p k n", p=P))],
                          [(0, by_kind, xw, None), (by_kind, H1, h, bias)],
                          stores=[(xw, by_kind, table_r.rearrange("(n r) h -> n (r h)", r=NREL))])
                h_odd = fi.sb("h_odd", [P, NB * H1])
                vector_work(nc, "l2_z", lambda dve, ch: dve.memset(h_odd[:, :], 0.0))
                aggregate_kinds(nc, "l2_a", k, moved, by_dst, index, table_r, share, (h, h_odd))
                vector_work(nc, "l2_y", lambda dve, ch: dve.tensor_tensor(h[:, :], h[:, :], h_odd[:, :], ALU.add))
            q = f.sb("q", [P, NB * C])
            skip = f.sb("skip", [P, NB * C])
            with ExitStack() as inner:
                fi = Phase(nc, inner, "l2p")
                kk = fi.sb("kk", [P, NB * C])
                v = fi.sb("v", [P, NB * C])
                biases = [fi.sb(n, [P, C]) for n in ("bq", "bk", "bv", "bskip")]
                load(nc, "l2_load2", [(t[:, :], on_all(A[f"L2_gnn_{n}"])) for t, n in zip(
                    biases, ("bq", "bk", "bv", "bskip"))])
                dense(nc, "l2_qkv", k, h, 1, 4 * C,
                      lambda w: [(w[:, 0, i * C:(i + 1) * C], A[f"L2_gnn_{n}"]) for i, n in enumerate(
                          ("wq", "wk", "wv", "wskip"))],
                      [(i * C, C, t, b) for i, (t, b) in enumerate(zip((q, kk, v, skip), biases))],
                      stores=[(kk, C, table), (v, C, table_v)])
            scores = f.sb("scores", [P, T * HEADS])
            edge_scores(nc, "l2_sc", k, moved, by_dst, table, q, scores)
            softmax_weights(nc, "l2_sm", k, by_dst, scores, ends_dram, carry_dram)
            acc = f.sb("acc", [P, NB * (C + HEADS)])
            acc_odd = f.sb("acc_odd", [P, NB * (C + HEADS)])
            gamma = f.sb("gamma", [P, C])
            beta = f.sb("beta", [P, C])

            def start_acc(dve, ch):
                dve.memset(acc_odd[:, :], 0.0)
                dve.memset(acc[:, :], 0.0)
            load(nc, "l2_load3", [(gamma[:, :], on_all(A["L2_gnn_bn_gamma"])), (beta[:, :], on_all(A["L2_gnn_bn_beta"]))],
                 start_acc)
            mix_values(nc, "l2_mix", k, moved, by_dst, table_v, scores, (acc, acc_odd))

            def end_attention(dve, ch, c):
                part = slice(c * DB, (c + 1) * DB)
                a3, odd3 = (blocks(t, C + HEADS)[:, part] for t in (acc, acc_odd))
                den = a3[:, :, C:C + HEADS]
                q3 = blocks(q)[:, part]
                ch.done(dve.tensor_tensor(a3, a3, odd3, ALU.add))
                ch.done(dve.tensor_scalar(den, den, 1e-16, None, ALU.max))
                ch.done(dve.reciprocal(den, den))
                ch.done(dve.tensor_tensor(
                    q3.rearrange("p b (h d) -> p b h d", h=HEADS),
                    a3[:, :, 0:C].rearrange("p b (h d) -> p b h d", h=HEADS),
                    den.unsqueeze(3).to_broadcast([P, DB, HEADS, HD]), ALU.mult))
                return dve.tensor_tensor(q3, q3, blocks(skip)[:, part], ALU.add)
            batch_norm(nc, "l2_bn", k, end_attention, q, gamma, beta, x)

        clear_semaphores(nc)

        with ExitStack() as ctx:
            f = Phase(nc, ctx, "l3")
            g = f.sb("g", [P, NB * C])
            kept = f.sb("kept", [P, NB * C])
            norm_relu(nc, "l3_in", x, g)
            dense(nc, "l3_w", k, g, C // P, 2 * C,
                  lambda w: [(w[:, :, 0:C], A["L3_gnn_W_self"].rearrange("(k p) n -> p k n", p=P)),
                             (w[:, :, C:2 * C], A["L3_gnn_W_neigh"].rearrange("(k p) n -> p k n", p=P))],
                  [(0, C, x, ADD), (C, C, None, None)], KeepLargest(kept))
            neighbour_sums(nc, "l3_a", k, adj_dram, kept, ToStream(mean_d, x), loops=False)
        finish()


_INS = ['x', 'src', 'dst', 'edge_type_8', 'L0_gnn_W1', 'L0_gnn_b1', 'L0_gnn_gamma1', 'L0_gnn_beta1', 'L0_gnn_W2',
        'L0_gnn_b2', 'L0_gnn_gamma2', 'L0_gnn_beta2', 'L1_gnn_W', 'L2_gnn_rgcn_weight', 'L2_gnn_rgcn_root',
        'L2_gnn_rgcn_bias', 'L2_gnn_wq', 'L2_gnn_bq', 'L2_gnn_wk', 'L2_gnn_bk', 'L2_gnn_wv', 'L2_gnn_bv',
        'L2_gnn_wskip', 'L2_gnn_bskip', 'L2_gnn_bn_gamma', 'L2_gnn_bn_beta', 'L3_gnn_W_self', 'L3_gnn_W_neigh']


def kernel(**inputs):
    import numpy as _np
    import concourse.bacc as _bacc
    from concourse import mybir as _mybir
    from concourse.bass_utils import run_bass_kernel_spmd as _run

    nc = _bacc.Bacc("TRN2", target_bir_lowering=False, num_devices=1)
    arrays, A = {}, {}
    for name in _INS:
        a = _np.asarray(inputs[name])
        if name == "L1_gnn_W":
            a = a.T
        a = _np.ascontiguousarray(a)
        arrays[f"in_{name}"] = a
        A[name] = nc.dram_tensor(f"in_{name}", a.shape, _mybir.dt.from_np(a.dtype), kind="ExternalInput").ap()
    out = nc.dram_tensor("out", (N, C), F32, kind="ExternalOutput").ap()
    build(nc, A, out)
    r = _run(nc, [arrays], core_ids=[0])
    return r.results[0]["out"]
```
